# Optimizing a Trainium2 kernel written in Bass

```python
import numpy as np
import jax
import jax.numpy as jnp

def _softmax(x, axis=-1):
    return jax.nn.softmax(x, axis=axis)

def _gelu(x):
    return jax.nn.gelu(x, approximate=True)

def _silu(x):
    return jax.nn.silu(x)

def _sigmoid(x):
    return jax.nn.sigmoid(x)

def _layernorm(x, axis=-1, eps=1e-05):
    m = jnp.mean(x, axis=axis, keepdims=True)
    v = jnp.var(x, axis=axis, keepdims=True)
    return (x - m) / jnp.sqrt(v + eps)

def _scatter_add(tgt, idx, src, axis=0):
    return tgt.at[idx].add(src)

def _segment_sum(src, seg, n):
    return jax.ops.segment_sum(src, seg, n)
kernel_name = 'mk_seq_preln_d1_jaxref_r8_83fac1'

def setup_inputs(seed: int=0):
    np.random.seed(seed)
    _w = jnp.asarray

    def _L0_attn_setup():
        import jax, jax.numpy as jnp
        import numpy as np
        from jax import lax
        D_MODEL = 256
        EXPAND = 2
        D_INNER = EXPAND * D_MODEL
        D_STATE = 64
        D_CONV = 4
        HEADDIM = 128
        NHEADS = D_INNER // HEADDIM
        NGROUPS = 1
        HPG = NHEADS // NGROUPS
        CHUNK = 32
        CONV_DIM = D_INNER + 2 * NGROUPS * D_STATE
        D_IN_PROJ = D_INNER + CONV_DIM + NHEADS
        BATCH = 4
        SEQLEN = 256
        EPS = 1.1920929e-07

        def _segsum(a):
            Q = a.shape[-1]
            cs = jnp.cumsum(a, axis=-1)
            seg = cs[..., :, None] - cs[..., None, :]
            mask = jnp.tril(jnp.ones((Q, Q), dtype=bool))
            return jnp.where(mask, seg, -jnp.inf)

        def _ssd(x, dt, A, B, C):
            b, L, H, P = x.shape
            nc = L // CHUNK
            xd = x * dt[..., None]
            xd_c = xd.reshape(b, nc, CHUNK, NGROUPS, HPG, P)
            B_c = B.reshape(b, nc, CHUNK, NGROUPS, D_STATE)
            C_c = C.reshape(b, nc, CHUNK, NGROUPS, D_STATE)
            dA = (dt * A).reshape(b, nc, CHUNK, NGROUPS, HPG)
            dA = jnp.transpose(dA, (0, 3, 4, 1, 2))
            A_cs = jnp.cumsum(dA, axis=-1)
            Lmat = jnp.exp(_segsum(dA))
            Y_diag = jnp.einsum('bcqgn,bckgn,bghcqk,bckghp->bcqghp', C_c, B_c, Lmat, xd_c)
            decay_states = jnp.exp(A_cs[..., -1:] - A_cs)
            states = jnp.einsum('bckgn,bghck,bckghp->bcghnp', B_c, decay_states, xd_c)
            chunk_decay = jnp.exp(A_cs[..., -1])

            def step(carry, inp):
                st, dec = inp
                return (carry * dec[..., None, None] + st, carry)
            init = jnp.zeros((b, NGROUPS, HPG, D_STATE, P), x.dtype)
            _, prev = lax.scan(step, init, (jnp.moveaxis(states, 1, 0), jnp.moveaxis(chunk_decay, 3, 0)))
            prev = jnp.moveaxis(prev, 0, 1)
            Y_off = jnp.einsum('bcqgn,bcghnp,bghcq->bcqghp', C_c, prev, jnp.exp(A_cs))
            return (Y_diag + Y_off).reshape(b, L, H, P)
        key = jax.random.key(seed)
        ks = jax.random.split(key, 8)
        x = jax.random.normal(ks[0], (BATCH, SEQLEN, D_MODEL), jnp.float32)
        W_in = jax.random.normal(ks[1], (D_IN_PROJ, D_MODEL), jnp.float32) * 0.02
        s = 1.0 / np.sqrt(D_CONV).astype(np.float32)
        conv_w = jax.random.uniform(ks[2], (CONV_DIM, D_CONV), jnp.float32, -s, s)
        conv_b = jax.random.uniform(ks[3], (CONV_DIM,), jnp.float32, -s, s)
        A_log = jnp.log(jax.random.uniform(ks[4], (NHEADS,), jnp.float32, 1.0, 16.0))
        dt = jnp.exp(jax.random.uniform(ks[5], (NHEADS,), jnp.float32) * (np.log(0.1) - np.log(0.001)) + np.log(0.001))
        dt = jnp.clip(dt, 0.001)
        dt_bias = dt + jnp.log(-jnp.expm1(-dt))
        D = jnp.ones((NHEADS,), jnp.float32)
        W_out = jax.random.normal(ks[6], (D_MODEL, D_INNER), jnp.float32) * 0.02
        return {'x': x, 'W_in': W_in, 'conv_w': conv_w, 'conv_b': conv_b, 'A_log': A_log, 'dt_bias': dt_bias, 'D': D, 'W_out': W_out}
    _L0_attn_in = _L0_attn_setup()

    def _L0_ffn_setup():
        import jax, jax.numpy as jnp
        import numpy as np
        E, K, H, F = (64, 6, 256, 96)
        G, KG = (8, 4)
        SHARED_F = 96
        SCALE = 2.5
        T = 2 * 128
        CAP = 2 * (T * K // E)

        def _grouped_topk(logits, bias):
            scores = jax.nn.sigmoid(logits.astype(jnp.float32))
            scores_b = scores + bias[None, :]
            gs = scores_b.reshape(-1, G, E // G)
            group_scores = jnp.sum(jax.lax.top_k(gs, 2)[0], axis=-1)
            gidx = jax.lax.top_k(group_scores, KG)[1]
            rows = jnp.arange(group_scores.shape[0])[:, None]
            group_mask = jnp.zeros_like(group_scores).at[rows, gidx].set(1.0)
            score_mask = jnp.repeat(group_mask, E // G, axis=-1) > 0
            tmp = jnp.where(score_mask, scores_b, -jnp.inf)
            topk_ids = jax.lax.top_k(tmp, K)[1]
            topk_w = jnp.take_along_axis(scores, topk_ids, axis=-1)
            topk_w = topk_w / jnp.sum(topk_w, axis=-1, keepdims=True)
            return (topk_w * SCALE, topk_ids)

        def _routed_moe(x, topk_w, topk_ids, w_gate, w_up, w_down):
            Tn = x.shape[0]
            flat_e = topk_ids.reshape(-1)
            order = jnp.argsort(flat_e)
            se = flat_e[order]
            pos = jnp.arange(Tn * K) - jnp.searchsorted(se, se, side='left')
            tok = order // K
            valid = pos < CAP
            slot = jnp.where(valid, pos, CAP)
            buf = jnp.zeros((E, CAP + 1, H), x.dtype).at[se, slot].set(x[tok])[:, :CAP]
            h = jax.nn.silu(jnp.einsum('ech,ehf->ecf', buf, w_gate)) * jnp.einsum('ech,ehf->ecf', buf, w_up)
            out = jnp.einsum('ecf,efh->ech', h, w_down)
            gathered = out[se, jnp.minimum(pos, CAP - 1)] * valid.astype(x.dtype)[:, None]
            w = topk_w.reshape(-1)[order].astype(x.dtype)[:, None]
            return jax.ops.segment_sum(gathered * w, tok, num_segments=Tn)
        key = jax.random.key(seed)
        ks = jax.random.split(key, 9)
        s = 0.02
        return dict(hidden_states=jax.random.normal(ks[0], (2, 128, H), jnp.float32), gate_w=jax.random.normal(ks[1], (H, E), jnp.float32) * s, bias=jax.random.normal(ks[2], (E,), jnp.float32) * s, w_gate=jax.random.normal(ks[3], (E, H, F), jnp.float32) * s, w_up=jax.random.normal(ks[4], (E, H, F), jnp.float32) * s, w_down=jax.random.normal(ks[5], (E, F, H), jnp.float32) * s, ws_gate=jax.random.normal(ks[6], (H, SHARED_F), jnp.float32) * s, ws_up=jax.random.normal(ks[7], (H, SHARED_F), jnp.float32) * s, ws_down=jax.random.normal(ks[8], (SHARED_F, H), jnp.float32) * s)
    _L0_ffn_in = _L0_ffn_setup()
    _d = {'L0_attn_x': _L0_attn_in['x'], 'L0_attn_W_in': _L0_attn_in['W_in'], 'L0_attn_conv_w': _L0_attn_in['conv_w'], 'L0_attn_conv_b': _L0_attn_in['conv_b'], 'L0_attn_A_log': _L0_attn_in['A_log'], 'L0_attn_dt_bias': _L0_attn_in['dt_bias'], 'L0_attn_D': _L0_attn_in['D'], 'L0_attn_W_out': _L0_attn_in['W_out'], 'L0_ffn_gate_w': _L0_ffn_in['gate_w'], 'L0_ffn_bias': _L0_ffn_in['bias'], 'L0_ffn_w_gate': _L0_ffn_in['w_gate'], 'L0_ffn_w_up': _L0_ffn_in['w_up'], 'L0_ffn_w_down': _L0_ffn_in['w_down'], 'L0_ffn_ws_gate': _L0_ffn_in['ws_gate'], 'L0_ffn_ws_up': _L0_ffn_in['ws_up'], 'L0_ffn_ws_down': _L0_ffn_in['ws_down']}
    _x0 = _d['L0_attn_x']
    _d['L0_attn_x'] = jax.random.normal(jax.random.fold_in(jax.random.key(seed), 1), (8, 512, 256), dtype=_x0.dtype)
    del _x0
    return _d

def reference(L0_attn_x, L0_attn_W_in, L0_attn_conv_w, L0_attn_conv_b, L0_attn_A_log, L0_attn_dt_bias, L0_attn_D, L0_attn_W_out, L0_ffn_gate_w, L0_ffn_bias, L0_ffn_w_gate, L0_ffn_w_up, L0_ffn_w_down, L0_ffn_ws_gate, L0_ffn_ws_up, L0_ffn_ws_down):

    def _L0_attn_ref(x, W_in, conv_w, conv_b, A_log, dt_bias, D, W_out):
        import jax, jax.numpy as jnp
        import numpy as np
        from jax import lax
        D_MODEL = 256
        EXPAND = 2
        D_INNER = EXPAND * D_MODEL
        D_STATE = 64
        D_CONV = 4
        HEADDIM = 128
        NHEADS = D_INNER // HEADDIM
        NGROUPS = 1
        HPG = NHEADS // NGROUPS
        CHUNK = 32
        CONV_DIM = D_INNER + 2 * NGROUPS * D_STATE
        D_IN_PROJ = D_INNER + CONV_DIM + NHEADS
        BATCH = 4
        SEQLEN = 256
        EPS = 1.1920929e-07

        def _segsum(a):
            Q = a.shape[-1]
            cs = jnp.cumsum(a, axis=-1)
            seg = cs[..., :, None] - cs[..., None, :]
            mask = jnp.tril(jnp.ones((Q, Q), dtype=bool))
            return jnp.where(mask, seg, -jnp.inf)

        def _ssd(x, dt, A, B, C):
            b, L, H, P = x.shape
            nc = L // CHUNK
            xd = x * dt[..., None]
            xd_c = xd.reshape(b, nc, CHUNK, NGROUPS, HPG, P)
            B_c = B.reshape(b, nc, CHUNK, NGROUPS, D_STATE)
            C_c = C.reshape(b, nc, CHUNK, NGROUPS, D_STATE)
            dA = (dt * A).reshape(b, nc, CHUNK, NGROUPS, HPG)
            dA = jnp.transpose(dA, (0, 3, 4, 1, 2))
            A_cs = jnp.cumsum(dA, axis=-1)
            Lmat = jnp.exp(_segsum(dA))
            Y_diag = jnp.einsum('bcqgn,bckgn,bghcqk,bckghp->bcqghp', C_c, B_c, Lmat, xd_c)
            decay_states = jnp.exp(A_cs[..., -1:] - A_cs)
            states = jnp.einsum('bckgn,bghck,bckghp->bcghnp', B_c, decay_states, xd_c)
            chunk_decay = jnp.exp(A_cs[..., -1])

            def step(carry, inp):
                st, dec = inp
                return (carry * dec[..., None, None] + st, carry)
            init = jnp.zeros((b, NGROUPS, HPG, D_STATE, P), x.dtype)
            _, prev = lax.scan(step, init, (jnp.moveaxis(states, 1, 0), jnp.moveaxis(chunk_decay, 3, 0)))
            prev = jnp.moveaxis(prev, 0, 1)
            Y_off = jnp.einsum('bcqgn,bcghnp,bghcq->bcqghp', C_c, prev, jnp.exp(A_cs))
            return (Y_diag + Y_off).reshape(b, L, H, P)
        b, L, _ = x.shape
        proj = x @ W_in.T
        z = proj[..., :D_INNER]
        xBC = proj[..., D_INNER:D_INNER + CONV_DIM]
        dt_raw = proj[..., D_INNER + CONV_DIM:D_INNER + CONV_DIM + NHEADS]
        xp = jnp.pad(xBC, ((0, 0), (D_CONV - 1, 0), (0, 0)))
        xc = conv_b + sum((xp[:, k:k + L, :] * conv_w[:, k] for k in range(D_CONV)))
        xc = jax.nn.silu(xc)
        x_ssm = xc[..., :D_INNER].reshape(b, L, NHEADS, HEADDIM)
        B_ssm = xc[..., D_INNER:D_INNER + NGROUPS * D_STATE].reshape(b, L, NGROUPS, D_STATE)
        C_ssm = xc[..., D_INNER + NGROUPS * D_STATE:].reshape(b, L, NGROUPS, D_STATE)
        dt = jax.nn.softplus(dt_raw + dt_bias)
        A = -jnp.exp(A_log)
        y = _ssd(x_ssm, dt, A, B_ssm, C_ssm) + x_ssm * D[:, None]
        y = y.reshape(b, L, D_INNER)
        y = y * lax.rsqrt(jnp.mean(y * y, axis=-1, keepdims=True) + EPS)
        return y * jax.nn.silu(z) @ W_out.T

    def _L0_ffn_ref(hidden_states, gate_w, bias, w_gate, w_up, w_down, ws_gate, ws_up, ws_down):
        import jax, jax.numpy as jnp
        import numpy as np
        E, K, H, F = (64, 6, 256, 96)
        G, KG = (8, 4)
        SHARED_F = 96
        SCALE = 2.5
        T = 2 * 128
        CAP = 2 * (T * K // E)

        def _grouped_topk(logits, bias):
            scores = jax.nn.sigmoid(logits.astype(jnp.float32))
            scores_b = scores + bias[None, :]
            gs = scores_b.reshape(-1, G, E // G)
            group_scores = jnp.sum(jax.lax.top_k(gs, 2)[0], axis=-1)
            gidx = jax.lax.top_k(group_scores, KG)[1]
            rows = jnp.arange(group_scores.shape[0])[:, None]
            group_mask = jnp.zeros_like(group_scores).at[rows, gidx].set(1.0)
            score_mask = jnp.repeat(group_mask, E // G, axis=-1) > 0
            tmp = jnp.where(score_mask, scores_b, -jnp.inf)
            topk_ids = jax.lax.top_k(tmp, K)[1]
            topk_w = jnp.take_along_axis(scores, topk_ids, axis=-1)
            topk_w = topk_w / jnp.sum(topk_w, axis=-1, keepdims=True)
            return (topk_w * SCALE, topk_ids)

        def _routed_moe(x, topk_w, topk_ids, w_gate, w_up, w_down):
            Tn = x.shape[0]
            flat_e = topk_ids.reshape(-1)
            order = jnp.argsort(flat_e)
            se = flat_e[order]
            pos = jnp.arange(Tn * K) - jnp.searchsorted(se, se, side='left')
            tok = order // K
            valid = pos < CAP
            slot = jnp.where(valid, pos, CAP)
            buf = jnp.zeros((E, CAP + 1, H), x.dtype).at[se, slot].set(x[tok])[:, :CAP]
            h = jax.nn.silu(jnp.einsum('ech,ehf->ecf', buf, w_gate)) * jnp.einsum('ech,ehf->ecf', buf, w_up)
            out = jnp.einsum('ecf,efh->ech', h, w_down)
            gathered = out[se, jnp.minimum(pos, CAP - 1)] * valid.astype(x.dtype)[:, None]
            w = topk_w.reshape(-1)[order].astype(x.dtype)[:, None]
            return jax.ops.segment_sum(gathered * w, tok, num_segments=Tn)
        orig_shape = hidden_states.shape
        x = hidden_states.reshape(-1, H)
        router_logits = x @ gate_w
        topk_w, topk_ids = _grouped_topk(router_logits, bias)
        y = _routed_moe(x, topk_w, topk_ids, w_gate, w_up, w_down)
        shared = jax.nn.silu(x @ ws_gate) * (x @ ws_up) @ ws_down
        return (y + shared).reshape(orig_shape)
    x = L0_attn_x
    x = x + _L0_attn_ref(_layernorm(x, axis=-1), L0_attn_W_in, L0_attn_conv_w, L0_attn_conv_b, L0_attn_A_log, L0_attn_dt_bias, L0_attn_D, L0_attn_W_out)
    x = x + _L0_ffn_ref(_layernorm(x, axis=-1), L0_ffn_gate_w, L0_ffn_bias, L0_ffn_w_gate, L0_ffn_w_up, L0_ffn_w_down, L0_ffn_ws_gate, L0_ffn_ws_up, L0_ffn_ws_down)
    return x

_drawn_inputs = setup_inputs


def setup_inputs(seed=0):
    import zlib

    import numpy as np

    out = dict(_drawn_inputs(seed))
    spreads = {'L0_attn_D': (1.0, 0.6)}
    factors = {'L0_attn_A_log': 8.0,
     'L0_attn_dt_bias': 8.0,
     'L0_ffn_gate_w': 8.0,
     'L0_ffn_bias': 8.0,
     'L0_ffn_w_gate': 8.0,
     'L0_ffn_w_up': 8.0,
     'L0_ffn_w_down': 8.0,
     'L0_ffn_ws_gate': 5.585,
     'L0_ffn_ws_up': 5.513,
     'L0_ffn_ws_down': 5.497}
    for name, (base, spread) in spreads.items():
        noise = np.random.default_rng([zlib.crc32(name.encode()), seed]).standard_normal(out[name].shape)
        drawn = base * np.exp(spread * noise) if base else spread * noise
        out[name] = jnp.asarray(drawn.astype(out[name].dtype))
    for name, factor in factors.items():
        out[name] = (out[name] * factor).astype(out[name].dtype)
    return out
```

```python
from contextlib import ExitStack

import concourse.bass as bass
from concourse import mybir

F32 = mybir.dt.float32
I32 = mybir.dt.int32
U32 = mybir.dt.uint32
ALU = mybir.AluOpType
ACT = mybir.ActivationFunctionType
AX = mybir.AxisListType

P = 128
NSEQ, L, D = 8, 512, 256
T = NSEQ * L
TILES = L // P
KD = D // P
H, HD = 4, 128
DI = H * HD
N = 64
PROJ = 2 * DI + 2 * N
E, K, F = 64, 6, 96
G, KG = 8, 4
EG = E // G
CAP = 2 * (256 * K // E)
SCALE = 2.5
ROW = D + E
LN_EPS, RMS_EPS = 1e-5, 1.1920929e-07
BIG = 3.0e38
ET = E // 2
WRING = 4
ROUNDS = CAP // 8

SLOTS = [("ssq", "C"), ("out0", "C"), ("out1", "C"), ("m8", "A"), ("dt", "A"), ("m4", "A"),
         ("m5", "A"), ("m6", "A"), ("router", "C"), ("gate", "C"), ("up", "C"), ("m7", "A"),
         ("m0", "A"), ("m1", "A"), ("down0", "C"), ("down1", "C"), ("m2", "A"), ("m3", "A"),
         ("sel", "C")]
BANK = {name: n % 2 for n, (name, _) in enumerate(SLOTS)}
A_SLOTS = [n for n, st in SLOTS if st == "A"]
C_SLOTS = [n for n, st in SLOTS if st == "C"]
CONV = ["m8", "m4", "m5", "m6", "m7"]
ZT = ["m0", "m1", "m2", "m3"]


def at(seq, per, n=0):
    return seq * per + (n + 1)


class Chain:

    def __init__(self, eng, sem, seq, per):
        self.eng, self.sem, self.seq, self.per, self.n = eng, sem, seq, per, 0

    def link(self, ins):
        ins.then_inc(self.sem, 1)
        self.n += 1
        self.eng.wait_ge(self.sem, at(self.seq, self.per, self.n - 1))

    def done(self):
        assert self.n == self.per, (str(self.sem), self.n, self.per)


def build(nc, x, w_in, conv_w, conv_b, a_log, dt_bias, dskip, w_out, gate_w, bias,
          w_gate, w_up, w_down, ws_gate, ws_up, ws_down, rows, out):
    x_t = x.rearrange("(s j p) d -> s p j d", j=TILES, p=P)
    rows_t = rows[0:T, :].rearrange("(s j p) d -> s p j d", j=TILES, p=P)
    out_t = out[0:T, :].rearrange("(s j p) d -> s p j d", j=TILES, p=P)

    with ExitStack() as ctx:
        def sb(name, shape, dt=F32):
            return ctx.enter_context(nc.sbuf_tensor(name, shape, dt))

        def sem(name):
            return ctx.enter_context(nc.semaphore(name))

        def bank(name):
            return ctx.enter_context(nc.psum_tensor(name, [P, 512], F32))

        win = sb("win", [P, KD, PROJ + H])
        wout = sb("wout", [P, H, D])
        gw = sb("gw", [P, KD, E])
        wsg = sb("wsg", [P, KD, F])
        wsu = sb("wsu", [P, KD, F])
        wsd = sb("wsd", [F, D])
        cw = sb("cw", [P, 5, 4])
        cb = sb("cb", [P, 5])
        abc = sb("abc", [P, H])
        dtb = sb("dtb", [P, H])
        dsk = sb("dsk", [P, H])
        bias_b = sb("bias_b", [P, E])
        ident = sb("ident", [P, P])
        tri = sb("tri", [P, P])
        strict = sb("strict", [P, P])
        ones = sb("ones", [P, P])
        rank_rev = sb("rank_rev", [P, L])
        spare_i = sb("spare_i", [P, 1], I32)
        spare = sb("spare", [P, 1])
        zrow = sb("zrow", [P, ROW])
        xin = sb("xin", [P, 2, TILES, D])
        st6 = sb("st6", [P, TILES, 6])
        mv = sb("mv", [P, TILES, 2])
        nw = sb("nw", [P, 4, TILES])
        nwi = sb("nwi", [P, TILES], I32)
        xn = sb("xn", [P, TILES, D])
        xnT = sb("xnT", [P, KD, L])
        acc = sb("acc", [P, 2, L])
        rank_i = acc[:, 0].bitcast(I32)
        cth = sb("cth", [P, 2, L])
        zth = sb("zth", [P, 2, L])
        xc = sb("xc", [P, 2, 5, L])
        ct0 = sb("ct0", [N, 2, L])
        sz = sb("sz", [P, 2, H, L])
        dtv = sb("dtv", [P, 8, TILES * H])
        dth = sb("dth", [P, 2, TILES * H])
        dA = sb("dA", [P, 2, TILES * H])
        datri = sb("datri", [P, 2, H, P])
        xd = sb("xd", [P, 2, H, HD])
        Ex = sb("Ex", [P, 2, H, P])
        cbm = sb("cbm", [P, 2, P])
        sm = sb("sm", [P, 2, P + 6])
        ec = sb("ec", [P, 2, 6])
        Wt = sb("Wt", [P, 2, H, P])
        bd = sb("bd", [P, 2, H, N])
        cs = sb("cs", [P, 2, H, N])
        csT = sb("csT", [P, 2, H, P])
        S = sb("S", [P, 2, 2, HD])
        xcd = sb("xcd", [P, 2, H, P])
        yt = xcd
        sq = sb("sq", [P, 2, H, P])
        sqh = sq[:, :, 0:2]
        g = sb("g", [P, 2, H, L])
        ss = sb("ss", [P, 2, L])
        xres = sb("xres", [P, TILES, D])
        rv = sb("rv", [P, 4, TILES])
        rvi = sb("rvi", [P, TILES], I32)
        x1 = sb("x1", [P, TILES, D])
        st6c = sb("st6c", [P, TILES, 6])
        mvc = sb("mvc", [P, TILES, 2])
        nwc = sb("nwc", [P, 4, TILES])
        nwci = sb("nwci", [P, TILES], I32)
        xr = sb("xr", [P, TILES, ROW])
        x2T = sb("x2T", [P, KD, L])
        lex = sb("lex", [P, TILES, E])
        sc = sb("sc", [P, TILES, E])
        sbz = sb("sbz", [P, TILES, E])
        hi = sb("hi", [P, TILES * G, 4])
        lo = sb("lo", [P, TILES * G, 4])
        hi2 = sb("hi2", [P, TILES * G, 2])
        lo2 = sb("lo2", [P, TILES * G, 2])
        mn2 = sb("mn2", [P, TILES * G, 2])
        gsx = sb("gsx", [P, TILES, G + 4])
        gs3 = sb("gs3", [P, 4, TILES * G])
        m8g = sb("m8g", [P, TILES, 8])
        grp = sb("grp", [P, TILES, G + 4])
        gm = sb("gm", [P, TILES, G])
        gneg = sb("gneg", [P, TILES, G])
        tmp = sb("tmp", [P, TILES, E])
        m8e = sb("m8e", [P, TILES, 8])
        rep = lex
        sel = sb("sel", [P, TILES, E])
        wsum = sb("wsum", [P, TILES])
        wrec = sb("wrec", [P, TILES])
        gth = sb("gth", [F, L])
        hs = sb("hs", [F, L])
        yo = sb("yo", [P, TILES, D])
        keys = sb("keys", [P, 2, L])
        first = sb("first", [P, CAP])
        lists = sb("lists", [P, NSEQ // 2, CAP])
        kfirst = sb("kfirst", [E, CAP])
        ktok = sb("ktok", [E, CAP])
        tokT = sb("tokT", [P, ET])
        idxT = sb("idxT", [P, ET], I32)
        idxc = sb("idxc", [P, WRING, 1], I32)
        tokc = sb("tokc", [P, WRING, 1])
        wgr = sb("wgr", [P, WRING, 2, KD, F])
        wur = sb("wur", [P, WRING, 2, KD, F])
        wdr = sb("wdr", [F, WRING, 2, D])
        wcol = sb("wcol", [P, 2, 1])
        cnt = sb("cnt", [P, 2, 1])
        sidx = sb("sidx", [P, 2, 2])
        sidxi = sb("sidxi", [P, WRING, 1], I32)
        flat, used = {"g": g[:].rearrange("p a h l -> p (a h l)"), "sz": sz[:].rearrange("p a h l -> p (a h l)")}, {"g": 0, "sz": 0}

        def part(n, of="g", rows_=P):
            used[of] += n
            return flat[of][0:rows_, used[of] - n:used[of]]

        xg = part(WRING * ROW).rearrange("p (n d) -> p n d", n=WRING)
        xgT = part(2 * D).rearrange("p (n k q) -> p n k q", n=2, k=KD)
        ow = part(2 * D).rearrange("p (n d) -> p n d", n=2)
        oc = part(WRING * D).rearrange("p (n d) -> p n d", n=WRING)
        eq = part(2 * P).rearrange("p (n q) -> p n q", n=2)
        eqs = part(2 * P).rearrange("p (n q) -> p n q", n=2)
        base = part(NSEQ // 2, "sz")
        gk = part(NSEQ // 2 * CAP, "sz").rearrange("p (u q) -> p u q", q=CAP)
        cat = part(2 * NSEQ * CAP, "sz", E).rearrange("p (n q) -> p n q", n=2)
        eth, ehg, ehs = (part(2 * P, "sz", F).rearrange("p (n q) -> p n q", n=2) for _ in range(3))

        bTR = bank("bTR")
        bR = [bank("bR0"), bank("bR1")]
        bXT = bank("bXT")
        bSEG = bank("bSEG")
        bSM = bank("bSM")
        bCS = bank("bCS")
        bY = bank("bY")

        sems = {}

        def S_(name):
            if name not in sems:
                sems[name] = sem(name)
            return sems[name]

        w_loaded = S_("w_loaded")
        consts_ready = S_("consts_ready")
        pool_const = S_("pool_const")
        abc_exp = S_("abc_exp")
        abc_ready = S_("abc_ready")
        x_loaded = [S_("x_loaded0"), S_("x_loaded1")]
        xres_loaded = S_("xres_loaded")
        ct_moved = S_("ct_moved")
        rows_stored = S_("rows_stored")
        y_stored = S_("y_stored")
        pad_stored = S_("pad_stored")
        xn_ready = S_("xn_ready")
        ln1_step = S_("ln1_step")
        trA_ready, trA_copied = S_("trA_ready"), S_("trA_copied")
        trC_ready, trC_copied = S_("trC_ready"), S_("trC_copied")
        projA_ready, projC_ready = S_("projA_ready"), S_("projC_ready")
        dt_read, ssq_read, gate_read, keys_ready = S_("dt_read"), S_("ssq_read"), S_("gate_read"), S_("keys_ready")
        tap_ready, conv_step, conv_ready, cth_ready, xc_ready = (
            S_("tap_ready"), S_("conv_step"), S_("conv_ready"), S_("cth_ready"), S_("xc_ready"))
        cth_step = S_("cth_step")
        zth_ready, sz_ready = S_("zth_ready"), S_("sz_ready")
        dt_step, dtabs_ready, dte_ready, dt_ready = (
            S_("dt_step"), S_("dtabs_ready"), S_("dte_ready"), S_("dt_ready"))
        datri_ready, seg_ready, ex_ready = S_("datri_ready"), S_("seg_ready"), S_("ex_ready")
        xt_ready, xd_ready = S_("xt_ready"), S_("xd_ready")
        small_ready, cb_ready, ec_ready = S_("small_ready"), S_("cb_ready"), S_("ec_ready")
        w_ready, bd_ready, cs_ready = S_("w_ready"), S_("bd_ready"), S_("cs_ready")
        cst_ready, cst_copied = S_("cst_ready"), S_("cst_copied")
        ds_ready, s_ready = S_("ds_ready"), S_("s_ready")
        y_ready, xcd_ready, yt_ready = S_("y_ready"), S_("xcd_ready"), S_("yt_ready")
        g_ready, sq_ready, sqh_step, ss_ready = S_("g_ready"), S_("sq_ready"), S_("sqh_step"), S_("ss_ready")
        c_step, x1_ready, x2_ready, lex_ready = S_("c_step"), S_("x1_ready"), S_("x2_ready"), S_("lex_ready")
        sel_ready, rw_ready = S_("sel_ready"), S_("rw_ready")
        gth_ready, hs_ready, yo_ready = S_("gth_ready"), S_("hs_ready"), S_("yo_ready")
        take_step, key_step = S_("take_step"), S_("key_step")
        merge_step, ktok_ready, tokt_ready, idx_ready = (
            S_("merge_step"), S_("ktok_ready"), S_("tokt_ready"), S_("idx_ready"))
        wx_loaded = [S_(f"wx_loaded{n}") for n in range(WRING)]
        idxc_ready, gathered = S_("idxc_ready"), [S_(f"gathered{n}") for n in range(WRING)]
        scattered = S_("scattered")
        xgt_ready, xgt_copied = S_("xgt_ready"), S_("xgt_copied")
        gu_ready, eth_ready, e_step, ehs_ready = S_("gu_ready"), S_("eth_ready"), S_("e_step"), S_("ehs_ready")
        down_ready, ow_ready = S_("down_ready"), S_("ow_ready")
        tokc_ready, rowb_ready, eq_ready, sidx_ready = (
            S_("tokc_ready"), S_("rowb_ready"), S_("eq_ready"), S_("sidx_ready"))
        sum_ready, oc_ready = S_("sum_ready"), S_("oc_ready")

        CONSTS = 9
        LOADS = 14
        LN_STEPS, DT_STEPS, CONV_STEPS = 20, 16, 2 * 5
        C_STEPS = 66

        waits_passed = S_("waits_passed")

        def apart(eng):
            eng.sem_inc(waits_passed, 1)

        def wait_read(eng, name, seq):
            if name in CONV:
                eng.wait_ge(conv_ready, at(seq, len(CONV), CONV.index(name)))
            elif name in ZT:
                eng.wait_ge(sz_ready, at(seq, len(ZT), ZT.index(name)))
            elif name in ("out0", "out1"):
                eng.wait_ge(x1_ready, at(seq, 2, int(name[3])))
            elif name in ("down0", "down1"):
                eng.wait_ge(yo_ready, at(seq, 2, int(name[4])))
            else:
                reader = {"dt": dt_read, "ssq": ssq_read, "router": lex_ready, "gate": gate_read,
                          "up": hs_ready, "sel": keys_ready}[name]
                eng.wait_ge(reader, at(seq, 1))

        def slot_wait(pe, name, seq, hasA, hasC, before):
            order = [n for n, st in SLOTS if (st == "A" and hasA) or (st == "C" and hasC)]
            it = seq - 1 if name in A_SLOTS else seq + 1
            last = [n for n in order[:order.index(name)] if BANK[n] == BANK[name]][-1:]
            if not last:
                if before is None:
                    return
                it = it - 1
                stages = [[n for n, st in SLOTS if BANK[n] == BANK[name] and st == "AC"[c] and before[c]]
                          for c in range(2)]
                order = [n for n, _ in SLOTS]
                last = sorted((x[-1] for x in stages if x), key=order.index)
                if before[1] != "maybe" or last[-1] in A_SLOTS:
                    last = last[-1:]
            for n in last:
                wait_read(pe, n, it + 1 if n in A_SLOTS else it - 1)

        def schedule(eng, iteration):
            iteration(-1, 1, True, False, False, None)
            iteration(0, 0, True, True, False, (True, False))
            with eng.Fori(0, (NSEQ - 2) // 2) as pair:
                iteration(2 * pair + 1, 1, True, True, True, None)
                iteration(2 * pair + 2, 0, True, True, True, None)
            iteration(NSEQ - 1, 1, False, True, True, (True, True))
            iteration(NSEQ, 0, False, False, True, (False, True))

        block = ctx.enter_context(nc.Block())

        @block.sync
        def _(sp):
            def load_x(s, par, reuse):
                src = x_t[s] if isinstance(s, int) else x_t[bass.ds(s, 1)].rearrange("s p j d -> p (s j) d")
                if reuse:
                    sp.wait_ge(xn_ready, at(s - 2, 1))
                sp.dma_start(xin[:, par], src).then_inc(x_loaded[par], 16)

            load_x(0, 0, False)
            for dst, src in ((win, w_in), (cw, conv_w), (cb, conv_b), (dtb, dt_bias), (abc, a_log),
                             (dsk, dskip), (wout, w_out), (gw, gate_w), (wsg, ws_gate), (wsu, ws_up),
                             (wsd, ws_down), (bias_b, bias)):
                sp.dma_start(dst[:], src).then_inc(w_loaded, 16)
            load_x(1, 1, False)
            sp.wait_ge(consts_ready, 1)
            sp.dma_start(rows[T:T + P, :], zrow[:]).then_inc(pad_stored, 16)
            sp.dma_start(out[T:T + P, :], zrow[:, 0:D]).then_inc(pad_stored, 16)

            def expert_weights(i, slot, reuse):
                if reuse:
                    sp.wait_ge(down_ready, i - WRING + 1)
                    idx = sp.snap(i)
                    g_src = w_gate[bass.ds(idx, 1)].rearrange("i p e k f -> p (i e) k f")
                    u_src = w_up[bass.ds(idx, 1)].rearrange("i p e k f -> p (i e) k f")
                    d_src = w_down[bass.ds(idx, 1)].rearrange("i f e d -> f (i e) d")
                else:
                    g_src, u_src, d_src = w_gate[i], w_up[i], w_down[i]
                sp.dma_start(wgr[:, slot], g_src).then_inc(wx_loaded[slot], 16)
                sp.dma_start(wur[:, slot], u_src).then_inc(wx_loaded[slot], 16)
                sp.dma_start(wdr[:, slot], d_src).then_inc(wx_loaded[slot], 16)

            for i in range(WRING):
                expert_weights(i, i, False)

            def move_c(s, par):
                sp.wait_ge(xc_ready, at(s, len(CONV), 0))
                if not isinstance(s, int) or s >= 2:
                    sp.wait_ge(small_ready, at(s - 2, TILES, TILES - 1))
                sp.dma_start(ct0[:, par], xc[N:2 * N, par, 4, :]).then_inc(ct_moved, 16)

            def load_residual(s):
                if not isinstance(s, int) or s >= 1:
                    sp.wait_ge(x1_ready, at(s - 1, 2, 1))
                src = x_t[s] if isinstance(s, int) else x_t[bass.ds(s, 1)].rearrange("s p j d -> p (s j) d")
                sp.dma_start(xres[:], src).then_inc(xres_loaded, 16)

            def store_c(s):
                if isinstance(s, int):
                    r_dst, y_dst = rows_t[s], out_t[s]
                else:
                    r_dst = rows_t[bass.ds(s, 1)].rearrange("s p j d -> p (s j) d")
                    y_dst = out_t[bass.ds(s, 1)].rearrange("s p j d -> p (s j) d")
                sp.wait_ge(rw_ready, at(s, 1))
                sp.dma_start(r_dst, xr[:]).then_inc(rows_stored, 16)
                sp.wait_ge(yo_ready, at(s, 2, 1))
                sp.dma_start(y_dst, yo[:]).then_inc(y_stored, 16)

            def iteration(it, par, hasA, hasB, hasC, before, more):
                if hasC:
                    load_residual(it - 1)
                if hasA:
                    move_c(it + 1, 1 - par)
                if more:
                    load_x(it + 2, par, True)
                if hasC:
                    store_c(it - 1)

            iteration(-1, 1, True, False, False, None, False)
            iteration(0, 0, True, True, False, None, True)
            with sp.Fori(0, (NSEQ - 4) // 2) as pair:
                iteration(2 * pair + 1, 1, True, True, True, None, True)
                iteration(2 * pair + 2, 0, True, True, True, None, True)
            iteration(NSEQ - 3, 1, True, True, True, None, True)
            iteration(NSEQ - 2, 0, True, True, True, None, False)
            iteration(NSEQ - 1, 1, False, True, True, None, False)
            iteration(NSEQ, 0, False, False, True, None, False)
            with sp.Fori(1, ET // WRING) as lot:
                for n in range(WRING):
                    expert_weights(WRING * lot + n, n, True)
            sp.wait_ge(scattered, 16 * ET)
            sp.wait_ge(rows_stored, 16 * NSEQ)
            sp.wait_ge(y_stored, 16 * NSEQ)
            sp.wait_ge(pad_stored, 32)

        @block.tensor
        def _(pe):
            mm, tr = nc.tensor.matmul, nc.tensor.transpose

            def front(s, par, j):
                b = j % 2
                tile = slice(j * P, (j + 1) * P)
                if j == 0:
                    pe.wait_ge(xc_ready, at(s, len(CONV), len(CONV) - 1))
                    pe.wait_ge(dt_ready, at(s, 1))
                    pe.wait_ge(ct_moved, 16 * (s + 1))
                    if not isinstance(s, int) or s > 0:
                        pe.wait_ge(xd_ready, at(s - 1, TILES, TILES - 1))
                        pe.wait_ge(ex_ready, at(s - 1, TILES, TILES - 1))
                        pe.wait_ge(cb_ready, at(s - 1, TILES, TILES - 1))
                else:
                    pe.wait_ge(xd_ready, at(s, TILES, j - 1))
                    pe.wait_ge(ex_ready, at(s, TILES, j - 1))
                    pe.wait_ge(cb_ready, at(s, TILES, j - 1))
                for h in range(H):
                    last = tr(bXT[:, h * HD:(h + 1) * HD], xc[:, par, h, tile], ident[:])
                last.then_inc(xt_ready, 1)
                pe.wait_ge(datri_ready, at(s, TILES, j))
                mm(bSEG[:], strict[:], datri[:, b].rearrange("p h q -> p (h q)"),
                   start=True, stop=True).then_inc(seg_ready, 1)
                mm(bSM[:, 0:P], xc[0:N, par, 4, tile], ct0[:, par, tile], start=True, stop=True)
                tr(bSM[:, P:2 * P], xc[:, par, 4, tile], ident[:])
                dcol = dA[:, par, j * H:(j + 1) * H]
                last = mm(bSM[:, 2 * P:2 * P + H], tri[:], dcol, start=True, stop=True)
                for hl in range(2):
                    last = mm(bSM[hl * N:(hl + 1) * N, 2 * P + H:2 * P + H + 2], ones[:, 0:N],
                              dcol.rearrange("p (a b) -> p a b", b=2)[:, :, hl], start=True, stop=True)
                last.then_inc(small_ready, 1)

            def turn_c(s, j):
                pe.wait_ge(cs_ready, at(s, TILES - 1, j - 1))
                pe.wait_ge(s_ready, at(s, TILES - 1, j - 1))
                c2 = cs[:, j % 2].rearrange("p (a h) n -> p a (h n)", a=2)
                for a in range(2):
                    last = tr(bCS[:, a * P:(a + 1) * P], c2[:, a], ident[:])
                last.then_inc(cst_ready, 1)

            def back(s, j):
                b = j % 2
                pe.wait_ge(xd_ready, at(s, TILES, j))
                if j < TILES - 1:
                    pe.wait_ge(bd_ready, at(s, TILES - 1, j))
                    if j == 0:
                        if not isinstance(s, int) or s > 0:
                            pe.wait_ge(cst_copied, at(s - 1, TILES - 1, TILES - 2))
                    else:
                        pe.wait_ge(cst_copied, at(s, TILES - 1, j - 1))
                    for h in range(H):
                        a, hl = divmod(h, 2)
                        last = mm(bCS[hl * N:(hl + 1) * N, 2 * P + a * HD:2 * P + (a + 1) * HD], bd[:, b, h],
                                  xd[:, b, h], start=True, stop=True)
                    last.then_inc(ds_ready, 1)
                pe.wait_ge(w_ready, at(s, TILES, j))
                if j > 0:
                    pe.wait_ge(cst_copied, at(s, TILES - 1, j - 1))
                    pe.wait_ge(yt_ready, at(s, TILES, j - 1))
                elif not isinstance(s, int) or s > 0:
                    pe.wait_ge(yt_ready, at(s - 1, TILES, TILES - 1))
                for h in range(H):
                    a, hl = divmod(h, 2)
                    last = mm(bY[:, h * P:(h + 1) * P], xd[:, b, h], Wt[:, b, h], start=True, stop=(j == 0))
                    if j > 0:
                        last = mm(bY[:, h * P:(h + 1) * P], S[:, b, a], csT[:, b, h], start=False, stop=True)
                last.then_inc(y_ready, 1)

            def turn_in(s, k, prev):
                if k == 0:
                    pe.wait_ge(xn_ready, at(s, 1))
                    for read in prev:
                        pe.wait_ge(*read)
                else:
                    pe.wait_ge(trA_copied, at(s, KD, k - 1))
                for j in range(TILES):
                    last = tr(bTR[:, j * P:(j + 1) * P], xn[:, j, k * P:(k + 1) * P], ident[:])
                last.then_inc(trA_ready, 1)

            def turn_mid(s, k, prev):
                if k == 0:
                    pe.wait_ge(x2_ready, at(s, 1))
                    pe.wait_ge(*prev)
                else:
                    pe.wait_ge(trC_copied, at(s, KD, k - 1))
                for j in range(TILES):
                    last = tr(bTR[:, j * P:(j + 1) * P], xr[:, j, k:D:KD], ident[:])
                last.then_inc(trC_ready, 1)

            def project(s, name):
                dst = bR[BANK[name]]
                if name == "m8":
                    pe.wait_ge(trA_copied, at(s, KD, KD - 1))
                if name == "dt":
                    for j in range(TILES):
                        for k in range(KD):
                            last = mm(dst[:, j * H:(j + 1) * H], xnT[:, k, j * P:(j + 1) * P],
                                      win[:, k, PROJ:PROJ + H], start=(k == 0), stop=(k == KD - 1))
                else:
                    m = int(name[1])
                    for k in range(KD):
                        last = mm(dst[:], win[:, k, m * P:(m + 1) * P], xnT[:, k, :],
                                  start=(k == 0), stop=(k == KD - 1))
                last.then_inc(projA_ready, 1)

            def finish(s, par, name):
                dst = bR[BANK[name]]
                if name == "ssq":
                    pe.wait_ge(ss_ready, at(s, TILES, TILES - 1))
                    for j in range(TILES):
                        last = mm(dst[:, j:j + 1], ss[:, par, j * P:(j + 1) * P], ones[:, 0:1], start=True, stop=True)
                elif name in ("out0", "out1"):
                    pe.wait_ge(g_ready, at(s, TILES, TILES - 1))
                    for half in range(2):
                        j = 2 * int(name[3]) + half
                        for h in range(H):
                            last = mm(dst[:, half * D:(half + 1) * D], g[:, par, h, j * P:(j + 1) * P],
                                      wout[:, h], start=(h == 0), stop=(h == H - 1))
                elif name == "router":
                    pe.wait_ge(trC_copied, at(s, KD, KD - 1))
                    for j in range(TILES):
                        for k in range(KD):
                            last = mm(dst[:, j * E:(j + 1) * E], x2T[:, k, j * P:(j + 1) * P], gw[:, k],
                                      start=(k == 0), stop=(k == KD - 1))
                elif name in ("gate", "up"):
                    w = wsg if name == "gate" else wsu
                    for k in range(KD):
                        last = mm(dst[0:F, :], w[:, k], x2T[:, k], start=(k == 0), stop=(k == KD - 1))
                elif name in ("down0", "down1"):
                    pe.wait_ge(hs_ready, at(s, 1))
                    for half in range(2):
                        j = 2 * int(name[4]) + half
                        last = mm(dst[:, half * D:(half + 1) * D], hs[:, j * P:(j + 1) * P], wsd[:],
                                  start=True, stop=True)
                else:
                    pe.wait_ge(sel_ready, at(s, 1))
                    apart(pe)
                    for j in range(TILES):
                        last = tr(dst[0:E, j * P:(j + 1) * P], sel[:, j], ident[:])
                last.then_inc(projC_ready, 1)

            pe.wait_ge(consts_ready, 1)
            pe.wait_ge(w_loaded, 16 * 12)

            def iteration(it, par, hasA, hasB, hasC, before):
                in_loop = before is None and not isinstance(it, int)
                prior = (True, True) if in_loop else before
                if in_loop and par == 1:
                    prior = (True, "maybe")

                def fill(*names):
                    for name in names:
                        if name == "LN1":
                            if hasA:
                                prev = []
                                if not isinstance(it, int) or it == 0:
                                    prev.append((trA_copied, at(it, KD, KD - 1)))
                                if not isinstance(it, int):
                                    prev.append((trC_copied, at(it - 2, KD, KD - 1)))
                                turn_in(it + 1, 0, prev)
                                turn_in(it + 1, 1, [])
                        elif name == "LN2":
                            if hasC:
                                prev = (trA_copied, at(it + 1, KD, KD - 1)) if hasA else \
                                       (trC_copied, at(it - 2, KD, KD - 1))
                                turn_mid(it - 1, 0, prev)
                                turn_mid(it - 1, 1, None)
                        elif name in A_SLOTS:
                            if hasA:
                                slot_wait(pe, name, it + 1, hasA, hasC, prior)
                                project(it + 1, name)
                        elif hasC:
                            slot_wait(pe, name, it - 1, hasA, hasC, prior)
                            finish(it - 1, 1 - par, name)

                if hasB:
                    front(it, par, 0)
                fill("ssq", "out0")
                fill("out1", "LN1")
                if hasB:
                    back(it, 0)
                    front(it, par, 1)
                fill("m8", "dt")
                if hasB:
                    turn_c(it, 1)
                fill("LN2", "m4")
                if hasB:
                    back(it, 1)
                    front(it, par, 2)
                fill("m5", "m6")
                if hasB:
                    turn_c(it, 2)
                fill("router", "gate", "up")
                if hasB:
                    back(it, 2)
                    front(it, par, 3)
                fill("m7", "m0", "m1")
                if hasB:
                    turn_c(it, 3)
                fill("down0", "down1")
                if hasB:
                    back(it, 3)
                fill("m2", "m3", "sel")

            schedule(pe, iteration)

            pe.wait_ge(ktok_ready, 1)
            wait_read(pe, "sel", NSEQ - 1)
            tr(bTR[0:CAP, 0:E], ktok[:], ident[0:E, 0:E]).then_inc(tokt_ready, 1)
            pe.wait_ge(idx_ready, 1)

            def expert_tile(i, n, first):
                b = n % 2
                some = not isinstance(i, int)
                pe.wait_ge(tokc_ready, i + 1)
                if some or i > 0:
                    pe.wait_ge(eq_ready, i)
                mm(bSM[:, 0:P], tokc[:, n].to_broadcast([P, P]), ident[:], start=True, stop=True).then_inc(rowb_ready, 1)
                pe.wait_ge(gathered[n], 16 * (i // WRING + 1) if isinstance(i, int) else (i - n) * 4 + 16)
                if some or i > 0:
                    pe.wait_ge(xgt_copied, i)
                for k in range(KD):
                    last = tr(bXT[:, k * P:(k + 1) * P], xg[:, n, k:D:KD], ident[:])
                last.then_inc(xgt_ready, 1)
                pe.wait_ge(xgt_copied, i + 1)
                pe.wait_ge(wx_loaded[n], 48 * (i // WRING + 1) if isinstance(i, int) else (i - n) * 12 + 48)
                if some or i > 0:
                    pe.wait_ge(ehs_ready, i)
                for e in range(2):
                    for u, w in enumerate((wgr, wur)):
                        o = u * P + e * 64
                        for k in range(KD):
                            last = mm(bSEG[0:F, o:o + 64], w[:, n, e, k], xgT[:, b, k, e * 64:(e + 1) * 64],
                                      start=(k == 0), stop=(k == KD - 1))
                last.then_inc(gu_ready, 1)
                pe.wait_ge(ehs_ready, i + 1)
                if some or i > 0:
                    pe.wait_ge(ow_ready, i)
                for e in range(2):
                    last = mm(bY[e * 64:(e + 1) * 64, 0:D], ehs[:, b, e * 64:(e + 1) * 64], wdr[:, n, e],
                              start=True, stop=True)
                last.then_inc(down_ready, 1)
                pe.wait_ge(ow_ready, i + 1)
                pe.wait_ge(eq_ready, i + 1)
                if some or i > 0:
                    pe.wait_ge(oc_ready, i)
                mm(bCS[:, 0:D], eq[:, b], ow[:, b], start=True, stop=True).then_inc(sum_ready, 1)

            for n in range(WRING):
                expert_tile(n, n, True)
            with pe.Fori(1, ET // WRING) as lot:
                for n in range(WRING):
                    expert_tile(WRING * lot + n, n, False)

        @block.scalar
        def _(act):
            fn = nc.scalar.activation

            def some(s):
                return not isinstance(s, int)

            def copy_in(s, k):
                act.wait_ge(trA_ready, at(s, KD, k))
                fn(xnT[:, k], bTR[:], ACT.Copy).then_inc(trA_copied, 1)

            def copy_mid(s, k):
                act.wait_ge(trC_ready, at(s, KD, k))
                fn(x2T[:, k], bTR[:], ACT.Copy).then_inc(trC_copied, 1)

            def tap(s, n):
                c = 4 if n == 0 else n - 1
                act.wait_ge(projA_ready, at(s, len(A_SLOTS), A_SLOTS.index(CONV[n])))
                if n >= 2:
                    act.wait_ge(xc_ready, at(s, 5, n - 2))
                elif some(s) or s > 0:
                    act.wait_ge(xc_ready, at(s - 1, 5, n + 3))
                fn(acc[:, n % 2], bR[BANK[CONV[n]]][:], ACT.Identity, bias=cb[:, c:c + 1],
                   scale=cw[:, c, 3:4]).then_inc(tap_ready, 1)

            def conv_tanh(s, n):
                act.wait_ge(conv_ready, at(s, 5, n))
                fn(cth[:, n % 2], acc[:, n % 2], ACT.Tanh, scale=0.5).then_inc(cth_step, 1)
                act.wait_ge(cth_step, at(s, 5, n))
                fn(cth[:, n % 2], cth[:, n % 2], ACT.Copy, bias=1.0).then_inc(cth_ready, 1)

            def z_tanh(s, n):
                act.wait_ge(projA_ready, at(s, len(A_SLOTS), A_SLOTS.index(ZT[n])))
                if n >= 2:
                    act.wait_ge(sz_ready, at(s, 4, n - 2))
                elif some(s) or s > 0:
                    act.wait_ge(sz_ready, at(s - 1, 4, n + 2))
                fn(zth[:, n % 2], bR[BANK[ZT[n]]][:], ACT.Tanh, scale=0.5).then_inc(zth_ready, 1)

            def dt_exp(s):
                act.wait_ge(dtabs_ready, at(s, 1))
                fn(dtv[:, 2], dtv[:, 1], ACT.Exp).then_inc(dte_ready, 1)

            def seg_exp(s, j):
                b = j % 2
                act.wait_ge(seg_ready, at(s, TILES, j))
                if j >= 2:
                    act.wait_ge(w_ready, at(s, TILES, j - 2))
                    act.wait_ge(bd_ready, at(s, 3, j - 2))
                elif some(s) or s > 0:
                    act.wait_ge(w_ready, at(s - 1, TILES, j + 2))
                    act.wait_ge(bd_ready, at(s - 1, 3, min(j + 2, 2)))
                fn(Ex[:, b].rearrange("p h q -> p (h q)"), bSEG[:], ACT.Exp).then_inc(ex_ready, 1)
                act.wait_ge(cb_ready, at(s, TILES, j))
                if j >= 2:
                    act.wait_ge(s_ready, at(s, 3, j - 2))
                    if j == 3:
                        act.wait_ge(cs_ready, at(s, 3, 0))
                elif some(s) or s > 0:
                    act.wait_ge(s_ready, at(s - 1, 3, 2))
                    act.wait_ge(cs_ready, at(s - 1, 3, 2 if j == 1 else 1))
                fn(ec[:, b], sm[:, b, P:P + 6], ACT.Exp).then_inc(ec_ready, 1)

            def copy_c(s, j):
                act.wait_ge(cst_ready, at(s, 3, j - 1))
                if j >= 3:
                    act.wait_ge(y_ready, at(s, TILES, j - 2))
                elif some(s) or s > 0:
                    act.wait_ge(y_ready, at(s - 1, TILES, TILES - 1))
                for hl in range(2):
                    r = slice(hl * N, (hl + 1) * N)
                    last = fn(csT[r, j % 2].rearrange("p (a h) q -> p a h q", h=2)[:, :, hl],
                              bCS[r, 0:2 * P].rearrange("p (a q) -> p a q", a=2), ACT.Copy)
                last.then_inc(cst_copied, 1)

            def square(s, j):
                act.wait_ge(yt_ready, at(s, TILES, j))
                if j >= 2:
                    act.wait_ge(ss_ready, at(s, TILES, j - 2))
                elif some(s) or s > 0:
                    act.wait_ge(ss_ready, at(s - 1, TILES, j + 2))
                fn(sq[:, j % 2], yt[:, j % 2], ACT.Square).then_inc(sq_ready, 1)

            def router_exp(s):
                act.wait_ge(projC_ready, at(s, len(C_SLOTS), C_SLOTS.index("router")))
                if some(s) or s > 0:
                    act.wait_ge(sel_ready, at(s - 1, 1))
                fn(lex[:].rearrange("p j e -> p (j e)"), bR[BANK["router"]][:, 0:TILES * E], ACT.Exp,
                   scale=-1.0).then_inc(lex_ready, 1)

            def gate_tanh(s):
                act.wait_ge(projC_ready, at(s, len(C_SLOTS), C_SLOTS.index("gate")))
                if some(s) or s > 0:
                    act.wait_ge(hs_ready, at(s - 1, 1))
                fn(gth[:], bR[BANK["gate"]][0:F, :], ACT.Tanh, scale=0.5).then_inc(gth_ready, 1)

            act.wait_ge(w_loaded, 16 * 12)
            act.wait_ge(consts_ready, 1)
            fn(abc[:], abc[:], ACT.Exp).then_inc(abc_exp, 1)

            def iteration(it, par, hasA, hasB, hasC, before):
                a, c = it + 1, it - 1
                if hasB:
                    seg_exp(it, 0)
                if hasA:
                    copy_in(a, 0)
                    copy_in(a, 1)
                if hasB:
                    square(it, 0)
                    seg_exp(it, 1)
                if hasA:
                    tap(a, 0)
                    dt_exp(a)
                if hasB:
                    copy_c(it, 1)
                if hasA:
                    conv_tanh(a, 0)
                if hasC:
                    copy_mid(c, 0)
                    copy_mid(c, 1)
                if hasA:
                    tap(a, 1)
                if hasB:
                    square(it, 1)
                    seg_exp(it, 2)
                if hasA:
                    conv_tanh(a, 1)
                    tap(a, 2)
                if hasB:
                    copy_c(it, 2)
                if hasA:
                    tap(a, 3)
                    conv_tanh(a, 2)
                if hasC:
                    router_exp(c)
                    gate_tanh(c)
                if hasB:
                    square(it, 2)
                    seg_exp(it, 3)
                if hasA:
                    conv_tanh(a, 3)
                    tap(a, 4)
                    z_tanh(a, 0)
                    conv_tanh(a, 4)
                    z_tanh(a, 1)
                if hasB:
                    copy_c(it, 3)
                    square(it, 3)
                if hasA:
                    z_tanh(a, 2)
                    z_tanh(a, 3)

            schedule(act, iteration)

            def expert_tile(i, n):
                b = n % 2
                act.wait_ge(xgt_ready, i + 1)
                if not isinstance(i, int) or i >= 2:
                    act.wait_ge(gu_ready, i - 1)
                fn(xgT[:, b].rearrange("p k q -> p (k q)"), bXT[:, 0:KD * P], ACT.Copy).then_inc(xgt_copied, 1)
                act.wait_ge(gu_ready, i + 1)
                if not isinstance(i, int) or i >= 2:
                    act.wait_ge(ehs_ready, i - 1)
                fn(eth[:, b], bSEG[0:F, 0:P], ACT.Tanh, scale=0.5).then_inc(eth_ready, 1)
                act.wait_ge(sum_ready, i + 1)
                if not isinstance(i, int) or i >= WRING:
                    act.wait_ge(scattered, 16 * (i - WRING + 1))
                fn(oc[:, n], bCS[:, 0:D], ACT.Copy).then_inc(oc_ready, 1)

            for n in range(WRING):
                expert_tile(n, n)
            with act.Fori(1, ET // WRING) as lot:
                for n in range(WRING):
                    expert_tile(WRING * lot + n, n)

        @block.gpsimd
        def _(pool):
            tt = nc.gpsimd.tensor_tensor

            def some(s):
                return not isinstance(s, int)

            nconst = [0]

            def const(ins):
                ins.then_inc(pool_const, 1)
                nconst[0] += 1
                pool.wait_ge(pool_const, nconst[0])

            const(nc.gpsimd.memset(ones[:], 1.0))
            sel_of = nc.gpsimd.affine_select
            const(sel_of(ident[:], ones[:], [[1, P]], ALU.is_equal, 0.0, base=0, channel_multiplier=-1))
            const(sel_of(tri[:], ones[:], [[1, P]], ALU.is_ge, 0.0, base=0, channel_multiplier=-1))
            const(sel_of(strict[:], ones[:], [[-1, P]], ALU.is_gt, 0.0, base=0, channel_multiplier=1))
            const(nc.gpsimd.iota(rank_i, [[-1, L]], base=L, channel_multiplier=0))
            const(nc.gpsimd.tensor_copy(rank_rev[:], rank_i))
            const(nc.gpsimd.iota(spare_i[:], [[0, 1]], base=T, channel_multiplier=1))
            const(nc.gpsimd.tensor_copy(spare[:], spare_i[:]))
            const(nc.gpsimd.memset(zrow[:], 0.0))
            const(nc.gpsimd.memset(csT[:], 0.0))
            nc.gpsimd.memset(gsx[:], -BIG).then_inc(consts_ready, 1)
            pool.wait_ge(abc_ready, 1)
            pool.wait_ge(w_loaded, 16 * 12)

            def decay_in(s, par, j):
                b = j % 2
                if j == 0:
                    pool.wait_ge(dt_ready, at(s, 1))
                if j >= 2:
                    pool.wait_ge(seg_ready, at(s, TILES, j - 2))
                elif some(s) or s > 0:
                    pool.wait_ge(seg_ready, at(s - 1, TILES, j + 2))
                tt(datri[:, b], tri[:].rearrange("p (o q) -> p o q", o=1).to_broadcast([P, H, P]),
                   dA[:, par, j * H:(j + 1) * H].rearrange("p (h o) -> p h o", o=1).to_broadcast([P, H, P]),
                   ALU.mult).then_inc(datri_ready, 1)

            def skip(s, par, j):
                b = j % 2
                if j == 0:
                    pool.wait_ge(xc_ready, at(s, 5, 4))
                for read in (sq_ready, g_ready):
                    if j >= 2:
                        pool.wait_ge(read, at(s, TILES, j - 2))
                    elif some(s) or s > 0:
                        pool.wait_ge(read, at(s - 1, TILES, j + 2))
                tt(xcd[:, b], xc[:, par, 0:H, j * P:(j + 1) * P],
                   dsk[:].rearrange("p (h o) -> p h o", o=1).to_broadcast([P, H, P]),
                   ALU.mult).then_inc(xcd_ready, 1)

            def weigh(s, j):
                b = j % 2
                pool.wait_ge(ex_ready, at(s, TILES, j))
                pool.wait_ge(cb_ready, at(s, TILES, j))
                if j >= 2:
                    pool.wait_ge(y_ready, at(s, TILES, j - 2))
                elif some(s) or s > 0:
                    pool.wait_ge(y_ready, at(s - 1, TILES, j + 2))
                tt(Wt[:, b], Ex[:, b], cbm[:, b].rearrange("p (o q) -> p o q", o=1).to_broadcast([P, H, P]),
                   ALU.mult).then_inc(w_ready, 1)

            def conv_silu(s, par, n):
                c = 4 if n == 0 else n - 1
                pool.wait_ge(cth_ready, at(s, 5, n))
                if n == 0 and (some(s) or s >= 2):
                    pool.wait_ge(y_ready, at(s - 2, TILES, TILES - 1))
                    pool.wait_ge(xcd_ready, at(s - 2, TILES, TILES - 1))
                    pool.wait_ge(ct_moved, 16 * (s - 1))
                tt(xc[:, par, c], cth[:, n % 2], acc[:, n % 2], ALU.mult).then_inc(xc_ready, 1)

            def sum_squares(s, par, j):
                b = j % 2
                pool.wait_ge(sq_ready, at(s, TILES, j))
                if j == 0 and (some(s) or s >= 2):
                    pool.wait_ge(projC_ready, at(s - 2, len(C_SLOTS), len(C_SLOTS) - 1))
                tt(sqh[:, b], sq[:, b, 0:2], sq[:, b, 2:4], ALU.add).then_inc(sqh_step, 1)
                pool.wait_ge(sqh_step, at(s, TILES, j))
                tt(ss[:, par, j * P:(j + 1) * P], sqh[:, b, 0], sqh[:, b, 1], ALU.add).then_inc(ss_ready, 1)

            def iteration(it, par, hasA, hasB, hasC, before):
                a, ap = it + 1, 1 - par
                if hasB:
                    decay_in(it, par, 0)
                    decay_in(it, par, 1)
                    skip(it, par, 0)
                    weigh(it, 0)
                    sum_squares(it, par, 0)
                    decay_in(it, par, 2)
                    skip(it, par, 1)
                    weigh(it, 1)
                if hasA:
                    conv_silu(a, ap, 0)
                if hasB:
                    sum_squares(it, par, 1)
                    decay_in(it, par, 3)
                    skip(it, par, 2)
                    weigh(it, 2)
                if hasA:
                    conv_silu(a, ap, 1)
                    conv_silu(a, ap, 2)
                if hasB:
                    sum_squares(it, par, 2)
                    skip(it, par, 3)
                    weigh(it, 3)
                if hasA:
                    conv_silu(a, ap, 3)
                    conv_silu(a, ap, 4)
                if hasB:
                    sum_squares(it, par, 3)

            schedule(pool, iteration)

            pool.wait_ge(idx_ready, 1)
            pool.wait_ge(rows_stored, 16 * NSEQ)
            pool.wait_ge(y_stored, 16 * NSEQ)
            pool.wait_ge(pad_stored, 32)

            def gather(i, n):
                if some(i) or i >= WRING:
                    pool.wait_ge(ow_ready, i - WRING + 1)
                nc.gpsimd.tensor_copy(idxc[:, n], idxT[:, bass.ds(i, 1)]).then_inc(idxc_ready, 1)
                pool.wait_ge(idxc_ready, i + 1)
                apart(pool)
                nc.gpsimd.indirect_dma_start(out=xg[:, n], out_offset=None, in_=rows[:, :],
                                             in_offset=bass.IndirectOffsetOnAxis(ap=idxc[:, n], axis=0)
                                             ).then_inc(gathered[n], 16)

            def scatter(i, n):
                pool.wait_ge(oc_ready, i + 1)
                pool.wait_ge(sidx_ready, i + 1)
                if some(i) or i > 0:
                    pool.wait_ge(scattered, 16 * i)
                apart(pool)
                nc.gpsimd.indirect_dma_start(out=out[:, :], out_offset=bass.IndirectOffsetOnAxis(ap=sidxi[:, n], axis=0),
                                             in_=oc[:, n], in_offset=None, compute_op=ALU.add
                                             ).then_inc(scattered, 16)

            AHEAD = 2
            for n in range(AHEAD):
                gather(n, n)
            for i in range(WRING):
                gather(i + AHEAD, (i + AHEAD) % WRING)
                scatter(i, i)
            with pool.Fori(1, ET // WRING - 1) as lot:
                for n in range(WRING):
                    gather(WRING * lot + n + AHEAD, (n + AHEAD) % WRING)
                    scatter(WRING * lot + n, n)
            for i in range(ET - WRING, ET):
                if i + AHEAD < ET:
                    gather(i + AHEAD, (i + AHEAD) % WRING)
                scatter(i, i % WRING)

        @block.vector
        def _(dve):
            v = nc.vector
            tt, ts, stt, cp = v.tensor_tensor, v.tensor_scalar, v.scalar_tensor_tensor, v.tensor_copy

            def some(s):
                return not isinstance(s, int)

            def rsqrt(link, y, yi, val):
                link(ts(yi[:], val.bitcast(I32), 1, None, ALU.logical_shift_right))
                link(ts(y[:, 0].bitcast(I32), yi[:], -1.0, float(0x5F3759DF), ALU.mult, ALU.add))
                for _ in range(3):
                    link(tt(y[:, 1], y[:, 0], y[:, 0], ALU.mult))
                    link(tt(y[:, 1], y[:, 1], val, ALU.mult))
                    link(ts(y[:, 1], y[:, 1], -0.5, 1.5, ALU.mult, ALU.add))
                    link(tt(y[:, 0], y[:, 0], y[:, 1], ALU.mult))

            def layernorm(link, src, dst, st, m, y, yi):
                for j in range(TILES):
                    last = v.bn_stats(st[:, j], src[:, j])
                link(last)
                apart(dve)
                for j in range(TILES):
                    last = v.bn_aggr(m[:, j], st[:, j])
                link(last)
                link(ts(y[:, 2], m[:, :, 1], LN_EPS, None, ALU.add))
                rsqrt(link, y, yi, y[:, 2])
                for j in range(TILES):
                    last = ts(dst[:, j, 0:D], src[:, j], m[:, j, 0:1], y[:, 0, j:j + 1], ALU.subtract, ALU.mult)
                return last

            def ln1(s, par):
                c = Chain(dve, ln1_step, s, LN_CHAIN)
                dve.wait_ge(x_loaded[par], (s // 2 + 1) * 16 if isinstance(s, int) else (s - par) * 8 + 16)
                if some(s) or s > 0:
                    dve.wait_ge(trA_ready, at(s - 1, KD, KD - 1))
                    dve.wait_ge(xn_ready, at(s - 1, 1))
                layernorm(c.link, xin[:, par], xn, st6, mv, nw, nwi).then_inc(xn_ready, 1)
                c.done()

            def dt_stage(s, par):
                c = Chain(dve, dt_step, s, DT_CHAIN)
                q = lambda n: dtv[:, n]
                raw = bR[BANK["dt"]][:, 0:TILES * H].rearrange("p (j h) -> p j h", h=H)
                dve.wait_ge(projA_ready, at(s, len(A_SLOTS), A_SLOTS.index("dt")))
                if some(s) or s > 0:
                    dve.wait_ge(dt_ready, at(s - 1, 1))
                tt(dtv[:, 0].rearrange("p (j h) -> p j h", h=H), raw,
                   dtb[:].rearrange("p (o h) -> p o h", o=1).to_broadcast([P, TILES, H]),
                   ALU.add).then_inc(dt_read, 1)
                dve.wait_ge(dt_read, at(s, 1))
                stt(q(1), q(0), -1.0, q(0), ALU.mult, ALU.min).then_inc(dtabs_ready, 1)
                dve.wait_ge(dte_ready, at(s, 1))
                link = c.link
                link(ts(q(3), q(2), 2.0, None, ALU.add))
                link(v.reciprocal(q(4), q(3)))
                link(tt(q(3), q(2), q(4), ALU.mult))
                link(tt(q(4), q(3), q(3), ALU.mult))
                link(ts(q(5), q(4), 1.0 / 17, None, ALU.mult))
                for k in (15, 13, 11, 9, 7, 5, 3):
                    link(stt(q(5), q(5), 1.0 / k, q(4), ALU.add, ALU.mult))
                link(stt(q(5), q(5), 1.0, q(3), ALU.add, ALU.mult))
                link(ts(q(6), q(0), 0.0, None, ALU.max))
                if some(s) or s >= 2:
                    dve.wait_ge(datri_ready, at(s - 2, TILES, TILES - 1))
                    dve.wait_ge(small_ready, at(s - 2, TILES, TILES - 1))
                    dve.wait_ge(xd_ready, at(s - 2, TILES, TILES - 1))
                link(stt(q(7), q(5), 2.0, q(6), ALU.mult, ALU.add))
                link(ts(dth[:, par], q(7), 0.5, None, ALU.mult))
                tt(dA[:, par].rearrange("p (j h) -> p j h", h=H), q(7).rearrange("p (j h) -> p j h", h=H),
                   abc[:].rearrange("p (o h) -> p o h", o=1).to_broadcast([P, TILES, H]),
                   ALU.mult).then_inc(dt_ready, 1)
                c.done()

            def conv(s, n):
                c = 4 if n == 0 else n - 1
                src = bR[BANK[CONV[n]]]
                dve.wait_ge(tap_ready, at(s, 5, n))
                a = acc[:, n % 2]
                for k in (1, 2):
                    stt(a[:, k:L], src[:, 0:L - k], cw[:, c, 3 - k:4 - k], a[:, k:L], ALU.mult, ALU.add
                        ).then_inc(conv_step, 1)
                    dve.wait_ge(conv_step, at(s, 10, 2 * n + k - 1))
                stt(a[:, 3:L], src[:, 0:L - 3], cw[:, c, 0:1], a[:, 3:L], ALU.mult, ALU.add
                    ).then_inc(conv_ready, 1)

            def z_silu(s, par, n):
                dve.wait_ge(zth_ready, at(s, 4, n))
                if n == 0 and (some(s) or s >= 2):
                    dve.wait_ge(g_ready, at(s - 2, TILES, TILES - 1))
                stt(sz[:, par, n], zth[:, n % 2], 1.0, bR[BANK[ZT[n]]][:], ALU.add, ALU.mult
                    ).then_inc(sz_ready, 1)

            def tile_in(s, par, j):
                b = j % 2
                dve.wait_ge(xt_ready, at(s, TILES, j))
                if j >= 2:
                    dve.wait_ge(y_ready, at(s, TILES, j - 2))
                elif some(s) or s > 0:
                    dve.wait_ge(y_ready, at(s - 1, TILES, j + 2))
                tt(xd[:, b], bXT[:].rearrange("p (h q) -> p h q", h=H),
                   dth[:, par, j * H:(j + 1) * H].rearrange("p (h o) -> p h o", o=1).to_broadcast([P, H, HD]),
                   ALU.mult).then_inc(xd_ready, 1)
                dve.wait_ge(small_ready, at(s, TILES, j))
                if j >= 2:
                    dve.wait_ge(w_ready, at(s, TILES, j - 2))
                    dve.wait_ge(ec_ready, at(s, TILES, j - 2))
                elif some(s) or s > 0:
                    dve.wait_ge(w_ready, at(s - 1, TILES, j + 2))
                    dve.wait_ge(ec_ready, at(s - 1, TILES, j + 2))
                stt(cbm[:, b], bSM[:, 0:P], 0.25, tri[:], ALU.mult, ALU.mult)
                cp(sm[:, b], bSM[:, P:2 * P + 6]).then_inc(cb_ready, 1)

            def decays(s, j):
                b = j % 2
                dve.wait_ge(ex_ready, at(s, TILES, j))
                dve.wait_ge(ec_ready, at(s, TILES, j))
                if j < TILES - 1:
                    tt(bd[:, b], sm[:, b, 0:N].rearrange("p (o n) -> p o n", o=1).to_broadcast([P, H, N]),
                       Ex[:, b, :, P - 1:P].to_broadcast([P, H, N]), ALU.mult).then_inc(bd_ready, 1)
                if j > 0:
                    stt(cs[:, b], sm[:, b, N:2 * N].rearrange("p (o n) -> p o n", o=1).to_broadcast([P, H, N]),
                        0.25, ec[:, b, 0:H].rearrange("p (h o) -> p h o", o=1).to_broadcast([P, H, N]),
                        ALU.mult, ALU.mult).then_inc(cs_ready, 1)

            def state(s, j):
                b, nb = j % 2, (j + 1) % 2
                dve.wait_ge(ds_ready, at(s, 3, j))
                if j == 2:
                    dve.wait_ge(y_ready, at(s, TILES, 1))
                elif some(s) or s > 0:
                    dve.wait_ge(y_ready, at(s - 1, TILES, TILES - 1))
                if j == 0:
                    cp(S[:, nb], bCS[:, 2 * P:4 * P].rearrange("p (a q) -> p a q", a=2)).then_inc(s_ready, 1)
                else:
                    for a in range(2):
                        last = stt(S[:, nb, a], S[:, b, a], ec[:, b, H + a:H + a + 1],
                                   bCS[:, 2 * P + a * HD:2 * P + (a + 1) * HD], ALU.mult, ALU.add)
                    last.then_inc(s_ready, 1)
                dve.wait_ge(s_ready, at(s, 3, j))

            def tile_out(s, par, j):
                b = j % 2
                dve.wait_ge(y_ready, at(s, TILES, j))
                dve.wait_ge(xcd_ready, at(s, TILES, j))
                if j >= 2:
                    dve.wait_ge(sq_ready, at(s, TILES, j - 2))
                elif some(s) or s > 0:
                    dve.wait_ge(sq_ready, at(s - 1, TILES, j + 2))
                tt(yt[:, b], bY[:].rearrange("p (h q) -> p h q", h=H), xcd[:, b], ALU.add).then_inc(yt_ready, 1)
                dve.wait_ge(yt_ready, at(s, TILES, j))
                if j == 0 and (some(s) or s >= 2):
                    dve.wait_ge(projC_ready, at(s - 2, len(C_SLOTS), len(C_SLOTS) - 1))
                tt(g[:, par, :, j * P:(j + 1) * P], yt[:, b], sz[:, par, :, j * P:(j + 1) * P], ALU.mult
                   ).then_inc(g_ready, 1)

            def c_ready(s, name):
                dve.wait_ge(projC_ready, at(s, len(C_SLOTS), C_SLOTS.index(name)))

            def norm_out(s, c):
                c_ready(s, "ssq")
                ts(rv[:, 2], bR[BANK["ssq"]][:, 0:TILES], 1.0 / DI, RMS_EPS, ALU.mult, ALU.add
                   ).then_inc(ssq_read, 1)
                wait_read(dve, "ssq", s)
                rsqrt(c.link, rv, rvi, rv[:, 2])
                c.link(ts(rv[:, 3], rv[:, 0], 0.5, None, ALU.mult))
                dve.wait_ge(xres_loaded, 16 * (s + 1))
                if some(s) or s > 0:
                    dve.wait_ge(yo_ready, at(s - 1, 2, 1))
                for half in range(2):
                    c_ready(s, f"out{half}")
                    for q in range(2):
                        j = 2 * half + q
                        last = stt(x1[:, j], bR[BANK[f"out{half}"]][:, q * D:(q + 1) * D], rv[:, 3, j:j + 1],
                                   xres[:, j], ALU.mult, ALU.add)
                    last.then_inc(x1_ready, 1)
                wait_read(dve, "out1", s)

            def ln2(s, c):
                if some(s) or s > 0:
                    dve.wait_ge(rows_stored, 16 * s)
                layernorm(c.link, x1, xr, st6c, mvc, nwc, nwci).then_inc(x2_ready, 1)

            def route(s, c):
                link = c.link
                dve.wait_ge(lex_ready, at(s, 1))
                if some(s) or s > 0:
                    dve.wait_ge(projC_ready, at(s - 1, len(C_SLOTS), C_SLOTS.index("sel")))
                link(ts(lex[:], lex[:], 1.0, None, ALU.add))
                link(v.reciprocal(sc[:], lex[:]))
                link(tt(sbz[:], sc[:], bias_b[:].rearrange("p (o e) -> p o e", o=1).to_broadcast([P, TILES, E]),
                        ALU.add))
                pair = sbz[:].rearrange("p j (g q t) -> p (j g) q t", q=4, t=2)
                tt(hi[:], pair[:, :, :, 0], pair[:, :, :, 1], ALU.max)
                link(tt(lo[:], pair[:, :, :, 0], pair[:, :, :, 1], ALU.min))
                tt(hi2[:], hi[:, :, 0:2], hi[:, :, 2:4], ALU.max)
                tt(mn2[:], hi[:, :, 0:2], hi[:, :, 2:4], ALU.min)
                link(tt(lo2[:], lo[:, :, 0:2], lo[:, :, 2:4], ALU.max))
                link(tt(lo2[:], lo2[:], mn2[:], ALU.max))
                tt(gs3[:, 0], hi2[:, :, 0], hi2[:, :, 1], ALU.max)
                tt(gs3[:, 1], hi2[:, :, 0], hi2[:, :, 1], ALU.min)
                link(tt(gs3[:, 2], lo2[:, :, 0], lo2[:, :, 1], ALU.max))
                link(tt(gs3[:, 3], gs3[:, 1], gs3[:, 2], ALU.max))
                link(tt(gsx[:, :, 0:G], gs3[:, 0].rearrange("p (j g) -> p j g", g=G),
                        gs3[:, 3].rearrange("p (j g) -> p j g", g=G), ALU.add))
                apart(dve)
                for j in range(TILES):
                    last = v.max(m8g[:, j], gsx[:, j])
                link(last)
                link(v.memset(m8g[:, :, KG:8], -BIG))
                apart(dve)
                for j in range(TILES):
                    last = v.match_replace(grp[:, j], m8g[:, j], gsx[:, j], BIG)
                link(last)
                link(ts(gm[:], grp[:, :, 0:G], BIG, None, ALU.is_equal))
                ts(gneg[:], gm[:], 1.0, BIG, ALU.subtract, ALU.mult)
                gmb = gm[:].rearrange("p j (g o) -> p (j g) o", o=1).to_broadcast([P, TILES * G, EG])
                link(tt(tmp[:].rearrange("p j (g q) -> p (j g) q", q=EG),
                        sbz[:].rearrange("p j (g q) -> p (j g) q", q=EG), gmb, ALU.mult))
                link(tt(tmp[:].rearrange("p j (g q) -> p (j g) q", q=EG),
                        tmp[:].rearrange("p j (g q) -> p (j g) q", q=EG),
                        gneg[:].rearrange("p j (g o) -> p (j g) o", o=1).to_broadcast([P, TILES * G, EG]),
                        ALU.add))
                apart(dve)
                for j in range(TILES):
                    last = v.max(m8e[:, j], tmp[:, j])
                link(last)
                link(v.memset(m8e[:, :, K:8], -BIG))
                apart(dve)
                for j in range(TILES):
                    last = v.match_replace(rep[:, j], m8e[:, j], tmp[:, j], BIG)
                link(last)
                link(stt(sel[:].rearrange("p j (g q) -> p (j g) q", q=EG),
                         rep[:].rearrange("p j (g q) -> p (j g) q", q=EG), BIG, gmb, ALU.is_equal, ALU.mult))
                tt(tmp[:], sel[:], sc[:], ALU.mult).then_inc(sel_ready, 1)
                dve.wait_ge(sel_ready, at(s, 1))
                link(v.tensor_reduce(wsum[:], tmp[:], AX.X, ALU.add))
                link(v.reciprocal(wrec[:], wsum[:]))
                stt(xr[:, :, D:ROW], tmp[:], SCALE,
                    wrec[:].rearrange("p (j o) -> p j o", o=1).to_broadcast([P, TILES, E]),
                    ALU.mult, ALU.mult).then_inc(rw_ready, 1)

            def shared(s, c):
                c_ready(s, "gate")
                dve.wait_ge(gth_ready, at(s, 1))
                if some(s) or s > 0:
                    dve.wait_ge(hs_ready, at(s - 1, 1))
                stt(gth[:], gth[:], 1.0, bR[BANK["gate"]][0:F, :], ALU.add, ALU.mult).then_inc(gate_read, 1)
                wait_read(dve, "gate", s)
                c_ready(s, "up")
                if some(s) or s > 0:
                    c_ready(s - 1, "sel")
                tt(hs[:], gth[:], bR[BANK["up"]][0:F, :], ALU.mult).then_inc(hs_ready, 1)

            def shared_out(s):
                if some(s) or s > 0:
                    dve.wait_ge(y_stored, 16 * s)
                for half in range(2):
                    c_ready(s, f"down{half}")
                    for q in range(2):
                        j = 2 * half + q
                        last = stt(yo[:, j], bR[BANK[f"down{half}"]][:, q * D:(q + 1) * D], 0.5, x1[:, j],
                                   ALU.mult, ALU.add)
                    last.then_inc(yo_ready, 1)

            def choose(s, par):
                c_ready(s, "sel")
                if some(s) or s > 0:
                    wait_read(dve, "sel", s - 1)
                    if some(s) or s >= 2:
                        dve.wait_ge(take_step, ((s - par) // 2 if isinstance(s, int) else 0) * TAKE
                                    if isinstance(s, int) else (s - par) * (TAKE // 2))
                tt(keys[par * E:(par + 1) * E, 0], bR[BANK["sel"]][0:E, :], rank_rev[0:E, :], ALU.mult
                   ).then_inc(keys_ready, 1)

            def take(s, dst):
                wait_read(dve, "sel", s)
                apart(dve)
                u = (s - 1) // 2 if isinstance(s, int) else None
                n = [0]

                def link(ins):
                    ins.then_inc(take_step, 1)
                    n[0] += 1
                    dve.wait_ge(take_step, u * TAKE + n[0] if u is not None else (s - 1) * (TAKE // 2) + n[0])
                    apart(dve)

                for r in range(ROUNDS):
                    link(v.max(first[:, 8 * r:8 * r + 8], keys[:, r % 2]))
                    if r < ROUNDS - 1:
                        link(v.match_replace(keys[:, (r + 1) % 2], first[:, 8 * r:8 * r + 8], keys[:, r % 2], 0.0))
                link(cp(dst, first[:]))
                assert n[0] == TAKE

            dve.wait_ge(abc_exp, 1)
            ts(abc[:], abc[:], -1.0, None, ALU.mult).then_inc(abc_ready, 1)
            dve.wait_ge(w_loaded, 16 * 12)
            dve.wait_ge(abc_ready, 1)
            ts(dsk[:], dsk[:], 0.5, None, ALU.mult).then_inc(abc_ready, 1)
            dve.wait_ge(abc_ready, 2)
            dve.wait_ge(consts_ready, 1)

            def iteration(it, par, hasA, hasB, hasC, before):
                a, ap, c, cpar = it + 1, 1 - par, it - 1, 1 - par
                ch = Chain(dve, c_step, c, C_CHAIN) if hasC else None
                if hasB:
                    tile_in(it, par, 0)
                if hasA:
                    ln1(a, ap)
                if hasB:
                    decays(it, 0)
                if hasC:
                    norm_out(c, ch)
                if hasB:
                    state(it, 0)
                    tile_out(it, par, 0)
                if hasB:
                    tile_in(it, par, 1)
                    decays(it, 1)
                if hasC:
                    ln2(c, ch)
                if hasA:
                    conv(a, 0)
                    dt_stage(a, ap)
                if hasB:
                    state(it, 1)
                    tile_out(it, par, 1)
                    tile_in(it, par, 2)
                    decays(it, 2)
                if hasA:
                    conv(a, 1)
                    conv(a, 2)
                if hasA:
                    conv(a, 3)
                if hasB:
                    state(it, 2)
                    tile_out(it, par, 2)
                    tile_in(it, par, 3)
                    decays(it, 3)
                if hasC:
                    shared(c, ch)
                if hasA:
                    conv(a, 4)
                    z_silu(a, ap, 0)
                    z_silu(a, ap, 1)
                if hasC:
                    shared_out(c)
                if hasB:
                    tile_out(it, par, 3)
                if hasC:
                    route(c, ch)
                if hasA:
                    z_silu(a, ap, 2)
                    z_silu(a, ap, 3)
                if hasC:
                    choose(c, cpar)
                    ch.done()
                    if cpar == 1:
                        if isinstance(c, int):
                            take(c, lists[:, c // 2])
                        else:
                            u = dve.snap((c - 1) // 2)
                            take(c, lists[:, bass.ds(u, 1)].rearrange("p o q -> p (o q)"))

            schedule(dve, iteration)

            nm = [0]

            def link(ins):
                ins.then_inc(merge_step, 1)
                nm[0] += 1
                dve.wait_ge(merge_step, nm[0])

            for u in range(NSEQ // 2):
                for par in range(2):
                    last = v.memset(base[par * E:(par + 1) * E, u:u + 1], float(T - L * (2 * u + par + 1)))
            link(last)
            link(v.memset(tokT[:], float(T)))
            link(stt(gk[:], lists[:], 0.0, base[:].rearrange("p (u o) -> p u o", o=1).to_broadcast([P, NSEQ // 2, CAP]),
                     ALU.is_gt, ALU.mult))
            link(tt(gk[:], gk[:], lists[:], ALU.add))
            for par in range(2):
                last = cp(cat[:, 0, par * 4 * CAP:(par + 1) * 4 * CAP], gk[par * E:(par + 1) * E].rearrange("p u q -> p (u q)"))
            link(last)
            for r in range(ROUNDS):
                link(v.max(kfirst[:, 8 * r:8 * r + 8], cat[:, r % 2]))
                if r < ROUNDS - 1:
                    link(v.match_replace(cat[:, (r + 1) % 2], kfirst[:, 8 * r:8 * r + 8], cat[:, r % 2], 0.0))
            ts(ktok[:], kfirst[:], -1.0, float(T), ALU.mult, ALU.add).then_inc(ktok_ready, 1)
            dve.wait_ge(tokt_ready, 1)
            for e in range(2):
                last = cp(tokT[e * 64:e * 64 + CAP], bTR[0:CAP, e:E:2])
            link(last)
            cp(idxT[:], tokT[:]).then_inc(idx_ready, 1)

            def same_token(i, n, start):
                b = n % 2
                if some(i) or i >= WRING:
                    dve.wait_ge(rowb_ready, i - WRING + 1)
                cp(tokc[:, n], tokT[:, bass.ds(i, 1)]).then_inc(tokc_ready, 1)
                dve.wait_ge(tokc_ready, i + 1)
                dve.wait_ge(rowb_ready, i + 1)
                if some(i) or i >= 2:
                    dve.wait_ge(sum_ready, i - 1)
                ts(eq[:, b], bSM[:, 0:P], tokc[:, n], None, ALU.is_equal).then_inc(eq_ready, 1)
                dve.wait_ge(eq_ready, i + 1)
                if some(i) or i >= WRING:
                    dve.wait_ge(scattered, 16 * (i - WRING + 1))
                e_link(i, 0, v.tensor_tensor_reduce(out=eqs[:, b], in0=eq[:, b], in1=strict[:], scale=1.0, scalar=0.0,
                                                    op0=ALU.mult, op1=ALU.add, accum_out=cnt[:, b]))
                e_link(i, 1, tt(sidx[:, b, 0:1], tokc[:, n], spare[:], ALU.subtract))
                e_link(i, 2, stt(sidx[:, b, 1:2], cnt[:, b], 0.0, sidx[:, b, 0:1], ALU.is_equal, ALU.mult))
                tt(sidxi[:, n], sidx[:, b, 1:2], spare[:], ALU.add).then_inc(sidx_ready, 1)

            def e_link(i, n, ins):
                ins.then_inc(e_step, 1)
                dve.wait_ge(e_step, i * 5 + n + 1)

            def expert_tile(i, n):
                b = n % 2
                same_token(i, n, 0)
                dve.wait_ge(gathered[n], 16 * (i // WRING + 1) if isinstance(i, int) else (i - n) * 4 + 16)
                for e in range(2):
                    r = slice(e * 64, (e + 1) * 64)
                    off = D + 2 * i + e if isinstance(i, int) else dve.snap(2 * i + (D + e))
                    last = ts(wcol[r, b], xg[r, n, bass.ds(off, 1)], 0.5, None, ALU.mult)
                e_link(i, 3, last)
                dve.wait_ge(eth_ready, i + 1)
                e_link(i, 4, stt(ehg[:, b], eth[:, b], 1.0, bSEG[0:F, 0:P], ALU.add, ALU.mult))
                if some(i) or i >= 2:
                    dve.wait_ge(down_ready, i - 1)
                tt(ehs[:, b], ehg[:, b], bSEG[0:F, P:2 * P], ALU.mult).then_inc(ehs_ready, 1)
                dve.wait_ge(down_ready, i + 1)
                if some(i) or i >= 2:
                    dve.wait_ge(sum_ready, i - 1)
                ts(ow[:, b], bY[:, 0:D], wcol[:, b], None, ALU.mult).then_inc(ow_ready, 1)

            for n in range(WRING):
                expert_tile(n, n)
            with dve.Fori(1, ET // WRING) as lot:
                for n in range(WRING):
                    expert_tile(WRING * lot + n, n)


LN_CHAIN = 17
DT_CHAIN = 16
TAKE = 2 * ROUNDS
C_CHAIN = 15 + LN_CHAIN + 21

def kernel(**inputs):
    import numpy as _np
    import concourse.bacc as _bacc
    from concourse import mybir as _mybir
    from concourse.bass_utils import run_bass_kernel_spmd as _run

    a = {k: _np.asarray(v) for k, v in inputs.items()}

    def spread(v):
        return _np.broadcast_to(v[None, :], (P, v.shape[0]))

    parts = {
        "x": a["L0_attn_x"].reshape(T, D),
        "w_in": a["L0_attn_W_in"].T.reshape(KD, P, PROJ + H).transpose(1, 0, 2),
        "conv_w": a["L0_attn_conv_w"].reshape(5, P, 4).transpose(1, 0, 2),
        "conv_b": a["L0_attn_conv_b"].reshape(5, P).T,
        "a_log": spread(a["L0_attn_A_log"]),
        "dt_bias": spread(a["L0_attn_dt_bias"]),
        "dskip": spread(a["L0_attn_D"]),
        "w_out": a["L0_attn_W_out"].T.reshape(H, P, D).transpose(1, 0, 2),
        "gate_w": a["L0_ffn_gate_w"].reshape(P, KD, E),
        "bias": spread(a["L0_ffn_bias"]),
        "w_gate": a["L0_ffn_w_gate"].reshape(ET, 2, P, KD, F).transpose(0, 2, 1, 3, 4),
        "w_up": a["L0_ffn_w_up"].reshape(ET, 2, P, KD, F).transpose(0, 2, 1, 3, 4),
        "w_down": a["L0_ffn_w_down"].reshape(ET, 2, F, D).transpose(0, 2, 1, 3),
        "ws_gate": a["L0_ffn_ws_gate"].reshape(P, KD, F),
        "ws_up": a["L0_ffn_ws_up"].reshape(P, KD, F),
        "ws_down": a["L0_ffn_ws_down"],
    }
    nc = _bacc.Bacc("TRN2", target_bir_lowering=False, num_devices=1)
    arrays, args = {}, {}
    for name, v in parts.items():
        v = _np.ascontiguousarray(v)
        arrays[f"in_{name}"] = v
        args[name] = nc.dram_tensor(f"in_{name}", v.shape, _mybir.dt.from_np(v.dtype), kind="ExternalInput").ap()
    rows = nc.dram_tensor("rows", (T + P, ROW), _mybir.dt.float32, kind="Internal").ap()
    out = nc.dram_tensor("out_y", (T + P, D), _mybir.dt.float32, kind="ExternalOutput").ap()
    build(nc, **args, rows=rows, out=out)
    r = _run(nc, [arrays], core_ids=[0])
    return r.results[0]["out_y"][:T].reshape(NSEQ, L, D)
```

```python
from contextlib import ExitStack

import concourse.bass as bass
from concourse import mybir

F32 = mybir.dt.float32
I32 = mybir.dt.int32
U32 = mybir.dt.uint32
ALU = mybir.AluOpType
ACT = mybir.ActivationFunctionType
AX = mybir.AxisListType

P = 128
NSEQ, L, D = 8, 512, 256
T = NSEQ * L
TILES = L // P
KD = D // P
H, HD = 4, 128
DI = H * HD
N = 64
PROJ = 2 * DI + 2 * N
E, K, F = 64, 6, 96
G, KG = 8, 4
EG = E // G
CAP = 2 * (256 * K // E)
SCALE = 2.5
ROW = D + E
LN_EPS, RMS_EPS = 1e-5, 1.1920929e-07
BIG = 3.0e38
ET = E // 2
WRING = 4
ROUNDS = CAP // 8

SLOTS = [("ssq", "C"), ("out0", "C"), ("out1", "C"), ("m8", "A"), ("dt", "A"), ("m4", "A"),
         ("router", "C"), ("m5", "A"), ("m6", "A"), ("gate", "C"), ("up", "C"), ("m7", "A"),
         ("m0", "A"), ("m1", "A"), ("down0", "C"), ("down1", "C"), ("m2", "A"), ("m3", "A"),
         ("sel", "C")]
BANK = {name: n % 2 for n, (name, _) in enumerate(SLOTS)}
A_SLOTS = [n for n, st in SLOTS if st == "A"]
C_SLOTS = [n for n, st in SLOTS if st == "C"]
CONV = ["m8", "m4", "m5", "m6", "m7"]
ZT = ["m0", "m1", "m2", "m3"]


def at(seq, per, n=0):
    return seq * per + (n + 1)


class Chain:

    def __init__(self, eng, sem, seq, per):
        self.eng, self.sem, self.seq, self.per, self.n = eng, sem, seq, per, 0

    def link(self, ins):
        ins.then_inc(self.sem, 1)
        self.n += 1
        self.eng.wait_ge(self.sem, at(self.seq, self.per, self.n - 1))

    def done(self):
        assert self.n == self.per, (str(self.sem), self.n, self.per)


def build(nc, x, w_in, conv_w, conv_b, a_log, dt_bias, dskip, w_out, gate_w, bias,
          w_gate, w_up, w_down, ws_gate, ws_up, ws_down, rows, out):
    x_t = x.rearrange("(s j p) d -> s p j d", j=TILES, p=P)
    rows_t = rows[0:T, :].rearrange("(s j p) d -> s p j d", j=TILES, p=P)
    out_t = out[0:T, :].rearrange("(s j p) d -> s p j d", j=TILES, p=P)

    with ExitStack() as ctx:
        def sb(name, shape, dt=F32):
            return ctx.enter_context(nc.sbuf_tensor(name, shape, dt))

        def sem(name):
            return ctx.enter_context(nc.semaphore(name))

        def bank(name):
            return ctx.enter_context(nc.psum_tensor(name, [P, 512], F32))

        win = sb("win", [P, KD, PROJ + H])
        wout = sb("wout", [P, H, D])
        gw = sb("gw", [P, KD, E])
        wsg = sb("wsg", [P, KD, F])
        wsu = sb("wsu", [P, KD, F])
        wsd = sb("wsd", [F, D])
        cw = sb("cw", [P, 5, 4])
        cb = sb("cb", [P, 5])
        abc = sb("abc", [P, H])
        dtb = sb("dtb", [P, H])
        dsk = sb("dsk", [P, H])
        dskip_diag = sb("dskip_diag", [P, H, P])
        bias_b = sb("bias_b", [P, E])
        ident = sb("ident", [P, P])
        tri = sb("tri", [P, P])
        strict = sb("strict", [P, P])
        ones = sb("ones", [P, P])
        rank_rev = sb("rank_rev", [P, L])
        spare_i = sb("spare_i", [P, 1], I32)
        spare = sb("spare", [P, 1])
        zrow = sb("zrow", [P, ROW])
        xin = sb("xin", [P, 2, TILES, D])
        st6 = sb("st6", [P, TILES, 6])
        mv = sb("mv", [P, TILES, 2])
        exponent = sb("exponent", [P, TILES])
        ve = sb("ve", [P, TILES])
        nw = sb("nw", [P, TILES])
        xn = sb("xn", [P, TILES, D])
        xnT = sb("xnT", [P, KD, L])
        acc = sb("acc", [P, 2, L])
        rank_i = acc[:, 0].bitcast(I32)
        cth = sb("cth", [P, 2, L])
        zth = sb("zth", [P, 2, L])
        xc = sb("xc", [P, 2, 5, L])
        ct0 = sb("ct0", [N, 2, L])
        sz = sb("sz", [P, 2, H, L])
        dtv = sb("dtv", [P, 8, TILES * H])
        dth = sb("dth", [P, 2, TILES * H])
        dA = sb("dA", [P, 2, TILES * H])
        datri = sb("datri", [P, 2, H, P])
        xd = sb("xd", [P, 2, H, HD])
        Ex = sb("Ex", [P, 2, H, P])
        cbm = sb("cbm", [P, 2, P])
        sm = sb("sm", [P, 2, P + 6])
        ec = sb("ec", [P, 2, 6])
        Wt = sb("Wt", [P, 2, H, P])
        bd = sb("bd", [P, 2, H, N])
        cs = sb("cs", [P, 2, H, N])
        csT = sb("csT", [P, 2, H, P])
        S = sb("S", [P, 2, 2, HD])
        sq = sb("sq", [P, 2, H, P])
        sqh = sq[:, :, 0:2]
        g = sb("g", [P, 2, H, L])
        ss = sb("ss", [P, 2, L])
        xres = sb("xres", [P, TILES, D])
        ms = sb("ms", [P, TILES])
        rms = sb("rms", [P, TILES])
        x1 = sb("x1", [P, TILES, D])
        st6c = sb("st6c", [P, TILES, 6])
        mvc = sb("mvc", [P, TILES, 2])
        vec = sb("vec", [P, TILES])
        nwc = sb("nwc", [P, TILES])
        xr = sb("xr", [P, TILES, ROW])
        x2T = sb("x2T", [P, KD, L])
        lex = sb("lex", [P, TILES, E])
        sc = sb("sc", [P, TILES, E])
        sbz = sb("sbz", [P, TILES, E])
        hi = sb("hi", [P, TILES * G, 4])
        lo = sb("lo", [P, TILES * G, 4])
        hi2 = sb("hi2", [P, TILES * G, 2])
        lo2 = sb("lo2", [P, TILES * G, 2])
        mn2 = sb("mn2", [P, TILES * G, 2])
        gsx = sb("gsx", [P, TILES, G + 4])
        gs3 = sb("gs3", [P, 4, TILES * G])
        m8g = sb("m8g", [P, TILES, 8])
        grp = sb("grp", [P, TILES, G + 4])
        gm = sb("gm", [P, TILES, G])
        gneg = sb("gneg", [P, TILES, G])
        tmp = sb("tmp", [P, TILES, E])
        m8e = sb("m8e", [P, TILES, 8])
        rep = lex
        sel = sb("sel", [P, TILES, E])
        wsum = sb("wsum", [P, TILES])
        wrec = sb("wrec", [P, TILES])
        gth = sb("gth", [F, L])
        hs = sb("hs", [F, L])
        yo = sb("yo", [P, TILES, D])
        keys = sb("keys", [P, 2, L])
        first = sb("first", [P, CAP])
        lists = sb("lists", [P, 1 + NSEQ // 2, CAP])
        kfirst = sb("kfirst", [E, CAP])
        ktok = sb("ktok", [E, CAP])
        tokT = sb("tokT", [P, ET])
        idxT = sb("idxT", [P, ET], I32)
        idxc = sb("idxc", [P, WRING, 1], I32)
        tokc = sb("tokc", [P, 2, 1])
        wgr = sb("wgr", [P, WRING, 2, KD, F])
        wur = sb("wur", [P, WRING, 2, KD, F])
        wdr = sb("wdr", [F, WRING, 2, D])
        wcol = sb("wcol", [P, 2, 1])
        cnt = sb("cnt", [P, 2, 1])
        sidx = sb("sidx", [P, 2, 2])
        sidxi = sb("sidxi", [P, WRING, 1], I32)
        flat, used = {"g": g[:].rearrange("p a h l -> p (a h l)"), "sz": sz[:].rearrange("p a h l -> p (a h l)")}, {"g": 0, "sz": 0}

        def part(n, of="g", rows_=P):
            used[of] += n
            return flat[of][0:rows_, used[of] - n:used[of]]

        xg = part(WRING * ROW).rearrange("p (n d) -> p n d", n=WRING)
        xgT = part(2 * D).rearrange("p (n k q) -> p n k q", n=2, k=KD)
        ow = part(2 * D).rearrange("p (n d) -> p n d", n=2)
        oc = part(2 * D).rearrange("p (n d) -> p n d", n=2)
        eq = part(2 * P).rearrange("p (n q) -> p n q", n=2)
        eqs = part(2 * P).rearrange("p (n q) -> p n q", n=2)
        base = part(NSEQ // 2, "sz")
        gk = part(NSEQ // 2 * CAP, "sz").rearrange("p (u q) -> p u q", q=CAP)
        cat = part(2 * NSEQ * CAP, "sz", E).rearrange("p (n q) -> p n q", n=2)
        eth, ehg, ehs = (part(2 * P, "sz", F).rearrange("p (n q) -> p n q", n=2) for _ in range(3))

        bTR = bank("bTR")
        bR = [bank("bR0"), bank("bR1")]
        bXT = bank("bXT")
        bSEG = bank("bSEG")
        bSM = bank("bSM")
        bCS = bank("bCS")
        bY = bank("bY")
        bGU = [bSEG, bTR]

        sems = {}

        def S_(name):
            if name not in sems:
                sems[name] = sem(name)
            return sems[name]

        w_loaded = S_("w_loaded")
        consts_ready = S_("consts_ready")
        pool_const = S_("pool_const")
        abc_exp = S_("abc_exp")
        abc_ready = S_("abc_ready")
        x_loaded = [S_("x_loaded0"), S_("x_loaded1")]
        xres_loaded = S_("xres_loaded")
        ct_moved = S_("ct_moved")
        rows_stored = S_("rows_stored")
        y_stored = S_("y_stored")
        pad_stored = S_("pad_stored")
        xn_ready = S_("xn_ready")
        ln1_sums, ln1_var, ln1_root = S_("ln1_sums"), S_("ln1_var"), S_("ln1_root")
        ln2_sums, ln2_var, ln2_root = S_("ln2_sums"), S_("ln2_var"), S_("ln2_root")
        ln1_mean, ln2_mean, rms_root = S_("ln1_mean"), S_("ln2_mean"), S_("rms_root")
        trA_ready, trA_copied = S_("trA_ready"), S_("trA_copied")
        trC_ready, trC_copied = S_("trC_ready"), S_("trC_copied")
        projA_ready, projC_ready = S_("projA_ready"), S_("projC_ready")
        dt_read, ssq_read, gate_read, keys_ready = S_("dt_read"), S_("ssq_read"), S_("gate_read"), S_("keys_ready")
        tap_ready, conv_step, conv_ready, cth_ready, xc_ready = (
            S_("tap_ready"), S_("conv_step"), S_("conv_ready"), S_("cth_ready"), S_("xc_ready"))
        cth_step = S_("cth_step")
        zth_ready, sz_ready = S_("zth_ready"), S_("sz_ready")
        dt_step, dtabs_ready, dte_ready, dt_ready = (
            S_("dt_step"), S_("dtabs_ready"), S_("dte_ready"), S_("dt_ready"))
        datri_ready, seg_ready, ex_ready = S_("datri_ready"), S_("seg_ready"), S_("ex_ready")
        xt_ready, xd_ready = S_("xt_ready"), S_("xd_ready")
        small_ready, cb_ready, ec_ready = S_("small_ready"), S_("cb_ready"), S_("ec_ready")
        w_ready, bd_ready, cs_ready = S_("w_ready"), S_("bd_ready"), S_("cs_ready")
        cst_ready, cst_copied = S_("cst_ready"), S_("cst_copied")
        ds_ready, s_ready = S_("ds_ready"), S_("s_ready")
        y_ready, skip_made = S_("y_ready"), S_("skip_made")
        g_ready, sq_ready, sqh_step, ss_ready = S_("g_ready"), S_("sq_ready"), S_("sqh_step"), S_("ss_ready")
        c_step, x1_ready, x2_ready, lex_ready = S_("c_step"), S_("x1_ready"), S_("x2_ready"), S_("lex_ready")
        sel_ready, rw_ready = S_("sel_ready"), S_("rw_ready")
        gth_ready, hs_ready, yo_ready = S_("gth_ready"), S_("hs_ready"), S_("yo_ready")
        take_step = S_("take_step")
        merge_step, ktok_ready, tokt_ready, idx_ready = (
            S_("merge_step"), S_("ktok_ready"), S_("tokt_ready"), S_("idx_ready"))
        wx_loaded = [S_(f"wx_loaded{n}") for n in range(WRING)]
        idxc_ready, gathered = S_("idxc_ready"), [S_(f"gathered{n}") for n in range(WRING)]
        scattered = S_("scattered")
        xgt_ready, xgt_copied = S_("xgt_ready"), S_("xgt_copied")
        gu_ready, eth_ready, ehg_ready, ehs_ready = S_("gu_ready"), S_("eth_ready"), S_("ehg_ready"), S_("ehs_ready")
        token_step, wcol_ready = S_("token_step"), S_("wcol_ready")
        down_ready, ow_ready = S_("down_ready"), S_("ow_ready")
        tokc_ready, rowb_ready, eq_ready, sidx_ready = (
            S_("tokc_ready"), S_("rowb_ready"), S_("eq_ready"), S_("sidx_ready"))
        sum_ready, oc_ready = S_("sum_ready"), S_("oc_ready")

        credited = [keys_ready, trC_copied, sel_ready, hs_ready, projC_ready, yo_ready, x1_ready,
                    rows_stored, y_stored, take_step]

        waits_passed = S_("waits_passed")

        def apart(eng):
            eng.sem_inc(waits_passed, 1)

        def wait_read(eng, name, seq):
            if name in CONV:
                eng.wait_ge(conv_ready, at(seq, len(CONV), CONV.index(name)))
            elif name in ZT:
                eng.wait_ge(sz_ready, at(seq, len(ZT), ZT.index(name)))
            elif name in ("out0", "out1"):
                eng.wait_ge(x1_ready, 1 + at(seq, 2, int(name[3])))
            elif name in ("down0", "down1"):
                eng.wait_ge(yo_ready, 1 + at(seq, 2, int(name[4])))
            else:
                reader = {"dt": dt_read, "ssq": ssq_read, "router": lex_ready, "gate": gate_read,
                          "up": hs_ready, "sel": keys_ready}[name]
                eng.wait_ge(reader, at(seq, 1) + (reader in credited))

        def slot_wait(pe, name, seq, hasA, hasC, before):
            order = [n for n, st in SLOTS if (st == "A" and hasA) or (st == "C" and hasC)]
            it = seq - 1 if name in A_SLOTS else seq + 1
            last = [n for n in order[:order.index(name)] if BANK[n] == BANK[name]][-1:]
            if not last:
                if before is None:
                    return
                it = it - 1
                stages = [[n for n, st in SLOTS if BANK[n] == BANK[name] and st == "AC"[c] and before[c]]
                          for c in range(2)]
                order = [n for n, _ in SLOTS]
                last = sorted((x[-1] for x in stages if x), key=order.index)
                if before[1] != "maybe" or last[-1] in A_SLOTS:
                    last = last[-1:]
            for n in last:
                wait_read(pe, n, it + 1 if n in A_SLOTS else it - 1)

        def schedule(eng, iteration):
            iteration(-1, 1, True, False, False, None)
            iteration(0, 0, True, True, False, (True, False))
            with eng.Fori(0, (NSEQ - 2) // 2) as pair:
                iteration(2 * pair + 1, 1, True, True, True, None)
                iteration(2 * pair + 2, 0, True, True, True, None)
            iteration(NSEQ - 1, 1, False, True, True, (True, True))
            iteration(NSEQ, 0, False, False, True, (False, True))

        def expert_schedule(eng, step):
            for i in range(WRING):
                step(i, i)
            with eng.Fori(1, ET // WRING - 1) as lot:
                for n in range(WRING):
                    step(WRING * lot + n, n)
            for i in range(ET - WRING, ET + 2):
                step(i, i % WRING)

        block = ctx.enter_context(nc.Block())

        @block.sync
        def _(sp):
            for semaphore in credited:
                sp.sem_inc(semaphore, 1)

            def load_x(s, par, reuse):
                src = x_t[s] if isinstance(s, int) else x_t[bass.ds(s, 1)].rearrange("s p j d -> p (s j) d")
                if reuse:
                    sp.wait_ge(xn_ready, at(s - 2, 1))
                sp.dma_start(xin[:, par], src).then_inc(x_loaded[par], 16)

            load_x(0, 0, False)
            for dst, src in ((win, w_in), (cw, conv_w), (cb, conv_b), (dtb, dt_bias), (abc, a_log),
                             (dsk, dskip), (wout, w_out), (gw, gate_w), (wsg, ws_gate), (wsu, ws_up),
                             (wsd, ws_down), (bias_b, bias)):
                sp.dma_start(dst[:], src).then_inc(w_loaded, 16)
            load_x(1, 1, False)
            sp.wait_ge(consts_ready, 1)
            sp.dma_start(rows[T:T + P, :], zrow[:]).then_inc(pad_stored, 16)
            sp.dma_start(out[T:T + P, :], zrow[:, 0:D]).then_inc(pad_stored, 16)

            def expert_weights(i, slot, reuse):
                if reuse:
                    sp.wait_ge(down_ready, i - WRING + 1)
                    idx = sp.snap(i)
                    g_src = w_gate[bass.ds(idx, 1)].rearrange("i p e k f -> p (i e) k f")
                    u_src = w_up[bass.ds(idx, 1)].rearrange("i p e k f -> p (i e) k f")
                    d_src = w_down[bass.ds(idx, 1)].rearrange("i f e d -> f (i e) d")
                else:
                    g_src, u_src, d_src = w_gate[i], w_up[i], w_down[i]
                sp.dma_start(wgr[:, slot], g_src).then_inc(wx_loaded[slot], 16)
                sp.dma_start(wur[:, slot], u_src).then_inc(wx_loaded[slot], 16)
                sp.dma_start(wdr[:, slot], d_src).then_inc(wx_loaded[slot], 16)

            for i in range(WRING):
                expert_weights(i, i, False)

            def move_c(s, par):
                sp.wait_ge(xc_ready, at(s, len(CONV), 0))
                if not isinstance(s, int) or s >= 2:
                    sp.wait_ge(small_ready, at(s - 2, TILES, TILES - 1))
                sp.dma_start(ct0[:, par], xc[N:2 * N, par, 4, :]).then_inc(ct_moved, 16)

            def load_residual(s):
                if not isinstance(s, int) or s >= 1:
                    sp.wait_ge(x1_ready, 1 + at(s - 1, 2, 1))
                src = x_t[s] if isinstance(s, int) else x_t[bass.ds(s, 1)].rearrange("s p j d -> p (s j) d")
                sp.dma_start(xres[:], src).then_inc(xres_loaded, 16)

            def store_c(s):
                if isinstance(s, int):
                    r_dst, y_dst = rows_t[s], out_t[s]
                else:
                    r_dst = rows_t[bass.ds(s, 1)].rearrange("s p j d -> p (s j) d")
                    y_dst = out_t[bass.ds(s, 1)].rearrange("s p j d -> p (s j) d")
                sp.wait_ge(rw_ready, at(s, 1))
                sp.dma_start(r_dst, xr[:]).then_inc(rows_stored, 16)
                sp.wait_ge(yo_ready, 1 + at(s, 2, 1))
                sp.dma_start(y_dst, yo[:]).then_inc(y_stored, 16)

            def iteration(it, par, hasA, hasB, hasC, before, more):
                if hasC:
                    load_residual(it - 1)
                if hasA:
                    move_c(it + 1, 1 - par)
                if more:
                    load_x(it + 2, par, True)
                if hasC:
                    store_c(it - 1)

            iteration(-1, 1, True, False, False, None, False)
            iteration(0, 0, True, True, False, None, True)
            with sp.Fori(0, (NSEQ - 4) // 2) as pair:
                iteration(2 * pair + 1, 1, True, True, True, None, True)
                iteration(2 * pair + 2, 0, True, True, True, None, True)
            iteration(NSEQ - 3, 1, True, True, True, None, True)
            iteration(NSEQ - 2, 0, True, True, True, None, False)
            iteration(NSEQ - 1, 1, False, True, True, None, False)
            iteration(NSEQ, 0, False, False, True, None, False)
            with sp.Fori(1, ET // WRING) as lot:
                for n in range(WRING):
                    expert_weights(WRING * lot + n, n, True)
            sp.wait_ge(scattered, 16 * ET)
            sp.wait_ge(rows_stored, 1 + 16 * NSEQ)
            sp.wait_ge(y_stored, 1 + 16 * NSEQ)
            sp.wait_ge(pad_stored, 32)

        @block.tensor
        def _(pe):
            mm, tr = nc.tensor.matmul, nc.tensor.transpose

            def front(s, par, j):
                b = j % 2
                tile = slice(j * P, (j + 1) * P)
                if j == 0:
                    pe.wait_ge(xc_ready, at(s, len(CONV), len(CONV) - 1))
                    pe.wait_ge(dt_ready, at(s, 1))
                    pe.wait_ge(ct_moved, 16 * (s + 1))
                    if not isinstance(s, int) or s > 0:
                        pe.wait_ge(xd_ready, at(s - 1, TILES, TILES - 1))
                        pe.wait_ge(ex_ready, at(s - 1, TILES, TILES - 1))
                        pe.wait_ge(cb_ready, at(s - 1, TILES, TILES - 1))
                else:
                    pe.wait_ge(xd_ready, at(s, TILES, j - 1))
                    pe.wait_ge(ex_ready, at(s, TILES, j - 1))
                    pe.wait_ge(cb_ready, at(s, TILES, j - 1))
                for h in range(H):
                    last = tr(bXT[:, h * HD:(h + 1) * HD], xc[:, par, h, tile], ident[:])
                last.then_inc(xt_ready, 1)
                pe.wait_ge(datri_ready, at(s, TILES, j))
                mm(bSEG[:], strict[:], datri[:, b].rearrange("p h q -> p (h q)"),
                   start=True, stop=True).then_inc(seg_ready, 1)
                mm(bSM[:, 0:P], xc[0:N, par, 4, tile], ct0[:, par, tile], start=True, stop=True)
                tr(bSM[:, P:2 * P], xc[:, par, 4, tile], ident[:])
                dcol = dA[:, par, j * H:(j + 1) * H]
                last = mm(bSM[:, 2 * P:2 * P + H], tri[:], dcol, start=True, stop=True)
                for hl in range(2):
                    last = mm(bSM[hl * N:(hl + 1) * N, 2 * P + H:2 * P + H + 2], ones[:, 0:N],
                              dcol.rearrange("p (a b) -> p a b", b=2)[:, :, hl], start=True, stop=True)
                last.then_inc(small_ready, 1)

            def turn_c(s, j):
                pe.wait_ge(cs_ready, at(s, TILES - 1, j - 1))
                pe.wait_ge(s_ready, at(s, TILES - 1, j - 1))
                c2 = cs[:, j % 2].rearrange("p (a h) n -> p a (h n)", a=2)
                for a in range(2):
                    last = tr(bCS[:, a * P:(a + 1) * P], c2[:, a], ident[:])
                last.then_inc(cst_ready, 1)

            def back(s, par, j):
                b = j % 2
                pe.wait_ge(xd_ready, at(s, TILES, j))
                if j < TILES - 1:
                    pe.wait_ge(bd_ready, at(s, TILES - 1, j))
                    if j == 0:
                        if not isinstance(s, int) or s > 0:
                            pe.wait_ge(cst_copied, at(s - 1, TILES - 1, TILES - 2))
                    else:
                        pe.wait_ge(cst_copied, at(s, TILES - 1, j - 1))
                    for h in range(H):
                        a, hl = divmod(h, 2)
                        last = mm(bCS[hl * N:(hl + 1) * N, 2 * P + a * HD:2 * P + (a + 1) * HD], bd[:, b, h],
                                  xd[:, b, h], start=True, stop=True)
                    last.then_inc(ds_ready, 1)
                if j > 0:
                    pe.wait_ge(g_ready, at(s, TILES, j - 1))
                elif not isinstance(s, int) or s > 0:
                    pe.wait_ge(g_ready, at(s - 1, TILES, TILES - 1))
                tile = slice(j * P, (j + 1) * P)
                pe.wait_ge(w_ready, at(s, TILES, j))
                if j > 0:
                    pe.wait_ge(cst_copied, at(s, TILES - 1, j - 1))
                for h in range(H):
                    a, hl = divmod(h, 2)
                    mm(bY[:, h * P:(h + 1) * P], dskip_diag[:, h], xc[:, par, h, tile], start=True, stop=False)
                    last = mm(bY[:, h * P:(h + 1) * P], xd[:, b, h], Wt[:, b, h], start=False, stop=(j == 0))
                    if j > 0:
                        last = mm(bY[:, h * P:(h + 1) * P], S[:, b, a], csT[:, b, h], start=False, stop=True)
                last.then_inc(y_ready, 1)

            def turn_in(s, k, prev):
                if k == 0:
                    pe.wait_ge(xn_ready, at(s, 1))
                    for read in prev:
                        pe.wait_ge(*read)
                else:
                    pe.wait_ge(trA_copied, at(s, KD, k - 1))
                for j in range(TILES):
                    last = tr(bTR[:, j * P:(j + 1) * P], xn[:, j, k * P:(k + 1) * P], ident[:])
                last.then_inc(trA_ready, 1)

            def turn_mid(s, k, prev):
                if k == 0:
                    pe.wait_ge(x2_ready, at(s, 1))
                    pe.wait_ge(*prev)
                else:
                    pe.wait_ge(trC_copied, 1 + at(s, KD, k - 1))
                for j in range(TILES):
                    last = tr(bTR[:, j * P:(j + 1) * P], xr[:, j, k:D:KD], ident[:])
                last.then_inc(trC_ready, 1)

            def project(s, name):
                dst = bR[BANK[name]]
                if name == "m8":
                    pe.wait_ge(trA_copied, at(s, KD, KD - 1))
                if name == "dt":
                    for j in range(TILES):
                        for k in range(KD):
                            last = mm(dst[:, j * H:(j + 1) * H], xnT[:, k, j * P:(j + 1) * P],
                                      win[:, k, PROJ:PROJ + H], start=(k == 0), stop=(k == KD - 1))
                else:
                    m = int(name[1])
                    for k in range(KD):
                        last = mm(dst[:], win[:, k, m * P:(m + 1) * P], xnT[:, k, :],
                                  start=(k == 0), stop=(k == KD - 1))
                last.then_inc(projA_ready, 1)

            def finish(s, par, name):
                dst = bR[BANK[name]]
                if name == "ssq":
                    pe.wait_ge(ss_ready, at(s, TILES, TILES - 1))
                    for j in range(TILES):
                        last = mm(dst[:, j:j + 1], ss[:, par, j * P:(j + 1) * P], ones[:, 0:1], start=True, stop=True)
                elif name in ("out0", "out1"):
                    pe.wait_ge(g_ready, at(s, TILES, TILES - 1))
                    for half in range(2):
                        j = 2 * int(name[3]) + half
                        for h in range(H):
                            last = mm(dst[:, half * D:(half + 1) * D], g[:, par, h, j * P:(j + 1) * P],
                                      wout[:, h], start=(h == 0), stop=(h == H - 1))
                elif name == "router":
                    pe.wait_ge(trC_copied, 1 + at(s, KD, KD - 1))
                    for j in range(TILES):
                        for k in range(KD):
                            last = mm(dst[:, j * E:(j + 1) * E], x2T[:, k, j * P:(j + 1) * P], gw[:, k],
                                      start=(k == 0), stop=(k == KD - 1))
                elif name in ("gate", "up"):
                    w = wsg if name == "gate" else wsu
                    for k in range(KD):
                        last = mm(dst[0:F, :], w[:, k], x2T[:, k], start=(k == 0), stop=(k == KD - 1))
                elif name in ("down0", "down1"):
                    pe.wait_ge(hs_ready, 1 + at(s, 1))
                    for half in range(2):
                        j = 2 * int(name[4]) + half
                        last = mm(dst[:, half * D:(half + 1) * D], hs[:, j * P:(j + 1) * P], wsd[:],
                                  start=True, stop=True)
                else:
                    pe.wait_ge(sel_ready, 1 + at(s, 1))
                    apart(pe)
                    for j in range(TILES):
                        last = tr(dst[0:E, j * P:(j + 1) * P], sel[:, j], ident[:])
                last.then_inc(projC_ready, 1)

            pe.wait_ge(consts_ready, 1)
            pe.wait_ge(skip_made, 1)
            pe.wait_ge(w_loaded, 16 * 12)

            def iteration(it, par, hasA, hasB, hasC, before):
                in_loop = before is None and not isinstance(it, int)
                prior = (True, True) if in_loop else before
                if in_loop and par == 1:
                    prior = (True, "maybe")

                def fill(*names):
                    for name in names:
                        if name == "LN1":
                            if hasA:
                                prev = []
                                if not isinstance(it, int) or it == 0:
                                    prev.append((trA_copied, at(it, KD, KD - 1)))
                                if not isinstance(it, int):
                                    prev.append((trC_copied, 1 + at(it - 2, KD, KD - 1)))
                                turn_in(it + 1, 0, prev)
                                turn_in(it + 1, 1, [])
                        elif name == "LN2a":
                            if hasC:
                                turn_mid(it - 1, 0, (trA_copied, at(it + 1, KD, KD - 1)) if hasA else
                                         (trC_copied, 1 + at(it - 2, KD, KD - 1)))
                        elif name == "LN2b":
                            if hasC:
                                turn_mid(it - 1, 1, None)
                        elif name in A_SLOTS:
                            if hasA:
                                slot_wait(pe, name, it + 1, hasA, hasC, prior)
                                project(it + 1, name)
                        elif hasC:
                            slot_wait(pe, name, it - 1, hasA, hasC, prior)
                            finish(it - 1, 1 - par, name)

                if hasB:
                    front(it, par, 0)
                fill("ssq", "out0", "out1", "LN1")
                if hasB:
                    back(it, par, 0)
                    front(it, par, 1)
                fill("m8", "dt")
                if hasB:
                    turn_c(it, 1)
                fill("LN2a", "m4", "LN2b")
                if hasB:
                    back(it, par, 1)
                    front(it, par, 2)
                fill("router", "m5")
                if hasB:
                    turn_c(it, 2)
                fill("m6")
                if hasB:
                    back(it, par, 2)
                    front(it, par, 3)
                fill("gate", "up")
                if hasB:
                    turn_c(it, 3)
                fill("m7", "m0")
                if hasB:
                    back(it, par, 3)
                fill("m1", "down0", "down1", "m2", "m3", "sel")

            schedule(pe, iteration)

            pe.wait_ge(ktok_ready, 1)
            wait_read(pe, "sel", NSEQ - 1)
            tr(bTR[0:CAP, 0:E], ktok[:], ident[0:E, 0:E]).then_inc(tokt_ready, 1)
            pe.wait_ge(idx_ready, 1)

            def turn_tokens(i, n):
                pe.wait_ge(gathered[n], 16 * (i // WRING + 1) if isinstance(i, int) else (i - n) * 4 + 16)
                if not isinstance(i, int) or i > 0:
                    pe.wait_ge(xgt_copied, i)
                for k in range(KD):
                    last = tr(bXT[:, k * P:(k + 1) * P], xg[:, n, k:D:KD], ident[:])
                last.then_inc(xgt_ready, 1)

            def gate_up(i, n):
                bank_gu = bGU[n % 2]
                pe.wait_ge(xgt_copied, i + 1)
                pe.wait_ge(wx_loaded[n], 48 * (i // WRING + 1) if isinstance(i, int) else (i - n) * 12 + 48)
                if not isinstance(i, int) or i > 1:
                    pe.wait_ge(ehs_ready, i - 1)
                for e in range(2):
                    for u, w in enumerate((wgr, wur)):
                        o = u * P + e * 64
                        for k in range(KD):
                            last = mm(bank_gu[0:F, o:o + 64], w[:, n, e, k], xgT[:, n % 2, k, e * 64:(e + 1) * 64],
                                      start=(k == 0), stop=(k == KD - 1))
                last.then_inc(gu_ready, 1)

            def token_rows(i, n):
                pe.wait_ge(tokc_ready, i + 1)
                if not isinstance(i, int) or i > 0:
                    pe.wait_ge(eq_ready, i)
                mm(bSM[:, 0:P], tokc[:, n % 2].to_broadcast([P, P]), ident[:], start=True, stop=True).then_inc(rowb_ready, 1)

            def down(i, n):
                pe.wait_ge(ehs_ready, i + 1)
                if not isinstance(i, int) or i > 0:
                    pe.wait_ge(ow_ready, i)
                for e in range(2):
                    last = mm(bY[e * 64:(e + 1) * 64, 0:D], ehs[:, n % 2, e * 64:(e + 1) * 64], wdr[:, n, e],
                              start=True, stop=True)
                last.then_inc(down_ready, 1)

            def sum_tokens(i, n):
                pe.wait_ge(ow_ready, i + 1)
                pe.wait_ge(eq_ready, i + 1)
                if not isinstance(i, int) or i > 0:
                    pe.wait_ge(oc_ready, i)
                mm(bCS[:, 0:D], eq[:, n % 2], ow[:, n % 2], start=True, stop=True).then_inc(sum_ready, 1)

            def expert_step(i, n):
                if not isinstance(i, int) or 1 <= i <= ET:
                    token_rows(i - 1, (n - 1) % WRING)
                if not isinstance(i, int) or i + 1 < ET:
                    turn_tokens(i + 1, (n + 1) % WRING)
                if not isinstance(i, int) or 2 <= i:
                    sum_tokens(i - 2, (n - 2) % WRING)
                if not isinstance(i, int) or i < ET:
                    gate_up(i, n)
                if not isinstance(i, int) or 1 <= i <= ET:
                    down(i - 1, (n - 1) % WRING)

            turn_tokens(0, 0)
            expert_schedule(pe, expert_step)

        @block.scalar
        def _(act):
            fn = nc.scalar.activation

            def some(s):
                return not isinstance(s, int)

            def copy_in(s, k):
                act.wait_ge(trA_ready, at(s, KD, k))
                fn(xnT[:, k], bTR[:], ACT.Copy).then_inc(trA_copied, 1)

            def copy_mid(s, k):
                act.wait_ge(trC_ready, at(s, KD, k))
                fn(x2T[:, k], bTR[:], ACT.Copy).then_inc(trC_copied, 1)

            def tap(s, n):
                c = 4 if n == 0 else n - 1
                act.wait_ge(projA_ready, at(s, len(A_SLOTS), A_SLOTS.index(CONV[n])))
                if n >= 2:
                    act.wait_ge(xc_ready, at(s, 5, n - 2))
                elif some(s) or s > 0:
                    act.wait_ge(xc_ready, at(s - 1, 5, n + 3))
                fn(acc[:, n % 2], bR[BANK[CONV[n]]][:], ACT.Identity, bias=cb[:, c:c + 1],
                   scale=cw[:, c, 3:4]).then_inc(tap_ready, 1)

            def conv_tanh(s, n):
                act.wait_ge(conv_ready, at(s, 5, n))
                fn(cth[:, n % 2], acc[:, n % 2], ACT.Tanh, scale=0.5).then_inc(cth_step, 1)
                act.wait_ge(cth_step, at(s, 5, n))
                fn(cth[:, n % 2], cth[:, n % 2], ACT.Copy, bias=1.0).then_inc(cth_ready, 1)

            def z_tanh(s, n):
                act.wait_ge(projA_ready, at(s, len(A_SLOTS), A_SLOTS.index(ZT[n])))
                if n >= 2:
                    act.wait_ge(sz_ready, at(s, 4, n - 2))
                elif some(s) or s > 0:
                    act.wait_ge(sz_ready, at(s - 1, 4, n + 2))
                fn(zth[:, n % 2], bR[BANK[ZT[n]]][:], ACT.Tanh, scale=0.5).then_inc(zth_ready, 1)

            def dt_exp(s):
                act.wait_ge(dtabs_ready, at(s, 1))
                fn(dtv[:, 2], dtv[:, 1], ACT.Exp).then_inc(dte_ready, 1)

            def seg_exp(s, j):
                b = j % 2
                act.wait_ge(seg_ready, at(s, TILES, j))
                if j >= 2:
                    act.wait_ge(w_ready, at(s, TILES, j - 2))
                    act.wait_ge(bd_ready, at(s, 3, j - 2))
                elif some(s) or s > 0:
                    act.wait_ge(w_ready, at(s - 1, TILES, j + 2))
                    act.wait_ge(bd_ready, at(s - 1, 3, min(j + 2, 2)))
                fn(Ex[:, b].rearrange("p h q -> p (h q)"), bSEG[:], ACT.Exp).then_inc(ex_ready, 1)
                act.wait_ge(cb_ready, at(s, TILES, j))
                if j >= 2:
                    act.wait_ge(s_ready, at(s, 3, j - 2))
                    if j == 3:
                        act.wait_ge(cs_ready, at(s, 3, 0))
                elif some(s) or s > 0:
                    act.wait_ge(s_ready, at(s - 1, 3, 2))
                    act.wait_ge(cs_ready, at(s - 1, 3, 2 if j == 1 else 1))
                fn(ec[:, b], sm[:, b, P:P + 6], ACT.Exp).then_inc(ec_ready, 1)

            def copy_c(s, j):
                act.wait_ge(cst_ready, at(s, 3, j - 1))
                if j >= 3:
                    act.wait_ge(y_ready, at(s, TILES, j - 2))
                elif some(s) or s > 0:
                    act.wait_ge(y_ready, at(s - 1, TILES, TILES - 1))
                for hl in range(2):
                    r = slice(hl * N, (hl + 1) * N)
                    last = fn(csT[r, j % 2].rearrange("p (a h) q -> p a h q", h=2)[:, :, hl],
                              bCS[r, 0:2 * P].rearrange("p (a q) -> p a q", a=2), ACT.Copy)
                last.then_inc(cst_copied, 1)

            def scale_x(s, par, j):
                act.wait_ge(xt_ready, at(s, TILES, j))
                if j == 0:
                    act.wait_ge(dt_ready, at(s, 1))
                if j >= 2:
                    act.wait_ge(y_ready, at(s, TILES, j - 2))
                elif some(s) or s > 0:
                    act.wait_ge(y_ready, at(s - 1, TILES, j + 2))
                for h in range(H):
                    last = fn(xd[:, j % 2, h], bXT[:, h * HD:(h + 1) * HD], ACT.Copy,
                              scale=dth[:, par, j * H + h:j * H + h + 1])
                last.then_inc(xd_ready, 1)

            def square(s, j):
                act.wait_ge(y_ready, at(s, TILES, j))
                if j >= 2:
                    act.wait_ge(ss_ready, at(s, TILES, j - 2))
                elif some(s) or s > 0:
                    act.wait_ge(ss_ready, at(s - 1, TILES, j + 2))
                fn(sq[:, j % 2].rearrange("p h q -> p (h q)"), bY[:], ACT.Square).then_inc(sq_ready, 1)

            def router_exp(s):
                act.wait_ge(projC_ready, 1 + at(s, len(C_SLOTS), C_SLOTS.index("router")))
                if some(s) or s > 0:
                    act.wait_ge(sel_ready, 1 + at(s - 1, 1))
                fn(lex[:].rearrange("p j e -> p (j e)"), bR[BANK["router"]][:, 0:TILES * E], ACT.Exp,
                   scale=-1.0).then_inc(lex_ready, 1)

            def gate_tanh(s):
                act.wait_ge(projC_ready, 1 + at(s, len(C_SLOTS), C_SLOTS.index("gate")))
                if some(s) or s > 0:
                    act.wait_ge(hs_ready, 1 + at(s - 1, 1))
                fn(gth[:], bR[BANK["gate"]][0:F, :], ACT.Tanh, scale=0.5).then_inc(gth_ready, 1)

            act.wait_ge(w_loaded, 16 * 12)
            act.wait_ge(consts_ready, 1)
            fn(abc[:], abc[:], ACT.Exp).then_inc(abc_exp, 1)

            def iteration(it, par, hasA, hasB, hasC, before):
                a, c = it + 1, it - 1
                if hasB:
                    scale_x(it, par, 0)
                    seg_exp(it, 0)
                if hasA:
                    copy_in(a, 0)
                    copy_in(a, 1)
                if hasB:
                    square(it, 0)
                    scale_x(it, par, 1)
                    seg_exp(it, 1)
                if hasA:
                    tap(a, 0)
                    dt_exp(a)
                if hasB:
                    copy_c(it, 1)
                if hasA:
                    conv_tanh(a, 0)
                if hasC:
                    copy_mid(c, 0)
                if hasA:
                    tap(a, 1)
                if hasC:
                    copy_mid(c, 1)
                if hasB:
                    square(it, 1)
                    scale_x(it, par, 2)
                    seg_exp(it, 2)
                if hasA:
                    conv_tanh(a, 1)
                if hasC:
                    router_exp(c)
                if hasA:
                    tap(a, 2)
                if hasB:
                    copy_c(it, 2)
                if hasA:
                    tap(a, 3)
                    conv_tanh(a, 2)
                if hasB:
                    square(it, 2)
                    scale_x(it, par, 3)
                    seg_exp(it, 3)
                if hasC:
                    gate_tanh(c)
                if hasB:
                    copy_c(it, 3)
                if hasA:
                    conv_tanh(a, 3)
                    tap(a, 4)
                    z_tanh(a, 0)
                if hasB:
                    square(it, 3)
                if hasA:
                    conv_tanh(a, 4)
                    z_tanh(a, 1)
                    z_tanh(a, 2)
                    z_tanh(a, 3)

            schedule(act, iteration)

            def copy_tokens(i, n):
                act.wait_ge(xgt_ready, i + 1)
                if not isinstance(i, int) or i >= 2:
                    act.wait_ge(gu_ready, i - 1)
                fn(xgT[:, n % 2].rearrange("p k q -> p (k q)"), bXT[:, 0:KD * P], ACT.Copy).then_inc(xgt_copied, 1)

            def expert_step(i, n):
                if not isinstance(i, int) or i + 1 < ET:
                    copy_tokens(i + 1, (n + 1) % WRING)
                if not isinstance(i, int) or i >= 2:
                    act.wait_ge(sum_ready, i - 1)
                    if not isinstance(i, int) or i >= 4:
                        act.wait_ge(scattered, 16 * (i - 3))
                    fn(oc[:, n % 2], bCS[:, 0:D], ACT.Copy).then_inc(oc_ready, 1)
                if not isinstance(i, int) or i < ET:
                    act.wait_ge(gu_ready, i + 1)
                    if not isinstance(i, int) or i >= 2:
                        act.wait_ge(ehs_ready, i - 1)
                    fn(eth[:, n % 2], bGU[n % 2][0:F, 0:P], ACT.Tanh, scale=0.5).then_inc(eth_ready, 1)

            copy_tokens(0, 0)
            expert_schedule(act, expert_step)

        @block.gpsimd
        def _(pool):
            tt = nc.gpsimd.tensor_tensor

            def some(s):
                return not isinstance(s, int)

            nconst = [0]

            def const(ins):
                ins.then_inc(pool_const, 1)
                nconst[0] += 1
                pool.wait_ge(pool_const, nconst[0])

            const(nc.gpsimd.memset(ones[:], 1.0))
            sel_of = nc.gpsimd.affine_select
            const(sel_of(ident[:], ones[:], [[1, P]], ALU.is_equal, 0.0, base=0, channel_multiplier=-1))
            const(sel_of(tri[:], ones[:], [[1, P]], ALU.is_ge, 0.0, base=0, channel_multiplier=-1))
            const(sel_of(strict[:], ones[:], [[-1, P]], ALU.is_gt, 0.0, base=0, channel_multiplier=1))
            const(nc.gpsimd.iota(rank_i, [[-1, L]], base=L, channel_multiplier=0))
            const(nc.gpsimd.tensor_copy(rank_rev[:], rank_i))
            const(nc.gpsimd.iota(spare_i[:], [[0, 1]], base=T, channel_multiplier=1))
            const(nc.gpsimd.tensor_copy(spare[:], spare_i[:]))
            const(nc.gpsimd.memset(zrow[:], 0.0))
            const(nc.gpsimd.memset(exponent[:], -0.5))
            const(nc.gpsimd.memset(csT[:], 0.0))
            const(nc.gpsimd.memset(keys[:], 0.0))
            nc.gpsimd.memset(gsx[:], -BIG).then_inc(consts_ready, 1)
            pool.wait_ge(abc_ready, 2)
            tt(dskip_diag[:], ident[:].rearrange("p (o q) -> p o q", o=1).to_broadcast([P, H, P]),
               dsk[:].rearrange("p (h o) -> p h o", o=1).to_broadcast([P, H, P]), ALU.mult).then_inc(skip_made, 1)

            def decay_in(s, par, j):
                b = j % 2
                if j == 0:
                    pool.wait_ge(dt_ready, at(s, 1))
                if j >= 2:
                    pool.wait_ge(seg_ready, at(s, TILES, j - 2))
                elif some(s) or s > 0:
                    pool.wait_ge(seg_ready, at(s - 1, TILES, j + 2))
                tt(datri[:, b], tri[:].rearrange("p (o q) -> p o q", o=1).to_broadcast([P, H, P]),
                   dA[:, par, j * H:(j + 1) * H].rearrange("p (h o) -> p h o", o=1).to_broadcast([P, H, P]),
                   ALU.mult).then_inc(datri_ready, 1)

            def weigh(s, j):
                b = j % 2
                pool.wait_ge(ex_ready, at(s, TILES, j))
                pool.wait_ge(cb_ready, at(s, TILES, j))
                if j >= 2:
                    pool.wait_ge(y_ready, at(s, TILES, j - 2))
                elif some(s) or s > 0:
                    pool.wait_ge(y_ready, at(s - 1, TILES, j + 2))
                tt(Wt[:, b], Ex[:, b], cbm[:, b].rearrange("p (o q) -> p o q", o=1).to_broadcast([P, H, P]),
                   ALU.mult).then_inc(w_ready, 1)

            def conv_silu(s, par, n):
                c = 4 if n == 0 else n - 1
                pool.wait_ge(cth_ready, at(s, 5, n))
                if n == 0 and (some(s) or s >= 2):
                    pool.wait_ge(y_ready, at(s - 2, TILES, TILES - 1))
                    pool.wait_ge(ct_moved, 16 * (s - 1))
                tt(xc[:, par, c], cth[:, n % 2], acc[:, n % 2], ALU.mult).then_inc(xc_ready, 1)

            def sum_squares(s, par, j):
                b = j % 2
                pool.wait_ge(sq_ready, at(s, TILES, j))
                if j == 0 and (some(s) or s >= 2):
                    pool.wait_ge(projC_ready, 1 + at(s - 2, len(C_SLOTS), len(C_SLOTS) - 1))
                tt(sqh[:, b], sq[:, b, 0:2], sq[:, b, 2:4], ALU.add).then_inc(sqh_step, 1)
                pool.wait_ge(sqh_step, at(s, TILES, j))
                tt(ss[:, par, j * P:(j + 1) * P], sqh[:, b, 0], sqh[:, b, 1], ALU.add).then_inc(ss_ready, 1)

            def root(s, y, val, given, made):
                pool.wait_ge(given, at(s, 1))
                tt(y[:], val[:], exponent[:], ALU.pow).then_inc(made, 1)

            def iteration(it, par, hasA, hasB, hasC, before):
                a, ap = it + 1, 1 - par
                if hasB:
                    decay_in(it, par, 0)
                    decay_in(it, par, 1)
                if hasA:
                    root(a, nw, ve, ln1_var, ln1_root)
                if hasC:
                    root(it - 1, rms, ms, ssq_read, rms_root)
                if hasB:
                    weigh(it, 0)
                    sum_squares(it, par, 0)
                if hasC:
                    root(it - 1, nwc, vec, ln2_var, ln2_root)
                if hasB:
                    decay_in(it, par, 2)
                    weigh(it, 1)
                if hasA:
                    conv_silu(a, ap, 0)
                if hasB:
                    sum_squares(it, par, 1)
                    decay_in(it, par, 3)
                    weigh(it, 2)
                if hasA:
                    conv_silu(a, ap, 1)
                    conv_silu(a, ap, 2)
                if hasB:
                    sum_squares(it, par, 2)
                    weigh(it, 3)
                if hasA:
                    conv_silu(a, ap, 3)
                if hasB:
                    sum_squares(it, par, 3)
                if hasA:
                    conv_silu(a, ap, 4)

            schedule(pool, iteration)

            pool.wait_ge(idx_ready, 1)
            pool.wait_ge(rows_stored, 1 + 16 * NSEQ)
            pool.wait_ge(y_stored, 1 + 16 * NSEQ)
            pool.wait_ge(pad_stored, 32)

            def gather(i, n):
                if some(i) or i >= WRING:
                    pool.wait_ge(ow_ready, i - WRING + 1)
                nc.gpsimd.tensor_copy(idxc[:, n], idxT[:, bass.ds(i, 1)]).then_inc(idxc_ready, 1)
                pool.wait_ge(idxc_ready, i + 1)
                apart(pool)
                nc.gpsimd.indirect_dma_start(out=xg[:, n], out_offset=None, in_=rows[:, :],
                                             in_offset=bass.IndirectOffsetOnAxis(ap=idxc[:, n], axis=0)
                                             ).then_inc(gathered[n], 16)

            def scatter(i, n):
                pool.wait_ge(oc_ready, i + 1)
                pool.wait_ge(sidx_ready, i + 1)
                if some(i) or i > 0:
                    pool.wait_ge(scattered, 16 * i)
                apart(pool)
                nc.gpsimd.indirect_dma_start(out=out[:, :], out_offset=bass.IndirectOffsetOnAxis(ap=sidxi[:, n], axis=0),
                                             in_=oc[:, n % 2], in_offset=None, compute_op=ALU.add
                                             ).then_inc(scattered, 16)

            def expert_step(i, n):
                if some(i) or i + 2 < ET:
                    gather(i + 2, (n + 2) % WRING)
                if some(i) or i >= 2:
                    scatter(i - 2, (n - 2) % WRING)

            for n in range(2):
                gather(n, n)
            expert_schedule(pool, expert_step)

        @block.vector
        def _(dve):
            v = nc.vector
            tt, ts, stt, cp = v.tensor_tensor, v.tensor_scalar, v.scalar_tensor_tensor, v.tensor_copy

            def some(s):
                return not isinstance(s, int)

            def statistics(src, st, m, summed, aggregated, var, var_ready, s):
                for j in range(TILES):
                    last = v.bn_stats(st[:, j], src[:, j])
                last.then_inc(summed, 1)
                dve.wait_ge(summed, at(s, 1))
                apart(dve)
                for j in range(TILES):
                    last = v.bn_aggr(m[:, j], st[:, j])
                last.then_inc(aggregated, 1)
                dve.wait_ge(aggregated, at(s, 1))
                ts(var[:], m[:, :, 1], LN_EPS, None, ALU.add).then_inc(var_ready, 1)

            def normalise(src, dst, m, y):
                for j in range(TILES):
                    last = ts(dst[:, j, 0:D], src[:, j], m[:, j, 0:1], y[:, j:j + 1], ALU.subtract, ALU.mult)
                return last

            def ln1_in(s, par):
                dve.wait_ge(x_loaded[par], (s // 2 + 1) * 16 if isinstance(s, int) else (s - par) * 8 + 16)
                statistics(xin[:, par], st6, mv, ln1_sums, ln1_mean, ve, ln1_var, s)

            def ln1_out(s, par):
                if some(s) or s > 0:
                    dve.wait_ge(trA_ready, at(s - 1, KD, KD - 1))
                dve.wait_ge(ln1_root, at(s, 1))
                normalise(xin[:, par], xn, mv, nw).then_inc(xn_ready, 1)

            def dt_stage(s, par):
                c = Chain(dve, dt_step, s, DT_CHAIN)
                q = lambda n: dtv[:, n]
                raw = bR[BANK["dt"]][:, 0:TILES * H].rearrange("p (j h) -> p j h", h=H)
                dve.wait_ge(projA_ready, at(s, len(A_SLOTS), A_SLOTS.index("dt")))
                if some(s) or s > 0:
                    dve.wait_ge(dt_ready, at(s - 1, 1))
                tt(dtv[:, 0].rearrange("p (j h) -> p j h", h=H), raw,
                   dtb[:].rearrange("p (o h) -> p o h", o=1).to_broadcast([P, TILES, H]),
                   ALU.add).then_inc(dt_read, 1)
                dve.wait_ge(dt_read, at(s, 1))
                stt(q(1), q(0), -1.0, q(0), ALU.mult, ALU.min).then_inc(dtabs_ready, 1)
                dve.wait_ge(dte_ready, at(s, 1))
                link = c.link
                link(ts(q(3), q(2), 2.0, None, ALU.add))
                link(v.reciprocal(q(4), q(3)))
                link(tt(q(3), q(2), q(4), ALU.mult))
                link(tt(q(4), q(3), q(3), ALU.mult))
                link(ts(q(5), q(4), 1.0 / 17, None, ALU.mult))
                for k in (15, 13, 11, 9, 7, 5, 3):
                    link(stt(q(5), q(5), 1.0 / k, q(4), ALU.add, ALU.mult))
                link(stt(q(5), q(5), 1.0, q(3), ALU.add, ALU.mult))
                link(ts(q(6), q(0), 0.0, None, ALU.max))
                if some(s) or s >= 2:
                    dve.wait_ge(datri_ready, at(s - 2, TILES, TILES - 1))
                    dve.wait_ge(small_ready, at(s - 2, TILES, TILES - 1))
                    dve.wait_ge(xd_ready, at(s - 2, TILES, TILES - 1))
                link(stt(q(7), q(5), 2.0, q(6), ALU.mult, ALU.add))
                link(ts(dth[:, par], q(7), 0.5, None, ALU.mult))
                tt(dA[:, par].rearrange("p (j h) -> p j h", h=H), q(7).rearrange("p (j h) -> p j h", h=H),
                   abc[:].rearrange("p (o h) -> p o h", o=1).to_broadcast([P, TILES, H]),
                   ALU.mult).then_inc(dt_ready, 1)
                c.done()

            def conv(s, n):
                c = 4 if n == 0 else n - 1
                src = bR[BANK[CONV[n]]]
                dve.wait_ge(tap_ready, at(s, 5, n))
                a = acc[:, n % 2]
                for k in (1, 2):
                    stt(a[:, k:L], src[:, 0:L - k], cw[:, c, 3 - k:4 - k], a[:, k:L], ALU.mult, ALU.add
                        ).then_inc(conv_step, 1)
                    dve.wait_ge(conv_step, at(s, 10, 2 * n + k - 1))
                stt(a[:, 3:L], src[:, 0:L - 3], cw[:, c, 0:1], a[:, 3:L], ALU.mult, ALU.add
                    ).then_inc(conv_ready, 1)

            def z_silu(s, par, n):
                dve.wait_ge(zth_ready, at(s, 4, n))
                if n == 0 and (some(s) or s >= 2):
                    dve.wait_ge(g_ready, at(s - 2, TILES, TILES - 1))
                stt(sz[:, par, n], zth[:, n % 2], 1.0, bR[BANK[ZT[n]]][:], ALU.add, ALU.mult
                    ).then_inc(sz_ready, 1)

            def read_small(s, j):
                b = j % 2
                dve.wait_ge(small_ready, at(s, TILES, j))
                if j >= 2:
                    dve.wait_ge(w_ready, at(s, TILES, j - 2))
                    dve.wait_ge(ec_ready, at(s, TILES, j - 2))
                elif some(s) or s > 0:
                    dve.wait_ge(w_ready, at(s - 1, TILES, j + 2))
                    dve.wait_ge(ec_ready, at(s - 1, TILES, j + 2))
                stt(cbm[:, b], bSM[:, 0:P], 0.25, tri[:], ALU.mult, ALU.mult)
                cp(sm[:, b], bSM[:, P:2 * P + 6]).then_inc(cb_ready, 1)

            def decays(s, j):
                b = j % 2
                dve.wait_ge(ex_ready, at(s, TILES, j))
                dve.wait_ge(ec_ready, at(s, TILES, j))
                if j < TILES - 1:
                    tt(bd[:, b], sm[:, b, 0:N].rearrange("p (o n) -> p o n", o=1).to_broadcast([P, H, N]),
                       Ex[:, b, :, P - 1:P].to_broadcast([P, H, N]), ALU.mult).then_inc(bd_ready, 1)
                if j > 0:
                    stt(cs[:, b], sm[:, b, N:2 * N].rearrange("p (o n) -> p o n", o=1).to_broadcast([P, H, N]),
                        0.25, ec[:, b, 0:H].rearrange("p (h o) -> p h o", o=1).to_broadcast([P, H, N]),
                        ALU.mult, ALU.mult).then_inc(cs_ready, 1)

            def state(s, j):
                b, nb = j % 2, (j + 1) % 2
                dve.wait_ge(ds_ready, at(s, 3, j))
                if j == 2:
                    dve.wait_ge(y_ready, at(s, TILES, 1))
                elif some(s) or s > 0:
                    dve.wait_ge(y_ready, at(s - 1, TILES, TILES - 1))
                if j == 0:
                    cp(S[:, nb], bCS[:, 2 * P:4 * P].rearrange("p (a q) -> p a q", a=2)).then_inc(s_ready, 1)
                else:
                    for a in range(2):
                        last = stt(S[:, nb, a], S[:, b, a], ec[:, b, H + a:H + a + 1],
                                   bCS[:, 2 * P + a * HD:2 * P + (a + 1) * HD], ALU.mult, ALU.add)
                    last.then_inc(s_ready, 1)
                dve.wait_ge(s_ready, at(s, 3, j))

            def tile_out(s, par, j):
                dve.wait_ge(y_ready, at(s, TILES, j))
                dve.wait_ge(sq_ready, at(s, TILES, j))
                if j == 0 and (some(s) or s >= 2):
                    dve.wait_ge(projC_ready, 1 + at(s - 2, len(C_SLOTS), len(C_SLOTS) - 1))
                tt(g[:, par, :, j * P:(j + 1) * P], bY[:].rearrange("p (h q) -> p h q", h=H),
                   sz[:, par, :, j * P:(j + 1) * P], ALU.mult).then_inc(g_ready, 1)

            def c_ready(s, name):
                dve.wait_ge(projC_ready, 1 + at(s, len(C_SLOTS), C_SLOTS.index(name)))

            def mean_square(s):
                c_ready(s, "ssq")
                ts(ms[:], bR[BANK["ssq"]][:, 0:TILES], 4.0 / DI, 4.0 * RMS_EPS, ALU.mult, ALU.add
                   ).then_inc(ssq_read, 1)

            def residual(s, half):
                if half == 0:
                    dve.wait_ge(rms_root, at(s, 1))
                    dve.wait_ge(xres_loaded, 16 * (s + 1))
                    if some(s) or s > 0:
                        dve.wait_ge(yo_ready, 1 + at(s - 1, 2, 1))
                c_ready(s, f"out{half}")
                for q in range(2):
                    j = 2 * half + q
                    last = stt(x1[:, j], bR[BANK[f"out{half}"]][:, q * D:(q + 1) * D], rms[:, j:j + 1],
                               xres[:, j], ALU.mult, ALU.add)
                last.then_inc(x1_ready, 1)

            def ln2_in(s):
                wait_read(dve, "out1", s)
                statistics(x1, st6c, mvc, ln2_sums, ln2_mean, vec, ln2_var, s)

            def ln2_out(s):
                if some(s) or s > 0:
                    dve.wait_ge(rows_stored, 1 + 16 * s)
                dve.wait_ge(ln2_root, at(s, 1))
                normalise(x1, xr, mvc, nwc).then_inc(x2_ready, 1)

            def route_groups(s, c):
                link = c.link
                dve.wait_ge(lex_ready, at(s, 1))
                if some(s) or s > 0:
                    dve.wait_ge(projC_ready, 1 + at(s - 1, len(C_SLOTS), C_SLOTS.index("sel")))
                link(ts(lex[:], lex[:], 1.0, None, ALU.add))
                link(v.reciprocal(sc[:], lex[:]))
                link(tt(sbz[:], sc[:], bias_b[:].rearrange("p (o e) -> p o e", o=1).to_broadcast([P, TILES, E]),
                        ALU.add))
                pair = sbz[:].rearrange("p j (g q t) -> p (j g) q t", q=4, t=2)
                tt(hi[:], pair[:, :, :, 0], pair[:, :, :, 1], ALU.max)
                link(tt(lo[:], pair[:, :, :, 0], pair[:, :, :, 1], ALU.min))
                tt(hi2[:], hi[:, :, 0:2], hi[:, :, 2:4], ALU.max)
                tt(mn2[:], hi[:, :, 0:2], hi[:, :, 2:4], ALU.min)
                link(tt(lo2[:], lo[:, :, 0:2], lo[:, :, 2:4], ALU.max))
                link(tt(lo2[:], lo2[:], mn2[:], ALU.max))
                tt(gs3[:, 0], hi2[:, :, 0], hi2[:, :, 1], ALU.max)
                tt(gs3[:, 1], hi2[:, :, 0], hi2[:, :, 1], ALU.min)
                link(tt(gs3[:, 2], lo2[:, :, 0], lo2[:, :, 1], ALU.max))
                link(tt(gs3[:, 3], gs3[:, 1], gs3[:, 2], ALU.max))
                link(tt(gsx[:, :, 0:G], gs3[:, 0].rearrange("p (j g) -> p j g", g=G),
                        gs3[:, 3].rearrange("p (j g) -> p j g", g=G), ALU.add))

            def choose_groups(s, c):
                link = c.link
                apart(dve)
                for j in range(TILES):
                    last = v.max(m8g[:, j], gsx[:, j])
                link(last)
                link(v.memset(m8g[:, :, KG:8], -BIG))
                apart(dve)
                for j in range(TILES):
                    last = v.match_replace(grp[:, j], m8g[:, j], gsx[:, j], BIG)
                link(last)
                link(ts(gm[:], grp[:, :, 0:G], BIG, None, ALU.is_equal))
                ts(gneg[:], gm[:], 1.0, BIG, ALU.subtract, ALU.mult)
                gmb = gm[:].rearrange("p j (g o) -> p (j g) o", o=1).to_broadcast([P, TILES * G, EG])
                link(tt(tmp[:].rearrange("p j (g q) -> p (j g) q", q=EG),
                        sbz[:].rearrange("p j (g q) -> p (j g) q", q=EG), gmb, ALU.mult))
                link(tt(tmp[:].rearrange("p j (g q) -> p (j g) q", q=EG),
                        tmp[:].rearrange("p j (g q) -> p (j g) q", q=EG),
                        gneg[:].rearrange("p j (g o) -> p (j g) o", o=1).to_broadcast([P, TILES * G, EG]),
                        ALU.add))

            def choose_experts(s, c):
                link = c.link
                gmb = gm[:].rearrange("p j (g o) -> p (j g) o", o=1).to_broadcast([P, TILES * G, EG])
                apart(dve)
                for j in range(TILES):
                    last = v.max(m8e[:, j], tmp[:, j])
                link(last)
                link(v.memset(m8e[:, :, K:8], -BIG))
                apart(dve)
                for j in range(TILES):
                    last = v.match_replace(rep[:, j], m8e[:, j], tmp[:, j], BIG)
                link(last)
                link(stt(sel[:].rearrange("p j (g q) -> p (j g) q", q=EG),
                         rep[:].rearrange("p j (g q) -> p (j g) q", q=EG), BIG, gmb, ALU.is_equal, ALU.mult))
                tt(tmp[:], sel[:], sc[:], ALU.mult).then_inc(sel_ready, 1)

            def expert_weights_of(s, c):
                link = c.link
                dve.wait_ge(sel_ready, 1 + at(s, 1))
                link(v.tensor_reduce(wsum[:], tmp[:], AX.X, ALU.add))
                link(v.reciprocal(wrec[:], wsum[:]))
                stt(xr[:, :, D:ROW], tmp[:], SCALE,
                    wrec[:].rearrange("p (j o) -> p j o", o=1).to_broadcast([P, TILES, E]),
                    ALU.mult, ALU.mult).then_inc(rw_ready, 1)

            def shared(s, c):
                c_ready(s, "gate")
                dve.wait_ge(gth_ready, at(s, 1))
                if some(s) or s > 0:
                    dve.wait_ge(hs_ready, 1 + at(s - 1, 1))
                stt(gth[:], gth[:], 1.0, bR[BANK["gate"]][0:F, :], ALU.add, ALU.mult).then_inc(gate_read, 1)
                wait_read(dve, "gate", s)
                c_ready(s, "up")
                if some(s) or s > 0:
                    c_ready(s - 1, "sel")
                tt(hs[:], gth[:], bR[BANK["up"]][0:F, :], ALU.mult).then_inc(hs_ready, 1)

            def shared_out(s):
                if some(s) or s > 0:
                    dve.wait_ge(y_stored, 1 + 16 * s)
                for half in range(2):
                    c_ready(s, f"down{half}")
                    for q in range(2):
                        j = 2 * half + q
                        last = stt(yo[:, j], bR[BANK[f"down{half}"]][:, q * D:(q + 1) * D], 0.5, x1[:, j],
                                   ALU.mult, ALU.add)
                    last.then_inc(yo_ready, 1)

            def choose(s, par):
                c_ready(s, "sel")
                if some(s) or s > 0:
                    wait_read(dve, "sel", s - 1)
                tt(keys[par * E:(par + 1) * E, 0], bR[BANK["sel"]][0:E, :], rank_rev[0:E, :], ALU.mult
                   ).then_inc(keys_ready, 1)

            def take(k, rounds):
                def link(n, ins):
                    ins.then_inc(take_step, 1)
                    dve.wait_ge(take_step, 1 + k * TAKE + n)

                if 0 in rounds:
                    if some(k) or k > 0:
                        wait_read(dve, "sel", 2 * k - 1)
                for r in rounds:
                    apart(dve)
                    link(2 * r + 1, v.max(first[:, 8 * r:8 * r + 8], keys[:, r % 2]))
                    if r < ROUNDS - 1:
                        apart(dve)
                        link(2 * r + 2, v.match_replace(keys[:, (r + 1) % 2], first[:, 8 * r:8 * r + 8],
                                                        keys[:, r % 2], 0.0))
                    else:
                        dst = lists[:, k] if isinstance(k, int) else \
                            lists[:, bass.ds(dve.snap(k), 1)].rearrange("p o q -> p (o q)")
                        link(TAKE, cp(dst, first[:]))

            dve.wait_ge(abc_exp, 1)
            ts(abc[:], abc[:], -1.0, None, ALU.mult).then_inc(abc_ready, 1)
            dve.wait_ge(w_loaded, 16 * 12)
            dve.wait_ge(abc_ready, 1)
            ts(dsk[:], dsk[:], 0.5, None, ALU.mult).then_inc(abc_ready, 1)
            dve.wait_ge(abc_ready, 2)
            dve.wait_ge(consts_ready, 1)

            def iteration(it, par, hasA, hasB, hasC, before):
                a, ap, c, cpar = it + 1, 1 - par, it - 1, 1 - par
                ch = Chain(dve, c_step, c, C_CHAIN) if hasC else None
                if hasB:
                    read_small(it, 0)
                if hasC:
                    mean_square(c)
                if hasA:
                    ln1_in(a, ap)
                if hasB:
                    decays(it, 0)
                if hasA:
                    ln1_out(a, ap)
                if hasC:
                    if cpar == 0:
                        k = (it - 1) // 2
                        take(k, range(3))
                    residual(c, 0)
                    if cpar == 0:
                        take(k, range(3, ROUNDS))
                    residual(c, 1)
                    ln2_in(c)
                if hasB:
                    state(it, 0)
                    tile_out(it, par, 0)
                    read_small(it, 1)
                    decays(it, 1)
                if hasC:
                    ln2_out(c)
                if hasA:
                    conv(a, 0)
                    dt_stage(a, ap)
                if hasB:
                    state(it, 1)
                    tile_out(it, par, 1)
                if hasA:
                    conv(a, 1)
                if hasB:
                    read_small(it, 2)
                    decays(it, 2)
                if hasC:
                    route_groups(c, ch)
                if hasA:
                    conv(a, 2)
                    conv(a, 3)
                if hasB:
                    state(it, 2)
                    tile_out(it, par, 2)
                    read_small(it, 3)
                    decays(it, 3)
                if hasC:
                    shared(c, ch)
                    choose_groups(c, ch)
                if hasA:
                    conv(a, 4)
                    z_silu(a, ap, 0)
                if hasB:
                    tile_out(it, par, 3)
                if hasA:
                    z_silu(a, ap, 1)
                if hasC:
                    choose_experts(c, ch)
                    shared_out(c)
                    expert_weights_of(c, ch)
                if hasA:
                    z_silu(a, ap, 2)
                    z_silu(a, ap, 3)
                if hasC:
                    choose(c, cpar)
                    ch.done()
            schedule(dve, iteration)
            take(NSEQ // 2, range(ROUNDS))

            nm = [0]

            def link(ins):
                ins.then_inc(merge_step, 1)
                nm[0] += 1
                dve.wait_ge(merge_step, nm[0])

            for u in range(NSEQ // 2):
                for par in range(2):
                    last = v.memset(base[par * E:(par + 1) * E, u:u + 1], float(T - L * (2 * u + par + 1)))
            link(last)
            link(v.memset(tokT[:], float(T)))
            link(stt(gk[:], lists[:, 1:], 0.0, base[:].rearrange("p (u o) -> p u o", o=1).to_broadcast([P, NSEQ // 2, CAP]),
                     ALU.is_gt, ALU.mult))
            link(tt(gk[:], gk[:], lists[:, 1:], ALU.add))
            for par in range(2):
                last = cp(cat[:, 0, par * 4 * CAP:(par + 1) * 4 * CAP], gk[par * E:(par + 1) * E].rearrange("p u q -> p (u q)"))
            link(last)
            for r in range(ROUNDS):
                link(v.max(kfirst[:, 8 * r:8 * r + 8], cat[:, r % 2]))
                if r < ROUNDS - 1:
                    link(v.match_replace(cat[:, (r + 1) % 2], kfirst[:, 8 * r:8 * r + 8], cat[:, r % 2], 0.0))
            ts(ktok[:], kfirst[:], -1.0, float(T), ALU.mult, ALU.add).then_inc(ktok_ready, 1)
            dve.wait_ge(tokt_ready, 1)
            for e in range(2):
                last = cp(tokT[e * 64:e * 64 + CAP], bTR[0:CAP, e:E:2])
            link(last)
            cp(idxT[:], tokT[:]).then_inc(idx_ready, 1)

            def same_token(i, n):
                b = n % 2

                def link(k, ins):
                    ins.then_inc(token_step, 1)
                    dve.wait_ge(token_step, i * 3 + k + 1)

                if some(i) or i >= 2:
                    dve.wait_ge(rowb_ready, i - 1)
                cp(tokc[:, n % 2], tokT[:, bass.ds(i, 1)]).then_inc(tokc_ready, 1)
                link(0, tt(sidx[:, b, 0:1], tokT[:, bass.ds(i, 1)], spare[:], ALU.subtract))
                dve.wait_ge(tokc_ready, i + 1)
                dve.wait_ge(rowb_ready, i + 1)
                if some(i) or i >= 2:
                    dve.wait_ge(sum_ready, i - 1)
                ts(eq[:, b], bSM[:, 0:P], tokc[:, n % 2], None, ALU.is_equal).then_inc(eq_ready, 1)
                dve.wait_ge(eq_ready, i + 1)
                if some(i) or i >= 3:
                    dve.wait_ge(scattered, 16 * (i - 2))
                link(1, v.tensor_tensor_reduce(out=eqs[:, b], in0=eq[:, b], in1=strict[:], scale=1.0, scalar=0.0,
                                               op0=ALU.mult, op1=ALU.add, accum_out=cnt[:, b]))
                link(2, stt(sidx[:, b, 1:2], cnt[:, b], 0.0, sidx[:, b, 0:1], ALU.is_equal, ALU.mult))
                tt(sidxi[:, n], sidx[:, b, 1:2], spare[:], ALU.add).then_inc(sidx_ready, 1)

            def activate(i, n):
                b = n % 2
                dve.wait_ge(eth_ready, i + 1)
                stt(ehg[:, b], eth[:, b], 1.0, bGU[b][0:F, 0:P], ALU.add, ALU.mult).then_inc(ehg_ready, 1)
                dve.wait_ge(ehg_ready, i + 1)
                if some(i) or i >= 2:
                    dve.wait_ge(down_ready, i - 1)
                tt(ehs[:, b], ehg[:, b], bGU[b][0:F, P:2 * P], ALU.mult).then_inc(ehs_ready, 1)

            def weight_of(i, n):
                dve.wait_ge(gathered[n], 16 * (i // WRING + 1) if isinstance(i, int) else (i - n) * 4 + 16)
                for e in range(2):
                    r = slice(e * 64, (e + 1) * 64)
                    off = D + 2 * i + e if isinstance(i, int) else dve.snap(2 * i + (D + e))
                    last = ts(wcol[r, n % 2], xg[r, n, bass.ds(off, 1)], 0.5, None, ALU.mult)
                last.then_inc(wcol_ready, 1)

            def weigh_out(i, n):
                dve.wait_ge(wcol_ready, i + 1)
                dve.wait_ge(down_ready, i + 1)
                if some(i) or i >= 2:
                    dve.wait_ge(sum_ready, i - 1)
                ts(ow[:, n % 2], bY[:, 0:D], wcol[:, n % 2], None, ALU.mult).then_inc(ow_ready, 1)

            def expert_step(i, n):
                if some(i) or 1 <= i <= ET:
                    same_token(i - 1, (n - 1) % WRING)
                if some(i) or i < ET:
                    weight_of(i, n)
                    activate(i, n)
                if some(i) or 1 <= i <= ET:
                    weigh_out(i - 1, (n - 1) % WRING)

            expert_schedule(dve, expert_step)


DT_CHAIN = 16
TAKE = 2 * ROUNDS
C_CHAIN = 21

def kernel(**inputs):
    import numpy as _np
    import concourse.bacc as _bacc
    from concourse import mybir as _mybir
    from concourse.bass_utils import run_bass_kernel_spmd as _run

    a = {k: _np.asarray(v) for k, v in inputs.items()}

    def spread(v):
        return _np.broadcast_to(v[None, :], (P, v.shape[0]))

    parts = {
        "x": a["L0_attn_x"].reshape(T, D),
        "w_in": a["L0_attn_W_in"].T.reshape(KD, P, PROJ + H).transpose(1, 0, 2),
        "conv_w": a["L0_attn_conv_w"].reshape(5, P, 4).transpose(1, 0, 2),
        "conv_b": a["L0_attn_conv_b"].reshape(5, P).T,
        "a_log": spread(a["L0_attn_A_log"]),
        "dt_bias": spread(a["L0_attn_dt_bias"]),
        "dskip": spread(a["L0_attn_D"]),
        "w_out": a["L0_attn_W_out"].T.reshape(H, P, D).transpose(1, 0, 2),
        "gate_w": a["L0_ffn_gate_w"].reshape(P, KD, E),
        "bias": spread(a["L0_ffn_bias"]),
        "w_gate": a["L0_ffn_w_gate"].reshape(ET, 2, P, KD, F).transpose(0, 2, 1, 3, 4),
        "w_up": a["L0_ffn_w_up"].reshape(ET, 2, P, KD, F).transpose(0, 2, 1, 3, 4),
        "w_down": a["L0_ffn_w_down"].reshape(ET, 2, F, D).transpose(0, 2, 1, 3),
        "ws_gate": a["L0_ffn_ws_gate"].reshape(P, KD, F),
        "ws_up": a["L0_ffn_ws_up"].reshape(P, KD, F),
        "ws_down": a["L0_ffn_ws_down"],
    }
    nc = _bacc.Bacc("TRN2", target_bir_lowering=False, num_devices=1)
    arrays, args = {}, {}
    for name, v in parts.items():
        v = _np.ascontiguousarray(v)
        arrays[f"in_{name}"] = v
        args[name] = nc.dram_tensor(f"in_{name}", v.shape, _mybir.dt.from_np(v.dtype), kind="ExternalInput").ap()
    rows = nc.dram_tensor("rows", (T + P, ROW), _mybir.dt.float32, kind="Internal").ap()
    out = nc.dram_tensor("out_y", (T + P, D), _mybir.dt.float32, kind="ExternalOutput").ap()
    build(nc, **args, rows=rows, out=out)
    r = _run(nc, [arrays], core_ids=[0])
    return r.results[0]["out_y"][:T].reshape(NSEQ, L, D)
```

```python
from contextlib import ExitStack

import concourse.bass as bass
from concourse import mybir

F32 = mybir.dt.float32
I32 = mybir.dt.int32
U32 = mybir.dt.uint32
ALU = mybir.AluOpType
ACT = mybir.ActivationFunctionType
AX = mybir.AxisListType

P = 128
NSEQ, L, D = 8, 512, 256
T = NSEQ * L
TILES = L // P
KD = D // P
H, HD = 4, 128
DI = H * HD
N = 64
PROJ = 2 * DI + 2 * N
E, K, F = 64, 6, 96
G, KG = 8, 4
EG = E // G
CAP = 2 * (256 * K // E)
SCALE = 2.5
ROW = D + E
LN_EPS, RMS_EPS = 1e-5, 1.1920929e-07
BIG = 3.0e38
ET = E // 2
WRING = 4
ROUNDS = CAP // 8

SLOTS = [("ssq", "C"), ("sel", "D"), ("out0", "C"), ("out1", "C"), ("m8", "A"), ("dt", "A"),
         ("m4", "A"), ("router", "C"), ("m5", "A"), ("m6", "A"), ("gate", "C"), ("up", "C"), ("m7", "A"),
         ("m0", "A"), ("m1", "A"), ("down0", "C"), ("down1", "C"), ("m2", "A"), ("m3", "A")]
BANK = {name: n % 2 for n, (name, _) in enumerate(SLOTS)}
A_SLOTS = [n for n, st in SLOTS if st == "A"]
C_SLOTS = [n for n, st in SLOTS if st == "C"]
CONV = ["m8", "m4", "m5", "m6", "m7"]
ZT = ["m0", "m1", "m2", "m3"]


def at(seq, per, n=0):
    return seq * per + (n + 1)


class Chain:

    def __init__(self, eng, sem, seq, per):
        self.eng, self.sem, self.seq, self.per, self.n = eng, sem, seq, per, 0

    def link(self, ins):
        ins.then_inc(self.sem, 1)
        self.n += 1
        self.eng.wait_ge(self.sem, at(self.seq, self.per, self.n - 1))

    def done(self):
        assert self.n == self.per, (str(self.sem), self.n, self.per)


def build(nc, x, w_in, conv_w, conv_b, a_log, dt_bias, dskip, w_out, gate_w, bias,
          w_gate, w_up, w_down, ws_gate, ws_up, ws_down, rows, out):
    x_t = x.rearrange("(s j p) d -> s p j d", j=TILES, p=P)
    rows_t = rows[0:T, :].rearrange("(s j p) d -> s p j d", j=TILES, p=P)
    out_t = out[0:T, :].rearrange("(s j p) d -> s p j d", j=TILES, p=P)

    with ExitStack() as ctx:
        def sb(name, shape, dt=F32):
            return ctx.enter_context(nc.sbuf_tensor(name, shape, dt))

        def sem(name):
            return ctx.enter_context(nc.semaphore(name))

        def bank(name):
            return ctx.enter_context(nc.psum_tensor(name, [P, 512], F32))

        win = sb("win", [P, KD, PROJ + H])
        wout = sb("wout", [P, H, D])
        gw = sb("gw", [P, KD, E])
        wsg = sb("wsg", [P, KD, F])
        wsu = sb("wsu", [P, KD, F])
        wsd = sb("wsd", [F, D])
        cw = sb("cw", [P, 5, 4])
        cb = sb("cb", [P, 5])
        abc = sb("abc", [P, H])
        dtb = sb("dtb", [P, H])
        dsk = sb("dsk", [P, H])
        dskip_diag = sb("dskip_diag", [P, H, P])
        bias_b = sb("bias_b", [P, E])
        ident = sb("ident", [P, P])
        tri = sb("tri", [P, P])
        strict = sb("strict", [P, P])
        ones = sb("ones", [P, P])
        rank_rev = sb("rank_rev", [P, L])
        spare_i = sb("spare_i", [P, 1], I32)
        spare = sb("spare", [P, 1])
        zrow = sb("zrow", [P, ROW])
        xin = sb("xin", [P, 2, TILES, D])
        st6 = sb("st6", [P, TILES, 6])
        mv = sb("mv", [P, TILES, 2])
        exponent = sb("exponent", [P, TILES])
        centre = sb("centre", [P, TILES])
        ve = sb("ve", [P, TILES])
        nw = sb("nw", [P, TILES])
        xn = sb("xn", [P, TILES, D])
        xnT = sb("xnT", [P, KD, L])
        acc = sb("acc", [P, 2, L])
        rank_i = acc[:, 0].bitcast(I32)
        cth = sb("cth", [P, 2, L])
        zth = sb("zth", [P, 2, L])
        xc = sb("xc", [P, 2, 5, L])
        ct0 = sb("ct0", [N, 2, L])
        sz = sb("sz", [P, 2, H, L])
        dtv = sb("dtv", [P, 8, TILES * H])
        dth = sb("dth", [P, 2, TILES * H])
        dA = sb("dA", [P, 2, TILES * H])
        datri = sb("datri", [P, 2, H, P])
        xd = sb("xd", [P, 2, H, HD])
        Ex = sb("Ex", [P, 2, H, P])
        cbm = sb("cbm", [P, 2, P])
        sm = sb("sm", [P, 2, P + 6])
        ec = sb("ec", [P, 2, 6])
        Wt = sb("Wt", [P, 2, H, P])
        bd = sb("bd", [P, 2, H, N])
        cs = sb("cs", [P, 2, H, N])
        csT = sb("csT", [P, 2, H, P])
        S = sb("S", [P, 2, 2, HD])
        sq = sb("sq", [P, 2, H, P])
        sqh = sq[:, :, 0:2]
        g = sb("g", [P, 2, H, L])
        ss = sb("ss", [P, 2, L])
        xres = sb("xres", [P, TILES, D])
        ms = sb("ms", [P, TILES])
        rms = sb("rms", [P, TILES])
        x1 = sb("x1", [P, TILES, D])
        st6c = sb("st6c", [P, TILES, 6])
        mvc = sb("mvc", [P, TILES, 2])
        centrec = sb("centrec", [P, TILES])
        vec = sb("vec", [P, TILES])
        nwc = sb("nwc", [P, TILES])
        xr = sb("xr", [P, TILES, ROW])
        x2T = sb("x2T", [P, KD, L])
        lex = sb("lex", [P, TILES, E])
        sc = sb("sc", [P, TILES, E])
        sbz = sb("sbz", [P, TILES, E])
        hi = sb("hi", [P, TILES * G, 4])
        lo = sb("lo", [P, TILES * G, 4])
        hi2 = sb("hi2", [P, TILES * G, 2])
        lo2 = sb("lo2", [P, TILES * G, 2])
        mn2 = sb("mn2", [P, TILES * G, 2])
        gsx = sb("gsx", [P, TILES, G + 4])
        gs3 = sb("gs3", [P, 4, TILES * G])
        m8g = sb("m8g", [P, TILES, 8])
        grp = sb("grp", [P, TILES, G + 4])
        gm = sb("gm", [P, TILES, G])
        gneg = sb("gneg", [P, TILES, G])
        tmp = sb("tmp", [P, TILES, E])
        m8e = sb("m8e", [P, TILES, 8])
        rep = lex
        sel = sb("sel", [P, TILES, E])
        wsum = sb("wsum", [P, TILES])
        wrec = sb("wrec", [P, TILES])
        gth = sb("gth", [F, L])
        hs = sb("hs", [F, L])
        yo = sb("yo", [P, TILES, D])
        keys = sb("keys", [P, 2, CAP + L])
        first = sb("first", [P, CAP])
        lists = sb("lists", [P, NSEQ // 2, CAP])
        kfirst = sb("kfirst", [P, CAP])
        ktok = sb("ktok", [P, CAP])
        tokT = sb("tokT", [P, ET])
        idxT = sb("idxT", [P, ET], I32)
        idxc = sb("idxc", [P, WRING, 1], I32)
        tokc = sb("tokc", [P, 2, 1])
        wgu = sb("wgu", [P, WRING, 2, 2, KD, F])
        wdr = sb("wdr", [F, WRING, 2, D])
        wcol = sb("wcol", [P, 2, 1])
        cnt = sb("cnt", [P, 2, 1])
        sidx = sb("sidx", [P, 2, 2])
        sidxi = sb("sidxi", [P, WRING, 1], I32)
        flat, used = {"g": g[:].rearrange("p a h l -> p (a h l)"), "sz": sz[:].rearrange("p a h l -> p (a h l)")}, {"g": 0, "sz": 0}

        def part(n, of="g", rows_=P):
            used[of] += n
            return flat[of][0:rows_, used[of] - n:used[of]]

        xg = part(WRING * ROW).rearrange("p (n d) -> p n d", n=WRING)
        xgT = part(2 * D).rearrange("p (n k q) -> p n k q", n=2, k=KD)
        oc = part(2 * D).rearrange("p (n d) -> p n d", n=2)
        eq = part(2 * P).rearrange("p (n q) -> p n q", n=2)
        eqs = part(2 * P).rearrange("p (n q) -> p n q", n=2)
        PAIRS = NSEQ // 2 - 1
        base = part(PAIRS, "sz")
        gk = part(PAIRS * CAP, "sz").rearrange("p (u q) -> p u q", q=CAP)
        cat = part(2 * (2 * PAIRS * CAP + L), "sz", E).rearrange("p (n q) -> p n q", n=2)
        eth, ehg, ehs = (part(2 * F, "sz").rearrange("p (n q) -> p n q", n=2) for _ in range(3))
        hsum = part(4 * P, "sz", F).rearrange("p (n e q) -> p n e q", n=2, e=2)

        bTR = bank("bTR")
        bR = [bank("bR0"), bank("bR1")]
        bXT = bank("bXT")
        bSEG = bank("bSEG")
        bSM = bank("bSM")
        bCS = bank("bCS")
        bY = bank("bY")
        bGU = [bSEG, bTR]

        sems = {}

        def S_(name):
            if name not in sems:
                sems[name] = sem(name)
            return sems[name]

        w_loaded = S_("w_loaded")
        consts_ready = S_("consts_ready")
        pool_const = S_("pool_const")
        abc_exp = S_("abc_exp")
        abc_ready = S_("abc_ready")
        x_loaded = [S_("x_loaded0"), S_("x_loaded1")]
        xres_loaded = S_("xres_loaded")
        ct_moved = S_("ct_moved")
        rows_stored = S_("rows_stored")
        y_stored = S_("y_stored")
        pad_stored = S_("pad_stored")
        xn_ready = S_("xn_ready")
        ln1_sums, ln1_var, ln1_root = S_("ln1_sums"), S_("ln1_var"), S_("ln1_root")
        ln2_sums, ln2_var, ln2_root = S_("ln2_sums"), S_("ln2_var"), S_("ln2_root")
        xn_centred, x2_centred = S_("xn_centred"), S_("x2_centred")
        ln1_mean, ln2_mean, rms_root = S_("ln1_mean"), S_("ln2_mean"), S_("rms_root")
        trA_ready, trA_copied = S_("trA_ready"), S_("trA_copied")
        trC_ready, trC_copied = S_("trC_ready"), S_("trC_copied")
        projA_ready, projC_ready = S_("projA_ready"), S_("projC_ready")
        dt_read, ssq_read, gate_read, keys_ready = S_("dt_read"), S_("ssq_read"), S_("gate_read"), S_("keys_ready")
        tap_ready, conv_step, conv_ready, cth_ready, xc_ready = (
            S_("tap_ready"), S_("conv_step"), S_("conv_ready"), S_("cth_ready"), S_("xc_ready"))
        cth_step = S_("cth_step")
        zth_ready, sz_ready = S_("zth_ready"), S_("sz_ready")
        dt_step, dtabs_ready, dte_ready, dt_ready = (
            S_("dt_step"), S_("dtabs_ready"), S_("dte_ready"), S_("dt_ready"))
        datri_ready, seg_ready, ex_ready = S_("datri_ready"), S_("seg_ready"), S_("ex_ready")
        xt_ready, xd_ready = S_("xt_ready"), S_("xd_ready")
        small_ready, cb_ready, ec_ready = S_("small_ready"), S_("cb_ready"), S_("ec_ready")
        w_ready, bd_ready, cs_ready = S_("w_ready"), S_("bd_ready"), S_("cs_ready")
        cst_ready, cst_copied = S_("cst_ready"), S_("cst_copied")
        ds_ready, s_ready = S_("ds_ready"), S_("s_ready")
        y_ready, skip_made = S_("y_ready"), S_("skip_made")
        g_ready, sq_ready, sqh_step, ss_ready = S_("g_ready"), S_("sq_ready"), S_("sqh_step"), S_("ss_ready")
        c_step, x1_ready, x2_ready, lex_ready = S_("c_step"), S_("x1_ready"), S_("x2_ready"), S_("lex_ready")
        selt_ready = S_("selt_ready")
        sel_ready, rw_ready = S_("sel_ready"), S_("rw_ready")
        gth_ready, hs_ready, yo_ready = S_("gth_ready"), S_("hs_ready"), S_("yo_ready")
        take_step = S_("take_step")
        merge_step, ktok_ready, tokt_ready, idx_ready = (
            S_("merge_step"), S_("ktok_ready"), S_("tokt_ready"), S_("idx_ready"))
        wx_loaded = [S_(f"wx_loaded{n}") for n in range(WRING)]
        idxc_ready, gathered = S_("idxc_ready"), [S_(f"gathered{n}") for n in range(WRING)]
        scattered = S_("scattered")
        xgt_ready, xgt_copied = S_("xgt_ready"), S_("xgt_copied")
        gu_ready, eth_ready, ehg_ready, ehs_ready = S_("gu_ready"), S_("eth_ready"), S_("ehg_ready"), S_("ehs_ready")
        token_step, wcol_ready = S_("token_step"), S_("wcol_ready")
        hsum_ready, hsum_copied, down_ready = S_("hsum_ready"), S_("hsum_copied"), S_("down_ready")
        tokc_ready, rowb_ready, eq_ready, sidx_ready = (
            S_("tokc_ready"), S_("rowb_ready"), S_("eq_ready"), S_("sidx_ready"))
        oc_ready = S_("oc_ready")

        credited = [trC_copied, sel_ready, hs_ready, projC_ready, yo_ready, x1_ready,
                    rows_stored, y_stored, take_step]

        waits_passed = S_("waits_passed")

        def apart(eng):
            eng.sem_inc(waits_passed, 1)

        def wait_read(eng, name, seq):
            if name in CONV:
                eng.wait_ge(conv_ready, at(seq, len(CONV), CONV.index(name)))
            elif name in ZT:
                eng.wait_ge(sz_ready, at(seq, len(ZT), ZT.index(name)))
            elif name in ("out0", "out1"):
                eng.wait_ge(x1_ready, 1 + at(seq, 2, int(name[3])))
            elif name in ("down0", "down1"):
                eng.wait_ge(yo_ready, 1 + at(seq, 2, int(name[4])))
            else:
                reader = {"dt": dt_read, "ssq": ssq_read, "router": lex_ready, "gate": gate_read,
                          "up": hs_ready, "sel": keys_ready}[name]
                eng.wait_ge(reader, at(seq, 1) + (reader in credited or name == "sel"))

        def slot_wait(pe, name, seq, hasA, hasC, before):
            order = [n for n, st in SLOTS if (st == "A" and hasA) or (st in "CD" and hasC)]
            behind = {n: {"A": -1, "C": 1, "D": 2}[st] for n, st in SLOTS}
            it = seq + behind[name]
            last = [n for n in order[:order.index(name)] if BANK[n] == BANK[name]][-1:]
            if not last:
                if before is None:
                    return
                it = it - 1
                stages = [[n for n, st in SLOTS if BANK[n] == BANK[name] and st in ("A", "CD")[c] and before[c]]
                          for c in range(2)]
                order = [n for n, _ in SLOTS]
                last = sorted((x[-1] for x in stages if x), key=order.index)
                if before[1] != "maybe" or last[-1] in A_SLOTS:
                    last = last[-1:]
            for n in last:
                wait_read(pe, n, it - behind[n])

        def schedule(eng, iteration):
            iteration(-1, 1, True, False, False, None)
            iteration(0, 0, True, True, False, (True, False))
            with eng.Fori(0, (NSEQ - 2) // 2) as pair:
                iteration(2 * pair + 1, 1, True, True, True, None)
                iteration(2 * pair + 2, 0, True, True, True, None)
            iteration(NSEQ - 1, 1, False, True, True, (True, True))
            iteration(NSEQ, 0, False, False, True, (False, True))

        def expert_schedule(eng, step):
            for i in range(WRING):
                step(i, i)
            with eng.Fori(1, ET // WRING - 1) as lot:
                for n in range(WRING):
                    step(WRING * lot + n, n)
            for i in range(ET - WRING, ET + 1):
                step(i, i % WRING)

        block = ctx.enter_context(nc.Block())

        @block.sync
        def _(sp):
            for semaphore in credited:
                sp.sem_inc(semaphore, 1)

            def load_x(s, par, reuse):
                src = x_t[s] if isinstance(s, int) else x_t[bass.ds(s, 1)].rearrange("s p j d -> p (s j) d")
                if reuse:
                    sp.wait_ge(xn_ready, at(s - 2, 1))
                sp.dma_start(xin[:, par], src).then_inc(x_loaded[par], 16)

            load_x(0, 0, False)
            for dst, src in ((win, w_in), (cw, conv_w), (cb, conv_b), (dtb, dt_bias), (abc, a_log),
                             (dsk, dskip), (wout, w_out), (gw, gate_w), (wsg, ws_gate), (wsu, ws_up),
                             (wsd, ws_down), (bias_b, bias)):
                sp.dma_start(dst[:], src).then_inc(w_loaded, 16)
            load_x(1, 1, False)
            sp.wait_ge(consts_ready, 1)
            sp.dma_start(rows[T:T + P, :], zrow[:]).then_inc(pad_stored, 16)
            sp.dma_start(out[T:T + P, :], zrow[:, 0:D]).then_inc(pad_stored, 16)

            def expert_weights(i, slot, reuse):
                if reuse:
                    sp.wait_ge(down_ready, i - WRING + 1)
                    idx = sp.snap(i)
                    g_src = w_gate[bass.ds(idx, 1)].rearrange("i p e k f -> p (i e) k f")
                    u_src = w_up[bass.ds(idx, 1)].rearrange("i p e k f -> p (i e) k f")
                    d_src = w_down[bass.ds(idx, 1)].rearrange("i f e d -> f (i e) d")
                else:
                    g_src, u_src, d_src = w_gate[i], w_up[i], w_down[i]
                sp.dma_start(wgu[:, slot, 0], g_src).then_inc(wx_loaded[slot], 16)
                sp.dma_start(wgu[:, slot, 1], u_src).then_inc(wx_loaded[slot], 16)
                sp.dma_start(wdr[:, slot], d_src).then_inc(wx_loaded[slot], 16)

            for i in range(WRING):
                expert_weights(i, i, False)

            def move_c(s, par):
                sp.wait_ge(xc_ready, at(s, len(CONV), 0))
                if not isinstance(s, int) or s >= 2:
                    sp.wait_ge(small_ready, at(s - 2, TILES, TILES - 1))
                sp.dma_start(ct0[:, par], xc[N:2 * N, par, 4, :]).then_inc(ct_moved, 16)

            def load_residual(s):
                if not isinstance(s, int) or s >= 1:
                    sp.wait_ge(x1_ready, 1 + at(s - 1, 2, 1))
                src = x_t[s] if isinstance(s, int) else x_t[bass.ds(s, 1)].rearrange("s p j d -> p (s j) d")
                sp.dma_start(xres[:], src).then_inc(xres_loaded, 16)

            def store_c(s):
                if isinstance(s, int):
                    r_dst, y_dst = rows_t[s], out_t[s]
                else:
                    r_dst = rows_t[bass.ds(s, 1)].rearrange("s p j d -> p (s j) d")
                    y_dst = out_t[bass.ds(s, 1)].rearrange("s p j d -> p (s j) d")
                sp.wait_ge(rw_ready, at(s, 1))
                sp.dma_start(r_dst, xr[:]).then_inc(rows_stored, 16)
                sp.wait_ge(yo_ready, 1 + at(s, 2, 1))
                sp.dma_start(y_dst, yo[:]).then_inc(y_stored, 16)

            def iteration(it, par, hasA, hasB, hasC, before, more):
                if hasC:
                    load_residual(it - 1)
                if hasA:
                    move_c(it + 1, 1 - par)
                if more:
                    load_x(it + 2, par, True)
                if hasC:
                    store_c(it - 1)

            iteration(-1, 1, True, False, False, None, False)
            iteration(0, 0, True, True, False, None, True)
            with sp.Fori(0, (NSEQ - 4) // 2) as pair:
                iteration(2 * pair + 1, 1, True, True, True, None, True)
                iteration(2 * pair + 2, 0, True, True, True, None, True)
            iteration(NSEQ - 3, 1, True, True, True, None, True)
            iteration(NSEQ - 2, 0, True, True, True, None, False)
            iteration(NSEQ - 1, 1, False, True, True, None, False)
            iteration(NSEQ, 0, False, False, True, None, False)
            with sp.Fori(1, ET // WRING) as lot:
                for n in range(WRING):
                    expert_weights(WRING * lot + n, n, True)
            sp.wait_ge(scattered, 16 * ET)
            sp.wait_ge(rows_stored, 1 + 16 * NSEQ)
            sp.wait_ge(y_stored, 1 + 16 * NSEQ)
            sp.wait_ge(pad_stored, 32)

        @block.tensor
        def _(pe):
            mm, tr = nc.tensor.matmul, nc.tensor.transpose

            def front(s, par, j):
                b = j % 2
                tile = slice(j * P, (j + 1) * P)
                if j == 0:
                    pe.wait_ge(xc_ready, at(s, len(CONV), len(CONV) - 1))
                    pe.wait_ge(dt_ready, at(s, 1))
                    pe.wait_ge(ct_moved, 16 * (s + 1))
                    if not isinstance(s, int) or s > 0:
                        pe.wait_ge(xd_ready, at(s - 1, TILES, TILES - 1))
                        pe.wait_ge(ex_ready, at(s - 1, TILES, TILES - 1))
                        pe.wait_ge(cb_ready, at(s - 1, TILES, TILES - 1))
                else:
                    pe.wait_ge(xd_ready, at(s, TILES, j - 1))
                    pe.wait_ge(ex_ready, at(s, TILES, j - 1))
                    pe.wait_ge(cb_ready, at(s, TILES, j - 1))
                for h in range(H):
                    last = tr(bXT[:, h * HD:(h + 1) * HD], xc[:, par, h, tile], ident[:])
                last.then_inc(xt_ready, 1)
                pe.wait_ge(datri_ready, at(s, TILES, j))
                mm(bSEG[:], strict[:], datri[:, b].rearrange("p h q -> p (h q)"),
                   start=True, stop=True).then_inc(seg_ready, 1)
                mm(bSM[:, 0:P], xc[0:N, par, 4, tile], ct0[:, par, tile], start=True, stop=True)
                tr(bSM[:, P:2 * P], xc[:, par, 4, tile], ident[:])
                dcol = dA[:, par, j * H:(j + 1) * H]
                last = mm(bSM[:, 2 * P:2 * P + H], tri[:], dcol, start=True, stop=True)
                for hl in range(2):
                    last = mm(bSM[hl * N:(hl + 1) * N, 2 * P + H:2 * P + H + 2], ones[:, 0:N],
                              dcol.rearrange("p (a b) -> p a b", b=2)[:, :, hl], start=True, stop=True)
                last.then_inc(small_ready, 1)

            def turn_c(s, j):
                pe.wait_ge(cs_ready, at(s, TILES - 1, j - 1))
                pe.wait_ge(s_ready, at(s, TILES - 1, j - 1))
                c2 = cs[:, j % 2].rearrange("p (a h) n -> p a (h n)", a=2)
                for a in range(2):
                    last = tr(bCS[:, a * P:(a + 1) * P], c2[:, a], ident[:])
                last.then_inc(cst_ready, 1)

            def back(s, par, j):
                b = j % 2
                pe.wait_ge(xd_ready, at(s, TILES, j))
                if j < TILES - 1:
                    pe.wait_ge(bd_ready, at(s, TILES - 1, j))
                    if j == 0:
                        if not isinstance(s, int) or s > 0:
                            pe.wait_ge(cst_copied, at(s - 1, TILES - 1, TILES - 2))
                    else:
                        pe.wait_ge(cst_copied, at(s, TILES - 1, j - 1))
                    for h in range(H):
                        a, hl = divmod(h, 2)
                        last = mm(bCS[hl * N:(hl + 1) * N, 2 * P + a * HD:2 * P + (a + 1) * HD], bd[:, b, h],
                                  xd[:, b, h], start=True, stop=True)
                    last.then_inc(ds_ready, 1)
                if j > 0:
                    pe.wait_ge(g_ready, at(s, TILES, j - 1))
                elif not isinstance(s, int) or s > 0:
                    pe.wait_ge(g_ready, at(s - 1, TILES, TILES - 1))
                tile = slice(j * P, (j + 1) * P)
                pe.wait_ge(w_ready, at(s, TILES, j))
                if j > 0:
                    pe.wait_ge(cst_copied, at(s, TILES - 1, j - 1))
                for h in range(H):
                    a, hl = divmod(h, 2)
                    mm(bY[:, h * P:(h + 1) * P], dskip_diag[:, h], xc[:, par, h, tile], start=True, stop=False)
                    last = mm(bY[:, h * P:(h + 1) * P], xd[:, b, h], Wt[:, b, h], start=False, stop=(j == 0))
                    if j > 0:
                        last = mm(bY[:, h * P:(h + 1) * P], S[:, b, a], csT[:, b, h], start=False, stop=True)
                last.then_inc(y_ready, 1)

            def turn_in(s, k, prev):
                if k == 0:
                    pe.wait_ge(xn_ready, at(s, 1))
                    for read in prev:
                        pe.wait_ge(*read)
                else:
                    pe.wait_ge(trA_copied, at(s, KD, k - 1))
                for j in range(TILES):
                    last = tr(bTR[:, j * P:(j + 1) * P], xn[:, j, k * P:(k + 1) * P], ident[:])
                last.then_inc(trA_ready, 1)

            def turn_mid(s, k, prev):
                if k == 0:
                    pe.wait_ge(x2_ready, at(s, 1))
                    pe.wait_ge(*prev)
                else:
                    pe.wait_ge(trC_copied, 1 + at(s, KD, k - 1))
                for j in range(TILES):
                    last = tr(bTR[:, j * P:(j + 1) * P], xr[:, j, k:D:KD], ident[:])
                last.then_inc(trC_ready, 1)

            def project(s, name):
                dst = bR[BANK[name]]
                if name == "m8":
                    pe.wait_ge(trA_copied, at(s, KD, KD - 1))
                    if isinstance(s, int) and s == 0:
                        pe.wait_ge(w_loaded, 16 * 12)
                        pe.wait_ge(consts_ready, 2)
                        pe.wait_ge(skip_made, 1)
                if name == "dt":
                    for j in range(TILES):
                        for k in range(KD):
                            last = mm(dst[:, j * H:(j + 1) * H], xnT[:, k, j * P:(j + 1) * P],
                                      win[:, k, PROJ:PROJ + H], start=(k == 0), stop=(k == KD - 1))
                else:
                    m = int(name[1])
                    for k in range(KD):
                        last = mm(dst[:], win[:, k, m * P:(m + 1) * P], xnT[:, k, :],
                                  start=(k == 0), stop=(k == KD - 1))
                last.then_inc(projA_ready, 1)

            def finish(s, par, name):
                dst = bR[BANK[name]]
                if name == "ssq":
                    pe.wait_ge(ss_ready, at(s, TILES, TILES - 1))
                    for j in range(TILES):
                        last = mm(dst[:, j:j + 1], ss[:, par, j * P:(j + 1) * P], ones[:, 0:1], start=True, stop=True)
                elif name in ("out0", "out1"):
                    pe.wait_ge(g_ready, at(s, TILES, TILES - 1))
                    for half in range(2):
                        j = 2 * int(name[3]) + half
                        for h in range(H):
                            last = mm(dst[:, half * D:(half + 1) * D], g[:, par, h, j * P:(j + 1) * P],
                                      wout[:, h], start=(h == 0), stop=(h == H - 1))
                elif name == "router":
                    pe.wait_ge(trC_copied, 1 + at(s, KD, KD - 1))
                    for j in range(TILES):
                        for k in range(KD):
                            last = mm(dst[:, j * E:(j + 1) * E], x2T[:, k, j * P:(j + 1) * P], gw[:, k],
                                      start=(k == 0), stop=(k == KD - 1))
                elif name in ("gate", "up"):
                    w = wsg if name == "gate" else wsu
                    for k in range(KD):
                        last = mm(dst[0:F, :], w[:, k], x2T[:, k], start=(k == 0), stop=(k == KD - 1))
                elif name in ("down0", "down1"):
                    pe.wait_ge(hs_ready, 1 + at(s, 1))
                    for half in range(2):
                        j = 2 * int(name[4]) + half
                        last = mm(dst[:, half * D:(half + 1) * D], hs[:, j * P:(j + 1) * P], wsd[:],
                                  start=True, stop=True)
                last.then_inc(projC_ready, 1)

            def turn_choices(s):
                pe.wait_ge(sel_ready, 1 + at(s, 1))
                apart(pe)
                for j in range(TILES):
                    last = tr(bR[BANK["sel"]][0:E, j * P:(j + 1) * P], sel[:, j], ident[:])
                last.then_inc(selt_ready, 1)

            pe.wait_ge(consts_ready, 1)

            def iteration(it, par, hasA, hasB, hasC, before):
                in_loop = before is None and not isinstance(it, int)
                prior = (True, True) if in_loop else before
                if in_loop and par == 1:
                    prior = (True, "maybe")

                def fill(*names):
                    for name in names:
                        if name == "LN1a":
                            if hasA:
                                prev = []
                                if not isinstance(it, int) or it == 0:
                                    prev.append((trA_copied, at(it, KD, KD - 1)))
                                if not isinstance(it, int):
                                    prev.append((trC_copied, 1 + at(it - 2, KD, KD - 1)))
                                turn_in(it + 1, 0, prev)
                        elif name == "LN1b":
                            if hasA:
                                turn_in(it + 1, 1, [])
                        elif name == "LN2a":
                            if hasC:
                                turn_mid(it - 1, 0, (trA_copied, at(it + 1, KD, KD - 1)) if hasA else
                                         (trC_copied, 1 + at(it - 2, KD, KD - 1)))
                        elif name == "LN2b":
                            if hasC:
                                turn_mid(it - 1, 1, None)
                        elif name in A_SLOTS:
                            if hasA:
                                slot_wait(pe, name, it + 1, hasA, hasC, prior)
                                project(it + 1, name)
                        elif name == "sel":
                            if hasC:
                                slot_wait(pe, name, it - 2, hasA, hasC, prior)
                                turn_choices(it - 2)
                        elif hasC:
                            slot_wait(pe, name, it - 1, hasA, hasC, prior)
                            finish(it - 1, 1 - par, name)

                if hasB:
                    front(it, par, 0)
                fill("ssq", "sel", "out0", "out1", "LN1a")
                if hasB:
                    back(it, par, 0)
                fill("LN1b")
                if hasB:
                    front(it, par, 1)
                fill("m8", "dt")
                if hasB:
                    turn_c(it, 1)
                fill("m4", "LN2a")
                if hasB:
                    back(it, par, 1)
                fill("LN2b")
                if hasB:
                    front(it, par, 2)
                fill("router", "m5")
                if hasB:
                    turn_c(it, 2)
                fill("m6")
                if hasB:
                    back(it, par, 2)
                    front(it, par, 3)
                fill("gate", "up")
                if hasB:
                    turn_c(it, 3)
                fill("m7", "m0")
                if hasB:
                    back(it, par, 3)
                fill("m1", "down0", "down1", "m2", "m3")

            schedule(pe, iteration)

            turn_choices(NSEQ - 1)
            pe.wait_ge(ktok_ready, 1)
            tr(bTR[0:CAP, 0:E], ktok[E:P], ident[E:P, E:P]).then_inc(tokt_ready, 1)
            pe.wait_ge(idx_ready, 1)

            def turn_tokens(i, n):
                pe.wait_ge(gathered[n], 16 * (i // WRING + 1) if isinstance(i, int) else (i - n) * 4 + 16)
                if not isinstance(i, int) or i > 0:
                    pe.wait_ge(xgt_copied, i)
                for k in range(KD):
                    last = tr(bXT[:, k * P:(k + 1) * P], xg[:, n, k:D:KD], ident[:])
                last.then_inc(xgt_ready, 1)

            def gate_up(i, n):
                pe.wait_ge(xgt_copied, i + 1)
                pe.wait_ge(wx_loaded[n], 48 * (i // WRING + 1) if isinstance(i, int) else (i - n) * 12 + 48)
                if not isinstance(i, int) or i > 1:
                    pe.wait_ge(ehs_ready, i - 1)
                for e in range(2):
                    for k in range(KD):
                        last = mm(bGU[n % 2][e * 64:(e + 1) * 64, 0:2 * F], xgT[:, n % 2, k, e * 64:(e + 1) * 64],
                                  wgu[:, n, :, e, k], start=(k == 0), stop=(k == KD - 1))
                last.then_inc(gu_ready, 1)

            def token_rows(i, n):
                pe.wait_ge(tokc_ready, i + 1)
                if not isinstance(i, int) or i > 0:
                    pe.wait_ge(eq_ready, i)
                mm(bSM[:, 0:P], tokc[:, n % 2].to_broadcast([P, P]), ident[:], start=True, stop=True
                   ).then_inc(rowb_ready, 1)

            def sum_tokens(i, n):
                pe.wait_ge(ehs_ready, i + 1)
                pe.wait_ge(eq_ready, i + 1)
                if not isinstance(i, int) or i > 0:
                    pe.wait_ge(hsum_copied, i)
                for e in range(2):
                    r = slice(e * 64, (e + 1) * 64)
                    last = mm(bR[e][0:F, 0:P], ehs[r, n % 2], eq[r, n % 2], start=True, stop=True)
                last.then_inc(hsum_ready, 1)

            def down(i, n):
                pe.wait_ge(hsum_copied, i + 1)
                if not isinstance(i, int) or i > 0:
                    pe.wait_ge(oc_ready, i)
                for e in range(2):
                    last = mm(bY[:, 0:D], hsum[:, n % 2, e], wdr[:, n, e], start=(e == 0), stop=(e == 1))
                last.then_inc(down_ready, 1)

            def expert_step(i, n):
                if not isinstance(i, int) or i + 1 < ET:
                    token_rows(i + 1, (n + 1) % WRING)
                    turn_tokens(i + 1, (n + 1) % WRING)
                if not isinstance(i, int) or 1 <= i:
                    sum_tokens(i - 1, (n - 1) % WRING)
                if not isinstance(i, int) or i < ET:
                    gate_up(i, n)
                if not isinstance(i, int) or 1 <= i:
                    down(i - 1, (n - 1) % WRING)

            token_rows(0, 0)
            turn_tokens(0, 0)
            expert_schedule(pe, expert_step)

        @block.scalar
        def _(act):
            fn = nc.scalar.activation

            def some(s):
                return not isinstance(s, int)

            def normalise(src, dst, centre_, mean_ready, root_, root_ready, s, step):
                act.wait_ge(mean_ready, at(s, 1))
                for j in range(TILES):
                    last = fn(dst[:, j, 0:D], src[:, j], ACT.Identity, bias=centre_[:, j:j + 1])
                last.then_inc(step, 1)
                act.wait_ge(step, at(s, 1))
                act.wait_ge(root_ready, at(s, 1))
                for j in range(TILES):
                    last = fn(dst[:, j, 0:D], dst[:, j, 0:D], ACT.Copy, scale=root_[:, j:j + 1])
                return last

            def ln1_out(s, par):
                if some(s) or s > 0:
                    act.wait_ge(trA_ready, at(s - 1, KD, KD - 1))
                normalise(xin[:, par], xn, centre, ln1_var, nw, ln1_root, s, xn_centred).then_inc(xn_ready, 1)

            def copy_in(s, k):
                act.wait_ge(trA_ready, at(s, KD, k))
                fn(xnT[:, k], bTR[:], ACT.Copy).then_inc(trA_copied, 1)

            def copy_mid(s, k):
                act.wait_ge(trC_ready, at(s, KD, k))
                fn(x2T[:, k], bTR[:], ACT.Copy).then_inc(trC_copied, 1)

            def tap(s, n):
                c = 4 if n == 0 else n - 1
                act.wait_ge(projA_ready, at(s, len(A_SLOTS), A_SLOTS.index(CONV[n])))
                if n >= 2:
                    act.wait_ge(xc_ready, at(s, 5, n - 2))
                elif some(s) or s > 0:
                    act.wait_ge(xc_ready, at(s - 1, 5, n + 3))
                fn(acc[:, n % 2], bR[BANK[CONV[n]]][:], ACT.Identity, bias=cb[:, c:c + 1],
                   scale=cw[:, c, 3:4]).then_inc(tap_ready, 1)

            def conv_tanh(s, n):
                act.wait_ge(conv_ready, at(s, 5, n))
                fn(cth[:, n % 2], acc[:, n % 2], ACT.Tanh, scale=0.5).then_inc(cth_step, 1)
                act.wait_ge(cth_step, at(s, 5, n))
                fn(cth[:, n % 2], cth[:, n % 2], ACT.Copy, bias=1.0).then_inc(cth_ready, 1)

            def z_tanh(s, n):
                act.wait_ge(projA_ready, at(s, len(A_SLOTS), A_SLOTS.index(ZT[n])))
                if n >= 2:
                    act.wait_ge(sz_ready, at(s, 4, n - 2))
                elif some(s) or s > 0:
                    act.wait_ge(sz_ready, at(s - 1, 4, n + 2))
                fn(zth[:, n % 2], bR[BANK[ZT[n]]][:], ACT.Tanh, scale=0.5).then_inc(zth_ready, 1)

            def dt_exp(s):
                act.wait_ge(dtabs_ready, at(s, 1))
                fn(dtv[:, 2], dtv[:, 1], ACT.Exp).then_inc(dte_ready, 1)

            def seg_exp(s, j):
                b = j % 2
                act.wait_ge(seg_ready, at(s, TILES, j))
                if j >= 2:
                    act.wait_ge(w_ready, at(s, TILES, j - 2))
                    act.wait_ge(bd_ready, at(s, 3, j - 2))
                elif some(s) or s > 0:
                    act.wait_ge(w_ready, at(s - 1, TILES, j + 2))
                    act.wait_ge(bd_ready, at(s - 1, 3, min(j + 2, 2)))
                fn(Ex[:, b].rearrange("p h q -> p (h q)"), bSEG[:], ACT.Exp).then_inc(ex_ready, 1)
                act.wait_ge(cb_ready, at(s, TILES, j))
                if j >= 2:
                    act.wait_ge(s_ready, at(s, 3, j - 2))
                    if j == 3:
                        act.wait_ge(cs_ready, at(s, 3, 0))
                elif some(s) or s > 0:
                    act.wait_ge(s_ready, at(s - 1, 3, 2))
                    act.wait_ge(cs_ready, at(s - 1, 3, 2 if j == 1 else 1))
                fn(ec[:, b], sm[:, b, P:P + 6], ACT.Exp).then_inc(ec_ready, 1)

            def copy_c(s, j):
                act.wait_ge(cst_ready, at(s, 3, j - 1))
                if j >= 3:
                    act.wait_ge(y_ready, at(s, TILES, j - 2))
                elif some(s) or s > 0:
                    act.wait_ge(y_ready, at(s - 1, TILES, TILES - 1))
                for hl in range(2):
                    r = slice(hl * N, (hl + 1) * N)
                    last = fn(csT[r, j % 2].rearrange("p (a h) q -> p a h q", h=2)[:, :, hl],
                              bCS[r, 0:2 * P].rearrange("p (a q) -> p a q", a=2), ACT.Copy)
                last.then_inc(cst_copied, 1)

            def scale_x(s, par, j):
                act.wait_ge(xt_ready, at(s, TILES, j))
                if j == 0:
                    act.wait_ge(dt_ready, at(s, 1))
                if j >= 2:
                    act.wait_ge(y_ready, at(s, TILES, j - 2))
                elif some(s) or s > 0:
                    act.wait_ge(y_ready, at(s - 1, TILES, j + 2))
                for h in range(H):
                    last = fn(xd[:, j % 2, h], bXT[:, h * HD:(h + 1) * HD], ACT.Copy,
                              scale=dth[:, par, j * H + h:j * H + h + 1])
                last.then_inc(xd_ready, 1)

            def square(s, j):
                act.wait_ge(y_ready, at(s, TILES, j))
                if j >= 2:
                    act.wait_ge(ss_ready, at(s, TILES, j - 2))
                elif some(s) or s > 0:
                    act.wait_ge(ss_ready, at(s - 1, TILES, j + 2))
                fn(sq[:, j % 2].rearrange("p h q -> p (h q)"), bY[:], ACT.Square).then_inc(sq_ready, 1)

            def router_exp(s):
                act.wait_ge(projC_ready, 1 + at(s, len(C_SLOTS), C_SLOTS.index("router")))
                if some(s) or s > 0:
                    act.wait_ge(sel_ready, 1 + at(s - 1, 1))
                fn(lex[:].rearrange("p j e -> p (j e)"), bR[BANK["router"]][:, 0:TILES * E], ACT.Exp,
                   scale=-1.0).then_inc(lex_ready, 1)

            def gate_tanh(s):
                act.wait_ge(projC_ready, 1 + at(s, len(C_SLOTS), C_SLOTS.index("gate")))
                if some(s) or s > 0:
                    act.wait_ge(hs_ready, 1 + at(s - 1, 1))
                fn(gth[:], bR[BANK["gate"]][0:F, :], ACT.Tanh, scale=0.5).then_inc(gth_ready, 1)

            def iteration(it, par, hasA, hasB, hasC, before):
                a, c = it + 1, it - 1
                if hasB:
                    scale_x(it, par, 0)
                    seg_exp(it, 0)
                if hasA:
                    ln1_out(a, 1 - par)
                if isinstance(it, int) and it == -1:
                    act.wait_ge(w_loaded, 16 * 12)
                    fn(abc[:], abc[:], ACT.Exp).then_inc(abc_exp, 1)
                if hasA:
                    copy_in(a, 0)
                    copy_in(a, 1)
                if isinstance(it, int) and it == -1:
                    act.wait_ge(consts_ready, 2)
                if hasB:
                    square(it, 0)
                    scale_x(it, par, 1)
                    seg_exp(it, 1)
                if hasA:
                    tap(a, 0)
                    dt_exp(a)
                if hasB:
                    copy_c(it, 1)
                if hasA:
                    conv_tanh(a, 0)
                if hasA:
                    tap(a, 1)
                if hasC:
                    copy_mid(c, 0)
                if hasB:
                    square(it, 1)
                if hasC:
                    copy_mid(c, 1)
                if hasB:
                    scale_x(it, par, 2)
                    seg_exp(it, 2)
                if hasA:
                    conv_tanh(a, 1)
                if hasC:
                    router_exp(c)
                if hasA:
                    tap(a, 2)
                if hasB:
                    copy_c(it, 2)
                if hasA:
                    tap(a, 3)
                    conv_tanh(a, 2)
                if hasB:
                    square(it, 2)
                    scale_x(it, par, 3)
                    seg_exp(it, 3)
                if hasC:
                    gate_tanh(c)
                if hasB:
                    copy_c(it, 3)
                if hasA:
                    conv_tanh(a, 3)
                    tap(a, 4)
                    z_tanh(a, 0)
                if hasB:
                    square(it, 3)
                if hasA:
                    conv_tanh(a, 4)
                    z_tanh(a, 1)
                    z_tanh(a, 2)
                    z_tanh(a, 3)

            schedule(act, iteration)

            def copy_tokens(i, n):
                act.wait_ge(xgt_ready, i + 1)
                if not isinstance(i, int) or i >= 2:
                    act.wait_ge(gu_ready, i - 1)
                fn(xgT[:, n % 2].rearrange("p k q -> p (k q)"), bXT[:, 0:KD * P], ACT.Copy).then_inc(xgt_copied, 1)

            def expert_step(i, n):
                if not isinstance(i, int) or i + 1 < ET:
                    copy_tokens(i + 1, (n + 1) % WRING)
                if not isinstance(i, int) or i >= 1:
                    act.wait_ge(hsum_ready, i)
                    if not isinstance(i, int) or i >= 3:
                        act.wait_ge(down_ready, i - 2)
                    for e in range(2):
                        last = fn(hsum[:, (n - 1) % 2, e], bR[e][0:F, 0:P], ACT.Copy)
                    last.then_inc(hsum_copied, 1)
                if not isinstance(i, int) or i < ET:
                    act.wait_ge(gu_ready, i + 1)
                    if not isinstance(i, int) or i >= 2:
                        act.wait_ge(ehs_ready, i - 1)
                    fn(eth[:, n % 2], bGU[n % 2][:, 0:F], ACT.Tanh, scale=0.5).then_inc(eth_ready, 1)
                if not isinstance(i, int) or i >= 1:
                    act.wait_ge(down_ready, i)
                    if not isinstance(i, int) or i >= 3:
                        act.wait_ge(scattered, 16 * (i - 2))
                    fn(oc[:, (n - 1) % 2], bY[:, 0:D], ACT.Copy).then_inc(oc_ready, 1)

            copy_tokens(0, 0)
            expert_schedule(act, expert_step)

        @block.gpsimd
        def _(pool):
            tt = nc.gpsimd.tensor_tensor

            def some(s):
                return not isinstance(s, int)

            nconst = [0]

            def const(ins):
                ins.then_inc(pool_const, 1)
                nconst[0] += 1
                pool.wait_ge(pool_const, nconst[0])

            const(nc.gpsimd.memset(ones[:], 1.0))
            sel_of = nc.gpsimd.affine_select
            const(sel_of(ident[:], ones[:], [[1, P]], ALU.is_equal, 0.0, base=0, channel_multiplier=-1))
            const(nc.gpsimd.memset(exponent[:], -0.5))
            nc.gpsimd.memset(zrow[:], 0.0).then_inc(consts_ready, 1)

            def later_constants():
                const(sel_of(tri[:], ones[:], [[1, P]], ALU.is_ge, 0.0, base=0, channel_multiplier=-1))
                const(sel_of(strict[:], ones[:], [[-1, P]], ALU.is_gt, 0.0, base=0, channel_multiplier=1))
                const(nc.gpsimd.iota(rank_i, [[-1, L]], base=L, channel_multiplier=0))
                const(nc.gpsimd.tensor_copy(rank_rev[:], rank_i))
                const(nc.gpsimd.iota(spare_i[:], [[0, 1]], base=T, channel_multiplier=1))
                const(nc.gpsimd.tensor_copy(spare[:], spare_i[:]))
                const(nc.gpsimd.memset(csT[:], 0.0))
                const(nc.gpsimd.memset(keys[:], 0.0))
                const(nc.gpsimd.memset(sel[:], 0.0))
                nc.gpsimd.memset(gsx[:], -BIG).then_inc(consts_ready, 1)
                pool.wait_ge(abc_ready, 2)
                tt(dskip_diag[:], ident[:].rearrange("p (o q) -> p o q", o=1).to_broadcast([P, H, P]),
                   dsk[:].rearrange("p (h o) -> p h o", o=1).to_broadcast([P, H, P]), ALU.mult).then_inc(skip_made, 1)

            def decay_in(s, par, j):
                b = j % 2
                if j == 0:
                    pool.wait_ge(dt_ready, at(s, 1))
                if j >= 2:
                    pool.wait_ge(seg_ready, at(s, TILES, j - 2))
                elif some(s) or s > 0:
                    pool.wait_ge(seg_ready, at(s - 1, TILES, j + 2))
                tt(datri[:, b], tri[:].rearrange("p (o q) -> p o q", o=1).to_broadcast([P, H, P]),
                   dA[:, par, j * H:(j + 1) * H].rearrange("p (h o) -> p h o", o=1).to_broadcast([P, H, P]),
                   ALU.mult).then_inc(datri_ready, 1)

            def weigh(s, j):
                b = j % 2
                pool.wait_ge(ex_ready, at(s, TILES, j))
                pool.wait_ge(cb_ready, at(s, TILES, j))
                if j >= 2:
                    pool.wait_ge(y_ready, at(s, TILES, j - 2))
                elif some(s) or s > 0:
                    pool.wait_ge(y_ready, at(s - 1, TILES, j + 2))
                tt(Wt[:, b], Ex[:, b], cbm[:, b].rearrange("p (o q) -> p o q", o=1).to_broadcast([P, H, P]),
                   ALU.mult).then_inc(w_ready, 1)

            def conv_silu(s, par, n):
                c = 4 if n == 0 else n - 1
                pool.wait_ge(cth_ready, at(s, 5, n))
                if n == 0 and (some(s) or s >= 2):
                    pool.wait_ge(y_ready, at(s - 2, TILES, TILES - 1))
                    pool.wait_ge(ct_moved, 16 * (s - 1))
                tt(xc[:, par, c], cth[:, n % 2], acc[:, n % 2], ALU.mult).then_inc(xc_ready, 1)

            def sum_squares(s, par, j):
                b = j % 2
                pool.wait_ge(sq_ready, at(s, TILES, j))
                if j == 0 and (some(s) or s >= 2):
                    pool.wait_ge(projC_ready, 1 + at(s - 2, len(C_SLOTS), len(C_SLOTS) - 1))
                tt(sqh[:, b], sq[:, b, 0:2], sq[:, b, 2:4], ALU.add).then_inc(sqh_step, 1)
                pool.wait_ge(sqh_step, at(s, TILES, j))
                tt(ss[:, par, j * P:(j + 1) * P], sqh[:, b, 0], sqh[:, b, 1], ALU.add).then_inc(ss_ready, 1)

            def root(s, y, val, given, made):
                pool.wait_ge(given, at(s, 1))
                tt(y[:], val[:], exponent[:], ALU.pow).then_inc(made, 1)

            def iteration(it, par, hasA, hasB, hasC, before):
                a, ap = it + 1, 1 - par
                if hasB:
                    decay_in(it, par, 0)
                    decay_in(it, par, 1)
                if hasA:
                    root(a, nw, ve, ln1_var, ln1_root)
                if isinstance(it, int) and it == -1:
                    later_constants()
                if hasC:
                    root(it - 1, rms, ms, ssq_read, rms_root)
                if hasB:
                    weigh(it, 0)
                    sum_squares(it, par, 0)
                if hasC:
                    root(it - 1, nwc, vec, ln2_var, ln2_root)
                if hasB:
                    decay_in(it, par, 2)
                    weigh(it, 1)
                if hasA:
                    conv_silu(a, ap, 0)
                if hasB:
                    sum_squares(it, par, 1)
                    decay_in(it, par, 3)
                    weigh(it, 2)
                if hasA:
                    conv_silu(a, ap, 1)
                    conv_silu(a, ap, 2)
                if hasB:
                    sum_squares(it, par, 2)
                    weigh(it, 3)
                if hasA:
                    conv_silu(a, ap, 3)
                if hasB:
                    sum_squares(it, par, 3)
                if hasA:
                    conv_silu(a, ap, 4)

            schedule(pool, iteration)

            pool.wait_ge(idx_ready, 1)
            pool.wait_ge(rows_stored, 1 + 16 * NSEQ)
            pool.wait_ge(y_stored, 1 + 16 * NSEQ)
            pool.wait_ge(pad_stored, 32)

            def gather(i, n):
                if some(i) or i >= WRING:
                    pool.wait_ge(xgt_ready, i - WRING + 1)
                    pool.wait_ge(wcol_ready, i - WRING + 1)
                nc.gpsimd.tensor_copy(idxc[:, n], idxT[:, bass.ds(i, 1)]).then_inc(idxc_ready, 1)
                pool.wait_ge(idxc_ready, i + 1)
                apart(pool)
                nc.gpsimd.indirect_dma_start(out=xg[:, n], out_offset=None, in_=rows[:, :],
                                             in_offset=bass.IndirectOffsetOnAxis(ap=idxc[:, n], axis=0)
                                             ).then_inc(gathered[n], 16)

            def scatter(i, n):
                pool.wait_ge(oc_ready, i + 1)
                pool.wait_ge(sidx_ready, i + 1)
                if some(i) or i > 0:
                    pool.wait_ge(scattered, 16 * i)
                apart(pool)
                nc.gpsimd.indirect_dma_start(out=out[:, :], out_offset=bass.IndirectOffsetOnAxis(ap=sidxi[:, n], axis=0),
                                             in_=oc[:, n % 2], in_offset=None, compute_op=ALU.add
                                             ).then_inc(scattered, 16)

            def expert_step(i, n):
                if some(i) or i + 3 < ET:
                    gather(i + 3, (n + 3) % WRING)
                if some(i) or i >= 1:
                    scatter(i - 1, (n - 1) % WRING)

            for n in range(3):
                gather(n, n)
            expert_schedule(pool, expert_step)

        @block.vector
        def _(dve):
            v = nc.vector
            tt, ts, stt, cp = v.tensor_tensor, v.tensor_scalar, v.scalar_tensor_tensor, v.tensor_copy

            def some(s):
                return not isinstance(s, int)

            def statistics(src, st, m, summed, aggregated, centre, var, var_ready, s):
                for j in range(TILES):
                    last = v.bn_stats(st[:, j], src[:, j])
                last.then_inc(summed, 1)
                dve.wait_ge(summed, at(s, 1))
                apart(dve)
                for j in range(TILES):
                    last = v.bn_aggr(m[:, j], st[:, j])
                last.then_inc(aggregated, 1)
                dve.wait_ge(aggregated, at(s, 1))
                ts(centre[:], m[:, :, 0], -1.0, None, ALU.mult)
                ts(var[:], m[:, :, 1], LN_EPS, None, ALU.add).then_inc(var_ready, 1)

            def normalise(src, dst, m, y):
                for j in range(TILES):
                    last = ts(dst[:, j, 0:D], src[:, j], m[:, j, 0:1], y[:, j:j + 1], ALU.subtract, ALU.mult)
                return last

            def ln1_in(s, par):
                dve.wait_ge(x_loaded[par], (s // 2 + 1) * 16 if isinstance(s, int) else (s - par) * 8 + 16)
                if some(s) or s > 0:
                    dve.wait_ge(xn_ready, at(s - 1, 1))
                statistics(xin[:, par], st6, mv, ln1_sums, ln1_mean, centre, ve, ln1_var, s)

            def dt_stage(s, par):
                c = Chain(dve, dt_step, s, DT_CHAIN)
                q = lambda n: dtv[:, n]
                raw = bR[BANK["dt"]][:, 0:TILES * H].rearrange("p (j h) -> p j h", h=H)
                dve.wait_ge(projA_ready, at(s, len(A_SLOTS), A_SLOTS.index("dt")))
                if some(s) or s > 0:
                    dve.wait_ge(dt_ready, at(s - 1, 1))
                tt(dtv[:, 0].rearrange("p (j h) -> p j h", h=H), raw,
                   dtb[:].rearrange("p (o h) -> p o h", o=1).to_broadcast([P, TILES, H]),
                   ALU.add).then_inc(dt_read, 1)
                dve.wait_ge(dt_read, at(s, 1))
                stt(q(1), q(0), -1.0, q(0), ALU.mult, ALU.min).then_inc(dtabs_ready, 1)
                dve.wait_ge(dte_ready, at(s, 1))
                link = c.link
                link(ts(q(3), q(2), 2.0, None, ALU.add))
                link(v.reciprocal(q(4), q(3)))
                link(tt(q(3), q(2), q(4), ALU.mult))
                link(tt(q(4), q(3), q(3), ALU.mult))
                link(ts(q(5), q(4), 1.0 / 17, None, ALU.mult))
                for k in (15, 13, 11, 9, 7, 5, 3):
                    link(stt(q(5), q(5), 1.0 / k, q(4), ALU.add, ALU.mult))
                link(stt(q(5), q(5), 1.0, q(3), ALU.add, ALU.mult))
                link(ts(q(6), q(0), 0.0, None, ALU.max))
                if some(s) or s >= 2:
                    dve.wait_ge(datri_ready, at(s - 2, TILES, TILES - 1))
                    dve.wait_ge(small_ready, at(s - 2, TILES, TILES - 1))
                    dve.wait_ge(xd_ready, at(s - 2, TILES, TILES - 1))
                link(stt(q(7), q(5), 2.0, q(6), ALU.mult, ALU.add))
                link(ts(dth[:, par], q(7), 0.5, None, ALU.mult))
                tt(dA[:, par].rearrange("p (j h) -> p j h", h=H), q(7).rearrange("p (j h) -> p j h", h=H),
                   abc[:].rearrange("p (o h) -> p o h", o=1).to_broadcast([P, TILES, H]),
                   ALU.mult).then_inc(dt_ready, 1)
                c.done()

            def conv(s, n):
                c = 4 if n == 0 else n - 1
                src = bR[BANK[CONV[n]]]
                dve.wait_ge(tap_ready, at(s, 5, n))
                a = acc[:, n % 2]
                for k in (1, 2):
                    stt(a[:, k:L], src[:, 0:L - k], cw[:, c, 3 - k:4 - k], a[:, k:L], ALU.mult, ALU.add
                        ).then_inc(conv_step, 1)
                    dve.wait_ge(conv_step, at(s, 10, 2 * n + k - 1))
                stt(a[:, 3:L], src[:, 0:L - 3], cw[:, c, 0:1], a[:, 3:L], ALU.mult, ALU.add
                    ).then_inc(conv_ready, 1)

            def z_silu(s, par, n):
                dve.wait_ge(zth_ready, at(s, 4, n))
                if n == 0 and (some(s) or s >= 2):
                    dve.wait_ge(g_ready, at(s - 2, TILES, TILES - 1))
                stt(sz[:, par, n], zth[:, n % 2], 1.0, bR[BANK[ZT[n]]][:], ALU.add, ALU.mult
                    ).then_inc(sz_ready, 1)

            def read_small(s, j):
                b = j % 2
                dve.wait_ge(small_ready, at(s, TILES, j))
                if j >= 2:
                    dve.wait_ge(w_ready, at(s, TILES, j - 2))
                    dve.wait_ge(ec_ready, at(s, TILES, j - 2))
                elif some(s) or s > 0:
                    dve.wait_ge(w_ready, at(s - 1, TILES, j + 2))
                    dve.wait_ge(ec_ready, at(s - 1, TILES, j + 2))
                stt(cbm[:, b], bSM[:, 0:P], 0.25, tri[:], ALU.mult, ALU.mult)
                cp(sm[:, b], bSM[:, P:2 * P + 6]).then_inc(cb_ready, 1)

            def decays(s, j):
                b = j % 2
                dve.wait_ge(ex_ready, at(s, TILES, j))
                dve.wait_ge(ec_ready, at(s, TILES, j))
                if j < TILES - 1:
                    tt(bd[:, b], sm[:, b, 0:N].rearrange("p (o n) -> p o n", o=1).to_broadcast([P, H, N]),
                       Ex[:, b, :, P - 1:P].to_broadcast([P, H, N]), ALU.mult).then_inc(bd_ready, 1)
                if j > 0:
                    stt(cs[:, b], sm[:, b, N:2 * N].rearrange("p (o n) -> p o n", o=1).to_broadcast([P, H, N]),
                        0.25, ec[:, b, 0:H].rearrange("p (h o) -> p h o", o=1).to_broadcast([P, H, N]),
                        ALU.mult, ALU.mult).then_inc(cs_ready, 1)

            def state(s, j):
                b, nb = j % 2, (j + 1) % 2
                dve.wait_ge(ds_ready, at(s, 3, j))
                if j == 2:
                    dve.wait_ge(y_ready, at(s, TILES, 1))
                elif some(s) or s > 0:
                    dve.wait_ge(y_ready, at(s - 1, TILES, TILES - 1))
                if j == 0:
                    cp(S[:, nb], bCS[:, 2 * P:4 * P].rearrange("p (a q) -> p a q", a=2)).then_inc(s_ready, 1)
                else:
                    for a in range(2):
                        last = stt(S[:, nb, a], S[:, b, a], ec[:, b, H + a:H + a + 1],
                                   bCS[:, 2 * P + a * HD:2 * P + (a + 1) * HD], ALU.mult, ALU.add)
                    last.then_inc(s_ready, 1)
                dve.wait_ge(s_ready, at(s, 3, j))

            def tile_out(s, par, j):
                dve.wait_ge(y_ready, at(s, TILES, j))
                dve.wait_ge(sq_ready, at(s, TILES, j))
                if j == 0 and (some(s) or s >= 2):
                    dve.wait_ge(projC_ready, 1 + at(s - 2, len(C_SLOTS), len(C_SLOTS) - 1))
                tt(g[:, par, :, j * P:(j + 1) * P], bY[:].rearrange("p (h q) -> p h q", h=H),
                   sz[:, par, :, j * P:(j + 1) * P], ALU.mult).then_inc(g_ready, 1)

            def c_ready(s, name):
                dve.wait_ge(projC_ready, 1 + at(s, len(C_SLOTS), C_SLOTS.index(name)))

            def mean_square(s):
                c_ready(s, "ssq")
                ts(ms[:], bR[BANK["ssq"]][:, 0:TILES], 4.0 / DI, 4.0 * RMS_EPS, ALU.mult, ALU.add
                   ).then_inc(ssq_read, 1)

            def residual(s, half):
                if half == 0:
                    dve.wait_ge(rms_root, at(s, 1))
                    dve.wait_ge(xres_loaded, 16 * (s + 1))
                    if some(s) or s > 0:
                        dve.wait_ge(yo_ready, 1 + at(s - 1, 2, 1))
                c_ready(s, f"out{half}")
                for q in range(2):
                    j = 2 * half + q
                    last = stt(x1[:, j], bR[BANK[f"out{half}"]][:, q * D:(q + 1) * D], rms[:, j:j + 1],
                               xres[:, j], ALU.mult, ALU.add)
                last.then_inc(x1_ready, 1)

            def ln2_in(s):
                wait_read(dve, "out1", s)
                statistics(x1, st6c, mvc, ln2_sums, ln2_mean, centrec, vec, ln2_var, s)

            def ln2_out(s):
                if some(s) or s > 0:
                    dve.wait_ge(rows_stored, 1 + 16 * s)
                dve.wait_ge(ln2_root, at(s, 1))
                normalise(x1, xr, mvc, nwc).then_inc(x2_ready, 1)

            def route_groups(s, c):
                link = c.link
                dve.wait_ge(lex_ready, at(s, 1))
                if some(s) or s > 0:
                    dve.wait_ge(selt_ready, 1 + at(s - 1, 1))
                link(ts(lex[:], lex[:], 1.0, None, ALU.add))
                link(v.reciprocal(sc[:], lex[:]))
                link(tt(sbz[:], sc[:], bias_b[:].rearrange("p (o e) -> p o e", o=1).to_broadcast([P, TILES, E]),
                        ALU.add))
                pair = sbz[:].rearrange("p j (g q t) -> p (j g) q t", q=4, t=2)
                tt(hi[:], pair[:, :, :, 0], pair[:, :, :, 1], ALU.max)
                link(tt(lo[:], pair[:, :, :, 0], pair[:, :, :, 1], ALU.min))
                tt(hi2[:], hi[:, :, 0:2], hi[:, :, 2:4], ALU.max)
                tt(mn2[:], hi[:, :, 0:2], hi[:, :, 2:4], ALU.min)
                link(tt(lo2[:], lo[:, :, 0:2], lo[:, :, 2:4], ALU.max))
                link(tt(lo2[:], lo2[:], mn2[:], ALU.max))
                tt(gs3[:, 0], hi2[:, :, 0], hi2[:, :, 1], ALU.max)
                tt(gs3[:, 1], hi2[:, :, 0], hi2[:, :, 1], ALU.min)
                link(tt(gs3[:, 2], lo2[:, :, 0], lo2[:, :, 1], ALU.max))
                link(tt(gs3[:, 3], gs3[:, 1], gs3[:, 2], ALU.max))
                link(tt(gsx[:, :, 0:G], gs3[:, 0].rearrange("p (j g) -> p j g", g=G),
                        gs3[:, 3].rearrange("p (j g) -> p j g", g=G), ALU.add))

            def choose_groups(s, c):
                link = c.link
                apart(dve)
                for j in range(TILES):
                    last = v.max(m8g[:, j], gsx[:, j])
                link(last)
                link(v.memset(m8g[:, :, KG:8], -BIG))
                apart(dve)
                for j in range(TILES):
                    last = v.match_replace(grp[:, j], m8g[:, j], gsx[:, j], BIG)
                link(last)
                link(ts(gm[:], grp[:, :, 0:G], BIG, None, ALU.is_equal))
                ts(gneg[:], gm[:], 1.0, BIG, ALU.subtract, ALU.mult)
                gmb = gm[:].rearrange("p j (g o) -> p (j g) o", o=1).to_broadcast([P, TILES * G, EG])
                link(tt(tmp[:].rearrange("p j (g q) -> p (j g) q", q=EG),
                        sbz[:].rearrange("p j (g q) -> p (j g) q", q=EG), gmb, ALU.mult))
                link(tt(tmp[:].rearrange("p j (g q) -> p (j g) q", q=EG),
                        tmp[:].rearrange("p j (g q) -> p (j g) q", q=EG),
                        gneg[:].rearrange("p j (g o) -> p (j g) o", o=1).to_broadcast([P, TILES * G, EG]),
                        ALU.add))

            def choose_experts(s, c):
                link = c.link
                gmb = gm[:].rearrange("p j (g o) -> p (j g) o", o=1).to_broadcast([P, TILES * G, EG])
                apart(dve)
                for j in range(TILES):
                    last = v.max(m8e[:, j], tmp[:, j])
                link(last)
                link(v.memset(m8e[:, :, K:8], -BIG))
                apart(dve)
                for j in range(TILES):
                    last = v.match_replace(rep[:, j], m8e[:, j], tmp[:, j], BIG)
                link(last)
                link(stt(sel[:].rearrange("p j (g q) -> p (j g) q", q=EG),
                         rep[:].rearrange("p j (g q) -> p (j g) q", q=EG), BIG, gmb, ALU.is_equal, ALU.mult))
                tt(tmp[:], sel[:], sc[:], ALU.mult).then_inc(sel_ready, 1)

            def expert_weights_of(s, c):
                link = c.link
                dve.wait_ge(sel_ready, 1 + at(s, 1))
                link(v.tensor_reduce(wsum[:], tmp[:], AX.X, ALU.add))
                link(v.reciprocal(wrec[:], wsum[:]))
                stt(xr[:, :, D:ROW], tmp[:], SCALE,
                    wrec[:].rearrange("p (j o) -> p j o", o=1).to_broadcast([P, TILES, E]),
                    ALU.mult, ALU.mult).then_inc(rw_ready, 1)

            def shared(s, c):
                c_ready(s, "gate")
                dve.wait_ge(gth_ready, at(s, 1))
                if some(s) or s > 0:
                    dve.wait_ge(hs_ready, 1 + at(s - 1, 1))
                stt(gth[:], gth[:], 1.0, bR[BANK["gate"]][0:F, :], ALU.add, ALU.mult).then_inc(gate_read, 1)
                wait_read(dve, "gate", s)
                c_ready(s, "up")
                if some(s) or s > 0:
                    c_ready(s - 1, "down1")
                tt(hs[:], gth[:], bR[BANK["up"]][0:F, :], ALU.mult).then_inc(hs_ready, 1)

            def shared_out(s):
                if some(s) or s > 0:
                    dve.wait_ge(y_stored, 1 + 16 * s)
                for half in range(2):
                    c_ready(s, f"down{half}")
                    for q in range(2):
                        j = 2 * half + q
                        last = stt(yo[:, j], bR[BANK[f"down{half}"]][:, q * D:(q + 1) * D], 0.5, x1[:, j],
                                   ALU.mult, ALU.add)
                    last.then_inc(yo_ready, 1)

            def choose(s, par):
                dve.wait_ge(selt_ready, 1 + at(s, 1))
                tt(keys[par * E:(par + 1) * E, 0, CAP:], bR[BANK["sel"]][0:E, :], rank_rev[0:E, :], ALU.mult
                   ).then_inc(keys_ready, 1)

            def take(k, rounds):
                def link(n, ins):
                    ins.then_inc(take_step, 1)
                    dve.wait_ge(take_step, 1 + k * TAKE + n)

                if 0 in rounds:
                    wait_read(dve, "sel", 2 * k - 1)
                for r in rounds:
                    apart(dve)
                    link(2 * r + 1, v.max(first[:, 8 * r:8 * r + 8], keys[:, r % 2, CAP:]))
                    if r < ROUNDS - 1:
                        apart(dve)
                        link(2 * r + 2, v.match_replace(keys[:, (r + 1) % 2, CAP:], first[:, 8 * r:8 * r + 8],
                                                        keys[:, r % 2, CAP:], 0.0))
                    else:
                        dst = lists[:, k] if isinstance(k, int) else \
                            lists[:, bass.ds(dve.snap(k), 1)].rearrange("p o q -> p (o q)")
                        link(TAKE, cp(dst, first[:]))

            nm = [0]

            def merge_link(ins):
                ins.then_inc(merge_step, 1)
                nm[0] += 1
                dve.wait_ge(merge_step, nm[0])

            def first_of(src, dst, rounds):
                for r in rounds:
                    merge_link(v.max(dst[:, 8 * r:8 * r + 8], src[:, r % 2]))
                    if r < ROUNDS - 1:
                        merge_link(v.match_replace(src[:, (r + 1) % 2], dst[:, 8 * r:8 * r + 8], src[:, r % 2], 0.0))

            def gather_lists():
                for u in range(PAIRS):
                    for par in range(2):
                        last = v.memset(base[par * E:(par + 1) * E, u:u + 1], float(T - L * (2 * u + par + 1)))
                merge_link(last)
                merge_link(v.memset(tokT[:], float(T)))
                merge_link(stt(gk[:], lists[:, 1:], 0.0,
                               base[:].rearrange("p (u o) -> p u o", o=1).to_broadcast([P, PAIRS, CAP]),
                               ALU.is_gt, ALU.mult))
                merge_link(tt(gk[:], gk[:], lists[:, 1:], ALU.add))
                for par in range(2):
                    cp(cat[:, 0, par * PAIRS * CAP:(par + 1) * PAIRS * CAP],
                       gk[par * E:(par + 1) * E].rearrange("p u q -> p (u q)"))
                wait_read(dve, "sel", NSEQ - 2)
                seventh = cat[:, :, 2 * PAIRS * CAP:]
                merge_link(ts(seventh[:, 1], keys[0:E, 0, CAP:], 0.0, float(L), ALU.is_gt, ALU.mult))
                merge_link(tt(seventh[:, 0], seventh[:, 1], keys[0:E, 0, CAP:], ALU.add))

            def merge(rounds):
                first_of(cat, kfirst[0:E], rounds)
                if ROUNDS - 1 in rounds:
                    merge_link(cp(keys[E:P, 0, 0:CAP], kfirst[0:E]))

            def signs_and_halves():
                dve.wait_ge(abc_exp, 1)
                ts(abc[:], abc[:], -1.0, None, ALU.mult).then_inc(abc_ready, 1)
                dve.wait_ge(w_loaded, 16 * 12)
                dve.wait_ge(abc_ready, 1)
                ts(dsk[:], dsk[:], 0.5, None, ALU.mult).then_inc(abc_ready, 1)
                dve.wait_ge(abc_ready, 2)
                dve.wait_ge(consts_ready, 2)

            def iteration(it, par, hasA, hasB, hasC, before):
                a, ap, c, cpar = it + 1, 1 - par, it - 1, 1 - par
                ch = Chain(dve, c_step, c, C_CHAIN) if hasC else None
                if hasB:
                    read_small(it, 0)
                if hasC:
                    mean_square(c)
                    choose(c - 1, par)
                if hasA:
                    ln1_in(a, ap)
                if hasB:
                    decays(it, 0)
                if isinstance(it, int) and it == -1:
                    signs_and_halves()
                if hasC:
                    if cpar == 0:
                        k = (it - 1) // 2
                        take(k, range(2))
                    if isinstance(it, int) and it == NSEQ:
                        gather_lists()
                        merge(range(2))
                    residual(c, 0)
                    if cpar == 0:
                        take(k, range(2, 4))
                    if isinstance(it, int) and it == NSEQ:
                        merge(range(2, 3))
                    residual(c, 1)
                    ln2_in(c)
                if hasB:
                    state(it, 0)
                    tile_out(it, par, 0)
                    read_small(it, 1)
                    decays(it, 1)
                if hasA:
                    conv(a, 0)
                if hasC:
                    ln2_out(c)
                if hasA:
                    dt_stage(a, ap)
                if hasC and cpar == 0:
                    take(k, range(4, 6))
                if hasB:
                    state(it, 1)
                    tile_out(it, par, 1)
                if hasA:
                    conv(a, 1)
                if hasB:
                    read_small(it, 2)
                    decays(it, 2)
                if isinstance(it, int) and it == NSEQ:
                    merge(range(3, 5))
                if hasC:
                    route_groups(c, ch)
                if hasA:
                    conv(a, 2)
                    conv(a, 3)
                if hasB:
                    state(it, 2)
                    tile_out(it, par, 2)
                    read_small(it, 3)
                    decays(it, 3)
                if hasC:
                    shared(c, ch)
                    if isinstance(it, int) and it == NSEQ:
                        merge(range(5, ROUNDS))
                    choose_groups(c, ch)
                if hasA:
                    conv(a, 4)
                    z_silu(a, ap, 0)
                if hasB:
                    tile_out(it, par, 3)
                if hasA:
                    z_silu(a, ap, 1)
                if hasC:
                    shared_out(c)
                    choose_experts(c, ch)
                    expert_weights_of(c, ch)
                if hasA:
                    z_silu(a, ap, 2)
                    z_silu(a, ap, 3)
                if hasC:
                    ch.done()
            schedule(dve, iteration)
            choose(NSEQ - 1, 1)
            dve.wait_ge(keys_ready, 1 + at(NSEQ - 1, 1))
            first_of(keys[E:P], kfirst[E:P], range(ROUNDS))
            ts(ktok[E:P], kfirst[E:P], -1.0, float(T), ALU.mult, ALU.add).then_inc(ktok_ready, 1)
            dve.wait_ge(tokt_ready, 1)
            for e in range(2):
                last = cp(tokT[e * 64:e * 64 + CAP], bTR[0:CAP, e:E:2])
            merge_link(last)
            cp(idxT[:], tokT[:]).then_inc(idx_ready, 1)

            def token_column(i, n):
                if some(i) or i >= 2:
                    dve.wait_ge(rowb_ready, i - 1)
                cp(tokc[:, n % 2], tokT[:, bass.ds(i, 1)]).then_inc(tokc_ready, 1)

            def same_token(i, n):
                b = n % 2

                def link(k, ins):
                    ins.then_inc(token_step, 1)
                    dve.wait_ge(token_step, i * 3 + k + 1)

                link(0, tt(sidx[:, b, 0:1], tokT[:, bass.ds(i, 1)], spare[:], ALU.subtract))
                dve.wait_ge(tokc_ready, i + 1)
                dve.wait_ge(rowb_ready, i + 1)
                if some(i) or i >= 2:
                    dve.wait_ge(hsum_ready, i - 1)
                ts(eq[:, b], bSM[:, 0:P], tokc[:, n % 2], None, ALU.is_equal).then_inc(eq_ready, 1)
                dve.wait_ge(eq_ready, i + 1)
                if some(i) or i >= WRING:
                    dve.wait_ge(scattered, 16 * (i - WRING + 1))
                link(1, v.tensor_tensor_reduce(out=eqs[:, b], in0=eq[:, b], in1=strict[:], scale=1.0, scalar=0.0,
                                               op0=ALU.mult, op1=ALU.add, accum_out=cnt[:, b]))
                link(2, stt(sidx[:, b, 1:2], cnt[:, b], 0.0, sidx[:, b, 0:1], ALU.is_equal, ALU.mult))
                tt(sidxi[:, n], sidx[:, b, 1:2], spare[:], ALU.add).then_inc(sidx_ready, 1)

            def activate(i, n):
                b = n % 2
                dve.wait_ge(eth_ready, i + 1)
                stt(ehg[:, b], eth[:, b], 1.0, bGU[b][:, 0:F], ALU.add, ALU.mult).then_inc(ehg_ready, 1)
                dve.wait_ge(ehg_ready, i + 1)
                dve.wait_ge(wcol_ready, i + 1)
                if some(i) or i >= 2:
                    dve.wait_ge(hsum_ready, i - 1)
                stt(ehs[:, b], ehg[:, b], wcol[:, b], bGU[b][:, F:2 * F], ALU.mult, ALU.mult).then_inc(ehs_ready, 1)

            def weight_of(i, n):
                dve.wait_ge(gathered[n], 16 * (i // WRING + 1) if isinstance(i, int) else (i - n) * 4 + 16)
                for e in range(2):
                    r = slice(e * 64, (e + 1) * 64)
                    off = D + 2 * i + e if isinstance(i, int) else dve.snap(2 * i + (D + e))
                    last = ts(wcol[r, n % 2], xg[r, n, bass.ds(off, 1)], 0.5, None, ALU.mult)
                last.then_inc(wcol_ready, 1)

            def expert_step(i, n):
                if some(i) or i + 1 < ET:
                    same_token(i + 1, (n + 1) % WRING)
                if some(i) or i + 2 < ET:
                    token_column(i + 2, (n + 2) % WRING)
                if some(i) or i < ET:
                    weight_of(i, n)
                    activate(i, n)

            for n in range(2):
                token_column(n, n)
            same_token(0, 0)
            expert_schedule(dve, expert_step)


DT_CHAIN = 16
TAKE = 2 * ROUNDS
C_CHAIN = 21

def kernel(**inputs):
    import numpy as _np
    import concourse.bacc as _bacc
    from concourse import mybir as _mybir
    from concourse.bass_utils import run_bass_kernel_spmd as _run

    a = {k: _np.asarray(v) for k, v in inputs.items()}

    def spread(v):
        return _np.broadcast_to(v[None, :], (P, v.shape[0]))

    parts = {
        "x": a["L0_attn_x"].reshape(T, D),
        "w_in": a["L0_attn_W_in"].T.reshape(KD, P, PROJ + H).transpose(1, 0, 2),
        "conv_w": a["L0_attn_conv_w"].reshape(5, P, 4).transpose(1, 0, 2),
        "conv_b": a["L0_attn_conv_b"].reshape(5, P).T,
        "a_log": spread(a["L0_attn_A_log"]),
        "dt_bias": spread(a["L0_attn_dt_bias"]),
        "dskip": spread(a["L0_attn_D"]),
        "w_out": a["L0_attn_W_out"].T.reshape(H, P, D).transpose(1, 0, 2),
        "gate_w": a["L0_ffn_gate_w"].reshape(P, KD, E),
        "bias": spread(a["L0_ffn_bias"]),
        "w_gate": a["L0_ffn_w_gate"].reshape(ET, 2, P, KD, F).transpose(0, 2, 1, 3, 4),
        "w_up": a["L0_ffn_w_up"].reshape(ET, 2, P, KD, F).transpose(0, 2, 1, 3, 4),
        "w_down": a["L0_ffn_w_down"].reshape(ET, 2, F, D).transpose(0, 2, 1, 3),
        "ws_gate": a["L0_ffn_ws_gate"].reshape(P, KD, F),
        "ws_up": a["L0_ffn_ws_up"].reshape(P, KD, F),
        "ws_down": a["L0_ffn_ws_down"],
    }
    nc = _bacc.Bacc("TRN2", target_bir_lowering=False, num_devices=1)
    arrays, args = {}, {}
    for name, v in parts.items():
        v = _np.ascontiguousarray(v)
        arrays[f"in_{name}"] = v
        args[name] = nc.dram_tensor(f"in_{name}", v.shape, _mybir.dt.from_np(v.dtype), kind="ExternalInput").ap()
    rows = nc.dram_tensor("rows", (T + P, ROW), _mybir.dt.float32, kind="Internal").ap()
    out = nc.dram_tensor("out_y", (T + P, D), _mybir.dt.float32, kind="ExternalOutput").ap()
    build(nc, **args, rows=rows, out=out)
    r = _run(nc, [arrays], core_ids=[0])
    return r.results[0]["out_y"][:T].reshape(NSEQ, L, D)
```
